# Optimizing a Trainium2 kernel written in Bass

```python
import numpy as np
import jax
import jax.numpy as jnp

def _softmax(x, axis=-1):
    return jax.nn.softmax(x, axis=axis)

def _gelu(x):
    return jax.nn.gelu(x, approximate=True)

def _silu(x):
    return jax.nn.silu(x)

def _sigmoid(x):
    return jax.nn.sigmoid(x)

def _layernorm(x, axis=-1, eps=1e-05):
    m = jnp.mean(x, axis=axis, keepdims=True)
    v = jnp.var(x, axis=axis, keepdims=True)
    return (x - m) / jnp.sqrt(v + eps)

def _scatter_add(tgt, idx, src, axis=0):
    return tgt.at[idx].add(src)

def _segment_sum(src, seg, n):
    return jax.ops.segment_sum(src, seg, n)
kernel_name = 'mk_seq_preln_d1_jaxref_r8_e04392'

def setup_inputs(seed: int=0):
    np.random.seed(seed)
    _w = jnp.asarray

    def _L0_attn_setup():
        import jax, jax.numpy as jnp
        import numpy as np
        import math
        N_HEAD = 16
        V_HEAD = 32
        NOPE = 32
        ROPE_D = 64
        KEEP = 32
        EPS = 1e-06

        def _freqs(T, dim=ROPE_D, theta=10000.0):
            f = 1.0 / theta ** (jnp.arange(0, dim, 2, dtype=jnp.float32) / dim)
            t = jnp.arange(T, dtype=jnp.float32)
            a = jnp.outer(t, f)
            return (jnp.cos(a), jnp.sin(a))

        def _rope(x, cos, sin):
            S = x.shape[-2]
            c = cos[:S][None, None]
            s = sin[:S][None, None]
            x1, x2 = jnp.split(x, 2, axis=-1)
            return jnp.concatenate([x1 * c - x2 * s, x1 * s + x2 * c], axis=-1)

        def _rms(x, g, eps=EPS):
            return x * jax.lax.rsqrt(jnp.mean(x * x, axis=-1, keepdims=True) + eps) * g

        def _attn(q, k, v, causal):
            scale = 1.0 / math.sqrt(q.shape[-1])
            s = jnp.einsum('bhqd,bhkd->bhqk', q, k) * scale
            if causal:
                Tq, Tk = (s.shape[-2], s.shape[-1])
                mask = jnp.tril(jnp.ones((Tq, Tk), dtype=bool))
                s = jnp.where(mask, s, jnp.finfo(s.dtype).min)
            return jnp.einsum('bhqk,bhkd->bhqd', jax.nn.softmax(s, axis=-1), v)

        def _forward(x, w_cq, g_qnorm, w_dq_nope, w_dq_rope, w_ckv, g_kvnorm, w_dk_nope, w_dv, w_krope, w_imp, w_selk, w_selv, w_wink, w_winv, w_gate, w_proj):
            B, T, C = x.shape
            cos, sin = _freqs(T)
            nq = _rms(x @ w_cq, g_qnorm)
            q_nope = (nq @ w_dq_nope).reshape(B, T, N_HEAD, NOPE).transpose(0, 2, 1, 3)
            q_rope = (nq @ w_dq_rope).reshape(B, T, N_HEAD, ROPE_D).transpose(0, 2, 1, 3)
            q_rope = _rope(q_rope, cos, sin)
            q = jnp.concatenate([q_nope, q_rope], axis=-1)
            gate = jax.nn.softmax((x @ w_gate).mean(axis=1), axis=-1)
            ckv = _rms(x @ w_ckv, g_kvnorm)
            k_nope = (ckv @ w_dk_nope).reshape(B, T, N_HEAD, NOPE).transpose(0, 2, 1, 3)
            v1 = (ckv @ w_dv).reshape(B, T, N_HEAD, V_HEAD).transpose(0, 2, 1, 3)
            k_rope = (x @ w_krope).reshape(B, T, 1, ROPE_D).transpose(0, 2, 1, 3) / N_HEAD
            k_rope = _rope(k_rope, cos, sin)
            k1 = jnp.concatenate([k_nope, jnp.broadcast_to(k_rope, (B, N_HEAD, T, ROPE_D))], axis=-1)
            scores = (x @ w_imp)[..., 0]
            _, idx = jax.lax.top_k(scores, KEEP)
            idx = jnp.sort(idx, axis=1)
            sel = jnp.take_along_axis(x, idx[:, :, None], axis=1)
            ks = (sel @ w_selk).reshape(B, KEEP, N_HEAD, NOPE + ROPE_D).transpose(0, 2, 1, 3)
            vs = (sel @ w_selv).reshape(B, KEEP, N_HEAD, V_HEAD).transpose(0, 2, 1, 3)
            ks = jnp.concatenate([ks[..., :NOPE], _rope(ks[..., NOPE:], cos, sin)], axis=-1)
            kw = (x @ w_wink).reshape(B, T, N_HEAD, NOPE + ROPE_D).transpose(0, 2, 1, 3)
            vw = (x @ w_winv).reshape(B, T, N_HEAD, V_HEAD).transpose(0, 2, 1, 3)
            kw = jnp.concatenate([kw[..., :NOPE], _rope(kw[..., NOPE:], cos, sin)], axis=-1)
            a1 = _attn(q, k1, v1, causal=True)
            a2 = _attn(q, ks, vs, causal=False)
            a3 = _attn(q, kw, vw, causal=True)
            g = gate[:, :, None, None, None]
            out = g[:, 0] * a1 + g[:, 1] * a2 + g[:, 2] * a3
            out = out.transpose(0, 2, 1, 3).reshape(B, T, N_HEAD * V_HEAD)
            return out @ w_proj
        key = jax.random.key(seed)
        ks = jax.random.split(key, 20)
        B, T, C = (2, 128, 128)
        q_lora, kv_lora = (96, 32)
        std = 0.02

        def w(k, shape):
            return jax.random.normal(k, shape, dtype=jnp.float32) * std
        return {'x': jax.random.normal(ks[0], (B, T, C), dtype=jnp.float32), 'w_cq': w(ks[1], (C, q_lora)), 'g_qnorm': jnp.ones((q_lora,), jnp.float32), 'w_dq_nope': w(ks[2], (q_lora, N_HEAD * NOPE)), 'w_dq_rope': w(ks[3], (q_lora, N_HEAD * ROPE_D)), 'w_ckv': w(ks[4], (C, kv_lora)), 'g_kvnorm': jnp.ones((kv_lora,), jnp.float32), 'w_dk_nope': w(ks[5], (kv_lora, N_HEAD * NOPE)), 'w_dv': w(ks[6], (kv_lora, N_HEAD * V_HEAD)), 'w_krope': w(ks[7], (C, ROPE_D)), 'w_imp': w(ks[8], (C, 1)), 'w_selk': w(ks[9], (C, N_HEAD * (NOPE + ROPE_D))), 'w_selv': w(ks[10], (C, N_HEAD * V_HEAD)), 'w_wink': w(ks[11], (C, N_HEAD * (NOPE + ROPE_D))), 'w_winv': w(ks[12], (C, N_HEAD * V_HEAD)), 'w_gate': w(ks[13], (C, 3)), 'w_proj': w(ks[14], (N_HEAD * V_HEAD, C))}
    _L0_attn_in = _L0_attn_setup()

    def _L0_ffn_setup():
        import jax, jax.numpy as jnp
        import numpy as np
        DIM = 128
        DEPTH = 2
        HEADS = 8
        DIM_HEAD = 64
        WINDOW = 64
        INNER = HEADS * DIM_HEAD
        HID = int(DIM * 4 * 2 / 3)
        B, N = (2, 1024)
        QK_SCALE = 8.0

        def shift_token(t):
            t1, t2 = jnp.split(t, 2, axis=-1)
            t2 = jnp.pad(t2, ((0, 0), (1, 0), (0, 0)))[:, :-1]
            return jnp.concatenate([t1, t2], axis=-1)

        def l2norm(t):
            return t / jnp.clip(jnp.linalg.norm(t, axis=-1, keepdims=True), 1e-12)

        def rotate_half(x):
            x1, x2 = jnp.split(x, 2, axis=-1)
            return jnp.concatenate([-x2, x1], axis=-1)

        def rotary_xpos(q, k):
            n = q.shape[-2]
            half_idx = jnp.arange(0, DIM_HEAD, 2, dtype=jnp.float32)
            inv_freq = 1.0 / 10000.0 ** (half_idx / DIM_HEAD)
            t = jnp.arange(n, dtype=jnp.float32)
            freqs = t[:, None] * inv_freq[None, :]
            freqs = jnp.concatenate([freqs, freqs], axis=-1)
            base = (half_idx + 0.4 * DIM_HEAD) / (1.4 * DIM_HEAD)
            power = (t - n // 2) / float(WINDOW // 2)
            scale = base[None, :] ** power[:, None]
            scale = jnp.concatenate([scale, scale], axis=-1)
            cos, sin = (jnp.cos(freqs), jnp.sin(freqs))
            q = q * cos * scale + rotate_half(q) * sin * scale
            k = k * cos / scale + rotate_half(k) * sin / scale
            return (q, k)

        def local_attention(q, k, v):
            b, h, n, d = q.shape
            w = n // WINDOW
            bq = q.reshape(b, h, w, WINDOW, d) * QK_SCALE
            bk = k.reshape(b, h, w, WINDOW, d)
            bv = v.reshape(b, h, w, WINDOW, d)

            def look_around(t):
                p = jnp.pad(t, ((0, 0), (0, 0), (1, 0), (0, 0), (0, 0)))
                return jnp.concatenate([p[:, :, :w], p[:, :, 1:]], axis=3)
            bk, bv = (look_around(bk), look_around(bv))
            bt = jnp.arange(n).reshape(w, WINDOW)
            btp = jnp.pad(bt, ((1, 0), (0, 0)), constant_values=-1)
            btk = jnp.concatenate([btp[:w], btp[1:]], axis=1)
            sim = jnp.einsum('bhwid,bhwjd->bhwij', bq, bk)
            i = bt[:, :, None]
            j = btk[:, None, :]
            mask = (i < j) | (i > j + WINDOW) | (j == -1)
            sim = jnp.where(mask, -jnp.finfo(sim.dtype).max, sim)
            attn = jax.nn.softmax(sim, axis=-1)
            out = jnp.einsum('bhwij,bhwjd->bhwid', attn, bv)
            return out.reshape(b, h, n, d)

        def _layer(x, wqkv, qs, ksc, wo, lg, lb, w1, b1, w2, b2):
            b, n, _ = x.shape
            h = shift_token(x)
            qkv = h @ wqkv
            q, k, v = jnp.split(qkv, 3, axis=-1)
            to_heads = lambda t: t.reshape(b, n, HEADS, DIM_HEAD).transpose(0, 2, 1, 3)
            q, k, v = (to_heads(q), to_heads(k), to_heads(v))
            q = l2norm(q) * qs
            k = l2norm(k) * ksc
            q, k = rotary_xpos(q, k)
            o = local_attention(q, k, v)
            o = o.transpose(0, 2, 1, 3).reshape(b, n, INNER)
            x = x + o @ wo
            h = shift_token(x)
            mu = h.mean(-1, keepdims=True)
            var = h.var(-1, keepdims=True)
            h = (h - mu) / jnp.sqrt(var + 1e-05) * lg + lb
            h = h @ w1 + b1
            a, g = jnp.split(h, 2, axis=-1)
            h = a * jax.nn.gelu(g, approximate=False)
            x = x + h @ w2 + b2
            return x
        key = jax.random.key(seed)
        ks = jax.random.split(key, 6)
        return {'x': jax.random.normal(ks[0], (B, N, DIM), jnp.float32), 'wqkv': jax.random.normal(ks[1], (DEPTH, DIM, 3 * INNER), jnp.float32) * 0.02, 'q_scale': jnp.ones((DEPTH, DIM_HEAD), jnp.float32), 'k_scale': jnp.ones((DEPTH, DIM_HEAD), jnp.float32), 'wo': jax.random.normal(ks[2], (DEPTH, INNER, DIM), jnp.float32) * 0.02, 'ln_g': jnp.ones((DEPTH, DIM), jnp.float32), 'ln_b': jnp.zeros((DEPTH, DIM), jnp.float32), 'w1': jax.random.normal(ks[3], (DEPTH, DIM, 2 * HID), jnp.float32) * 0.02, 'b1': jnp.zeros((DEPTH, 2 * HID), jnp.float32), 'w2': jax.random.normal(ks[4], (DEPTH, HID, DIM), jnp.float32) * 0.02, 'b2': jnp.zeros((DEPTH, DIM), jnp.float32)}
    _L0_ffn_in = _L0_ffn_setup()
    _d = {'L0_attn_x': _L0_attn_in['x'], 'L0_attn_w_cq': _L0_attn_in['w_cq'], 'L0_attn_g_qnorm': _L0_attn_in['g_qnorm'], 'L0_attn_w_dq_nope': _L0_attn_in['w_dq_nope'], 'L0_attn_w_dq_rope': _L0_attn_in['w_dq_rope'], 'L0_attn_w_ckv': _L0_attn_in['w_ckv'], 'L0_attn_g_kvnorm': _L0_attn_in['g_kvnorm'], 'L0_attn_w_dk_nope': _L0_attn_in['w_dk_nope'], 'L0_attn_w_dv': _L0_attn_in['w_dv'], 'L0_attn_w_krope': _L0_attn_in['w_krope'], 'L0_attn_w_imp': _L0_attn_in['w_imp'], 'L0_attn_w_selk': _L0_attn_in['w_selk'], 'L0_attn_w_selv': _L0_attn_in['w_selv'], 'L0_attn_w_wink': _L0_attn_in['w_wink'], 'L0_attn_w_winv': _L0_attn_in['w_winv'], 'L0_attn_w_gate': _L0_attn_in['w_gate'], 'L0_attn_w_proj': _L0_attn_in['w_proj'], 'L0_ffn_wqkv': _L0_ffn_in['wqkv'], 'L0_ffn_q_scale': _L0_ffn_in['q_scale'], 'L0_ffn_k_scale': _L0_ffn_in['k_scale'], 'L0_ffn_wo': _L0_ffn_in['wo'], 'L0_ffn_ln_g': _L0_ffn_in['ln_g'], 'L0_ffn_ln_b': _L0_ffn_in['ln_b'], 'L0_ffn_w1': _L0_ffn_in['w1'], 'L0_ffn_b1': _L0_ffn_in['b1'], 'L0_ffn_w2': _L0_ffn_in['w2'], 'L0_ffn_b2': _L0_ffn_in['b2']}
    _x0 = _d['L0_attn_x']
    _d['L0_attn_x'] = jax.random.normal(jax.random.fold_in(jax.random.key(seed), 1), (2, 1024, 128), dtype=_x0.dtype)
    del _x0
    return _d

def reference(L0_attn_x, L0_attn_w_cq, L0_attn_g_qnorm, L0_attn_w_dq_nope, L0_attn_w_dq_rope, L0_attn_w_ckv, L0_attn_g_kvnorm, L0_attn_w_dk_nope, L0_attn_w_dv, L0_attn_w_krope, L0_attn_w_imp, L0_attn_w_selk, L0_attn_w_selv, L0_attn_w_wink, L0_attn_w_winv, L0_attn_w_gate, L0_attn_w_proj, L0_ffn_wqkv, L0_ffn_q_scale, L0_ffn_k_scale, L0_ffn_wo, L0_ffn_ln_g, L0_ffn_ln_b, L0_ffn_w1, L0_ffn_b1, L0_ffn_w2, L0_ffn_b2):

    def _L0_attn_ref(x, w_cq, g_qnorm, w_dq_nope, w_dq_rope, w_ckv, g_kvnorm, w_dk_nope, w_dv, w_krope, w_imp, w_selk, w_selv, w_wink, w_winv, w_gate, w_proj):
        import jax, jax.numpy as jnp
        import numpy as np
        import math
        N_HEAD = 16
        V_HEAD = 32
        NOPE = 32
        ROPE_D = 64
        KEEP = 32
        EPS = 1e-06

        def _freqs(T, dim=ROPE_D, theta=10000.0):
            f = 1.0 / theta ** (jnp.arange(0, dim, 2, dtype=jnp.float32) / dim)
            t = jnp.arange(T, dtype=jnp.float32)
            a = jnp.outer(t, f)
            return (jnp.cos(a), jnp.sin(a))

        def _rope(x, cos, sin):
            S = x.shape[-2]
            c = cos[:S][None, None]
            s = sin[:S][None, None]
            x1, x2 = jnp.split(x, 2, axis=-1)
            return jnp.concatenate([x1 * c - x2 * s, x1 * s + x2 * c], axis=-1)

        def _rms(x, g, eps=EPS):
            return x * jax.lax.rsqrt(jnp.mean(x * x, axis=-1, keepdims=True) + eps) * g

        def _attn(q, k, v, causal):
            scale = 1.0 / math.sqrt(q.shape[-1])
            s = jnp.einsum('bhqd,bhkd->bhqk', q, k) * scale
            if causal:
                Tq, Tk = (s.shape[-2], s.shape[-1])
                mask = jnp.tril(jnp.ones((Tq, Tk), dtype=bool))
                s = jnp.where(mask, s, jnp.finfo(s.dtype).min)
            return jnp.einsum('bhqk,bhkd->bhqd', jax.nn.softmax(s, axis=-1), v)

        def _forward(x, w_cq, g_qnorm, w_dq_nope, w_dq_rope, w_ckv, g_kvnorm, w_dk_nope, w_dv, w_krope, w_imp, w_selk, w_selv, w_wink, w_winv, w_gate, w_proj):
            B, T, C = x.shape
            cos, sin = _freqs(T)
            nq = _rms(x @ w_cq, g_qnorm)
            q_nope = (nq @ w_dq_nope).reshape(B, T, N_HEAD, NOPE).transpose(0, 2, 1, 3)
            q_rope = (nq @ w_dq_rope).reshape(B, T, N_HEAD, ROPE_D).transpose(0, 2, 1, 3)
            q_rope = _rope(q_rope, cos, sin)
            q = jnp.concatenate([q_nope, q_rope], axis=-1)
            gate = jax.nn.softmax((x @ w_gate).mean(axis=1), axis=-1)
            ckv = _rms(x @ w_ckv, g_kvnorm)
            k_nope = (ckv @ w_dk_nope).reshape(B, T, N_HEAD, NOPE).transpose(0, 2, 1, 3)
            v1 = (ckv @ w_dv).reshape(B, T, N_HEAD, V_HEAD).transpose(0, 2, 1, 3)
            k_rope = (x @ w_krope).reshape(B, T, 1, ROPE_D).transpose(0, 2, 1, 3) / N_HEAD
            k_rope = _rope(k_rope, cos, sin)
            k1 = jnp.concatenate([k_nope, jnp.broadcast_to(k_rope, (B, N_HEAD, T, ROPE_D))], axis=-1)
            scores = (x @ w_imp)[..., 0]
            _, idx = jax.lax.top_k(scores, KEEP)
            idx = jnp.sort(idx, axis=1)
            sel = jnp.take_along_axis(x, idx[:, :, None], axis=1)
            ks = (sel @ w_selk).reshape(B, KEEP, N_HEAD, NOPE + ROPE_D).transpose(0, 2, 1, 3)
            vs = (sel @ w_selv).reshape(B, KEEP, N_HEAD, V_HEAD).transpose(0, 2, 1, 3)
            ks = jnp.concatenate([ks[..., :NOPE], _rope(ks[..., NOPE:], cos, sin)], axis=-1)
            kw = (x @ w_wink).reshape(B, T, N_HEAD, NOPE + ROPE_D).transpose(0, 2, 1, 3)
            vw = (x @ w_winv).reshape(B, T, N_HEAD, V_HEAD).transpose(0, 2, 1, 3)
            kw = jnp.concatenate([kw[..., :NOPE], _rope(kw[..., NOPE:], cos, sin)], axis=-1)
            a1 = _attn(q, k1, v1, causal=True)
            a2 = _attn(q, ks, vs, causal=False)
            a3 = _attn(q, kw, vw, causal=True)
            g = gate[:, :, None, None, None]
            out = g[:, 0] * a1 + g[:, 1] * a2 + g[:, 2] * a3
            out = out.transpose(0, 2, 1, 3).reshape(B, T, N_HEAD * V_HEAD)
            return out @ w_proj
        return _forward(x, w_cq, g_qnorm, w_dq_nope, w_dq_rope, w_ckv, g_kvnorm, w_dk_nope, w_dv, w_krope, w_imp, w_selk, w_selv, w_wink, w_winv, w_gate, w_proj)

    def _L0_ffn_ref(x, wqkv, q_scale, k_scale, wo, ln_g, ln_b, w1, b1, w2, b2):
        import jax, jax.numpy as jnp
        import numpy as np
        DIM = 128
        DEPTH = 2
        HEADS = 8
        DIM_HEAD = 64
        WINDOW = 64
        INNER = HEADS * DIM_HEAD
        HID = int(DIM * 4 * 2 / 3)
        B, N = (2, 1024)
        QK_SCALE = 8.0

        def shift_token(t):
            t1, t2 = jnp.split(t, 2, axis=-1)
            t2 = jnp.pad(t2, ((0, 0), (1, 0), (0, 0)))[:, :-1]
            return jnp.concatenate([t1, t2], axis=-1)

        def l2norm(t):
            return t / jnp.clip(jnp.linalg.norm(t, axis=-1, keepdims=True), 1e-12)

        def rotate_half(x):
            x1, x2 = jnp.split(x, 2, axis=-1)
            return jnp.concatenate([-x2, x1], axis=-1)

        def rotary_xpos(q, k):
            n = q.shape[-2]
            half_idx = jnp.arange(0, DIM_HEAD, 2, dtype=jnp.float32)
            inv_freq = 1.0 / 10000.0 ** (half_idx / DIM_HEAD)
            t = jnp.arange(n, dtype=jnp.float32)
            freqs = t[:, None] * inv_freq[None, :]
            freqs = jnp.concatenate([freqs, freqs], axis=-1)
            base = (half_idx + 0.4 * DIM_HEAD) / (1.4 * DIM_HEAD)
            power = (t - n // 2) / float(WINDOW // 2)
            scale = base[None, :] ** power[:, None]
            scale = jnp.concatenate([scale, scale], axis=-1)
            cos, sin = (jnp.cos(freqs), jnp.sin(freqs))
            q = q * cos * scale + rotate_half(q) * sin * scale
            k = k * cos / scale + rotate_half(k) * sin / scale
            return (q, k)

        def local_attention(q, k, v):
            b, h, n, d = q.shape
            w = n // WINDOW
            bq = q.reshape(b, h, w, WINDOW, d) * QK_SCALE
            bk = k.reshape(b, h, w, WINDOW, d)
            bv = v.reshape(b, h, w, WINDOW, d)

            def look_around(t):
                p = jnp.pad(t, ((0, 0), (0, 0), (1, 0), (0, 0), (0, 0)))
                return jnp.concatenate([p[:, :, :w], p[:, :, 1:]], axis=3)
            bk, bv = (look_around(bk), look_around(bv))
            bt = jnp.arange(n).reshape(w, WINDOW)
            btp = jnp.pad(bt, ((1, 0), (0, 0)), constant_values=-1)
            btk = jnp.concatenate([btp[:w], btp[1:]], axis=1)
            sim = jnp.einsum('bhwid,bhwjd->bhwij', bq, bk)
            i = bt[:, :, None]
            j = btk[:, None, :]
            mask = (i < j) | (i > j + WINDOW) | (j == -1)
            sim = jnp.where(mask, -jnp.finfo(sim.dtype).max, sim)
            attn = jax.nn.softmax(sim, axis=-1)
            out = jnp.einsum('bhwij,bhwjd->bhwid', attn, bv)
            return out.reshape(b, h, n, d)

        def _layer(x, wqkv, qs, ksc, wo, lg, lb, w1, b1, w2, b2):
            b, n, _ = x.shape
            h = shift_token(x)
            qkv = h @ wqkv
            q, k, v = jnp.split(qkv, 3, axis=-1)
            to_heads = lambda t: t.reshape(b, n, HEADS, DIM_HEAD).transpose(0, 2, 1, 3)
            q, k, v = (to_heads(q), to_heads(k), to_heads(v))
            q = l2norm(q) * qs
            k = l2norm(k) * ksc
            q, k = rotary_xpos(q, k)
            o = local_attention(q, k, v)
            o = o.transpose(0, 2, 1, 3).reshape(b, n, INNER)
            x = x + o @ wo
            h = shift_token(x)
            mu = h.mean(-1, keepdims=True)
            var = h.var(-1, keepdims=True)
            h = (h - mu) / jnp.sqrt(var + 1e-05) * lg + lb
            h = h @ w1 + b1
            a, g = jnp.split(h, 2, axis=-1)
            h = a * jax.nn.gelu(g, approximate=False)
            x = x + h @ w2 + b2
            return x
        for l in range(DEPTH):
            x = _layer(x, wqkv[l], q_scale[l], k_scale[l], wo[l], ln_g[l], ln_b[l], w1[l], b1[l], w2[l], b2[l])
        return x
    x = L0_attn_x
    x = x + _L0_attn_ref(_layernorm(x, axis=-1), L0_attn_w_cq, L0_attn_g_qnorm, L0_attn_w_dq_nope, L0_attn_w_dq_rope, L0_attn_w_ckv, L0_attn_g_kvnorm, L0_attn_w_dk_nope, L0_attn_w_dv, L0_attn_w_krope, L0_attn_w_imp, L0_attn_w_selk, L0_attn_w_selv, L0_attn_w_wink, L0_attn_w_winv, L0_attn_w_gate, L0_attn_w_proj)
    x = x + _L0_ffn_ref(_layernorm(x, axis=-1), L0_ffn_wqkv, L0_ffn_q_scale, L0_ffn_k_scale, L0_ffn_wo, L0_ffn_ln_g, L0_ffn_ln_b, L0_ffn_w1, L0_ffn_b1, L0_ffn_w2, L0_ffn_b2)
    return x

_drawn_inputs = setup_inputs


def setup_inputs(seed=0):
    import zlib

    import numpy as np

    out = dict(_drawn_inputs(seed))
    spreads = {'L0_attn_g_qnorm': (1.0, 0.6),
     'L0_attn_g_kvnorm': (1.0, 0.6),
     'L0_ffn_q_scale': (1.0, 0.6),
     'L0_ffn_k_scale': (1.0, 0.6),
     'L0_ffn_ln_g': (1.0, 0.6),
     'L0_ffn_ln_b': (0.0, 0.8),
     'L0_ffn_b1': (0.0, 0.8),
     'L0_ffn_b2': (0.0, 0.422)}
    factors = {'L0_attn_w_cq': 8.0,
     'L0_attn_w_dq_nope': 8.0,
     'L0_attn_w_dq_rope': 8.0,
     'L0_attn_w_ckv': 8.0,
     'L0_attn_w_dk_nope': 8.0,
     'L0_attn_w_dv': 8.0,
     'L0_attn_w_krope': 8.0,
     'L0_attn_w_imp': 6.524,
     'L0_attn_w_selk': 8.0,
     'L0_attn_w_selv': 6.221,
     'L0_attn_w_wink': 8.0,
     'L0_attn_w_winv': 8.0,
     'L0_attn_w_gate': 8.0,
     'L0_attn_w_proj': 5.981,
     'L0_ffn_wqkv': 3.977,
     'L0_ffn_wo': 3.976,
     'L0_ffn_w1': 6.157,
     'L0_ffn_w2': 6.061}
    for name, (base, spread) in spreads.items():
        noise = np.random.default_rng([zlib.crc32(name.encode()), seed]).standard_normal(out[name].shape)
        drawn = base * np.exp(spread * noise) if base else spread * noise
        out[name] = jnp.asarray(drawn.astype(out[name].dtype))
    for name, factor in factors.items():
        out[name] = (out[name] * factor).astype(out[name].dtype)
    return out
```

```python
from contextlib import ExitStack

import numpy as np

import concourse.bass as bass
from concourse import mybir
from concourse.alu_op_type import AluOpType as ALU

F32 = mybir.dt.float32
F32R = mybir.dt.float32r
BF16 = mybir.dt.bfloat16
ACT = mybir.ActivationFunctionType
AX = mybir.AxisListType

P = 128
B, T, C = 2, 1024, 128
NT = B * T // P
TB = T // P
H = 16
NOPE, ROPE, VD = 32, 64, 32
QK = NOPE + ROPE
HALF = ROPE // 2
KEEP = 32
QL, KVL = 96, 32
NBR = 3
BANK = 512
NEG = -1.0e30

DEPTH, FH, FD, WIN = 2, 8, 64, 64
INNER = FH * FD
HID = int(C * 4 * 2 / 3)
HCH = [(0, 114), (114, 114), (228, 113)]


class Sems:

    def __init__(self, nc, ctx, stage):
        self.nc, self.ctx, self.stage, self.made = nc, ctx, stage, {}

    def __call__(self, name):
        if name not in self.made:
            self.made[name] = self.ctx.enter_context(self.nc.semaphore(self.stage + name))
        return self.made[name]

    def clear(self, eng):
        for made in self.made.values():
            eng.sem_clear(made)


def wait_past(eng, sem, value):
    if not (isinstance(value, int) and value <= 0):
        eng.wait_ge(sem, value)


def wait_apart(eng, S, sem, value):
    wait_past(eng, sem, value)
    eng.sem_inc(S(f"passed_{eng.engine.name}"), 1)


def prepare(nc, ins, K, ps, S):
    with ExitStack() as ctx:
        def sb(name, shape, dt=F32):
            return ctx.enter_context(nc.sbuf_tensor(name, shape, dt))

        stats = sb("stats", [P, NT, 6])
        mv = sb("mv", [P, NT, 2])
        rstd = sb("rstd", [P, NT])
        std = sb("std", [P, NT])
        y = sb("y", [P, NT, C])
        wc = sb("wc", [P, QL + KVL + ROPE])
        wimp = sb("wimp", [P, 1])
        wgate = sb("wgate", [P, 3])
        gq = sb("gq", [QL, 1])
        gqs = sb("gqs", [QL, 1])
        gkv = sb("gkv", [96, 1])
        cosn = sb("cosn", [P, TB, HALF])
        sinn = sb("sinn", [P, TB, HALF])
        iota = sb("iota", [P, KEEP])
        onehot3 = sb("onehot3", [99, 3])
        z = sb("z", [P, NT, QL + KVL + ROPE])
        ssq = sb("ssq", [P, 2, NT])
        sroot = sb("sroot", [P, 2, NT])
        srec = sb("srec", [P, 2, NT])
        sqj = sb("sqj", [P, QL])
        zq = sb("zq", [P, NT, QL])
        zk = sb("zk", [P, NT, ROPE + KVL])
        ra = sb("ra", [P, TB, HALF])
        rb = sb("rb", [P, TB, HALF])
        sc = sb("sc", [33, T])
        scw = sb("scw", [33, 2, T])
        top = sb("top", [33, 4, 8])
        selm = sb("selm", [33, T])
        rank = sb("rank", [33, T])
        one1 = sb("one1", [33, 1])
        rkn = sb("rkn", [P, NT])
        hot = sb("hot", [P, NT, KEEP])
        ysum = sb("ysum", [P, B])
        gl = sb("gl", [96, B, 3])
        gm = sb("gm", [96, B])
        ge = sb("ge", [96, B, 3])
        gs = sb("gs", [96, B])
        gr = sb("gr", [96, B])

        block = ctx.enter_context(nc.Block())
        res, yT, nqT, kcT = K["res"], K["yT"], K["nqT"], K["kcT"]

        x_v = ins["L0_attn_x"].rearrange("b (t p) c -> p (b t) c", p=P)
        consts = [
            (K["ident"][:], ins["c_ident"]), (K["maskf"][:], ins["c_causal"]),
            (K["cosT"][:], ins["c_cosT"]), (K["sinT"][:], ins["c_sinT"]),
            (cosn[:], ins["c_cosN"].rearrange("(t p) d -> p t d", p=P)),
            (sinn[:], ins["c_sinN"].rearrange("(t p) d -> p t d", p=P)),
            (iota[:], ins["c_iota"]), (onehot3[96:99, :], ins["c_ident"][0:3, 0:3]),
            (wc[:, 0:QL], ins["L0_attn_w_cq"]), (wc[:, QL:QL + KVL], ins["L0_attn_w_ckv"]),
            (wc[:, QL + KVL:], ins["L0_attn_w_krope"]),
            (wimp[:], ins["L0_attn_w_imp"]), (wgate[:], ins["L0_attn_w_gate"]),
            (gq[:], ins["L0_attn_g_qnorm"].rearrange("(a o) -> a o", o=1)),
            (gkv[64:96, :], ins["L0_attn_g_kvnorm"].rearrange("(a o) -> a o", o=1)),
        ]

        @block.sync
        def _(sp):
            for c in range(4):
                sp.dma_start(res[:, 4 * c:4 * c + 4, :], x_v[:, 4 * c:4 * c + 4, :]).then_inc(S(f"x_loaded{c}"), 16)
            for dst, src in consts:
                sp.dma_start(dst, src).then_inc(S("consts_loaded"), 16)

        ALLC = 16 * len(consts)

        @block.vector
        def _(dve):
            for t in range(NT):
                if t % 4 == 0:
                    dve.wait_ge(S(f"x_loaded{t // 4}"), 16)
                dve.bn_stats(stats[:, t, :], res[:, t, :]).then_inc(S("ln_stats"), 1)
            for t in range(NT):
                dve.wait_ge(S("ln_stats"), t + 1)
                dve.bn_aggr(mv[:, t, :], stats[:, t, :]).then_inc(S("ln_aggr"), 1)
            dve.wait_ge(S("ln_aggr"), NT)
            dve.tensor_scalar(rstd[:], mv[:, :, 1], 1e-5, None, ALU.add).then_inc(S("ln_var"), 1)
            dve.wait_ge(S("ln_std"), 1)
            dve.reciprocal(rstd[:], std[:]).then_inc(S("ln_rstd"), 1)
            dve.wait_ge(S("ln_rstd"), 1)
            for t in range(NT):
                dve.tensor_scalar(y[:, t, :], res[:, t, :], mv[:, t, 0:1], rstd[:, t:t + 1],
                                  ALU.subtract, ALU.mult).then_inc(S("y_ready"), 1)
            dve.wait_ge(S("consts_loaded"), ALLC)
            dve.tensor_copy(K["identb"][:], K["ident"][:]).then_inc(S("misc_const"), 1)
            dve.tensor_copy(K["maskb"][:], K["maskf"][:]).then_inc(S("misc_const"), 1)
            dve.memset(K["ones"][:], 1.0).then_inc(S("misc_const"), 1)
            dve.memset(sc[:], 0.0).then_inc(S("sc_zero"), 1)
            dve.memset(one1[:], 1.0).then_inc(S("one1"), 1)
            dve.tensor_scalar(gqs[:], gq[:], float(QK) ** -0.5, None, ALU.mult).then_inc(S("gqs"), 1)
            for t in range(NT):
                dve.wait_ge(S("lat_full"), t + 1)
                dve.tensor_copy(z[:, t, :], ps[:, 4 + t % 2, 0:QL + KVL + ROPE]).then_inc(S("lat_copied"), 1)
            for b in range(B):
                dve.wait_ge(S("yT"), 2 * b + 2)
                dve.tensor_reduce(ysum[:, b:b + 1], yT[:, T * b:T * (b + 1)], AX.X, ALU.add).then_inc(S("ysum"), 1)
            for b in range(B):
                for c in range(2):
                    i = 2 * b + c
                    dve.wait_ge(S("imp_full"), i + 1)
                    if i == 0:
                        dve.wait_ge(S("sc_zero"), 1)
                    dve.tensor_copy(sc[32 * b:32 * b + 1, BANK * c:BANK * (c + 1)],
                                    ps[32 * b:32 * b + 1, 6 + c, :]).then_inc(S("imp_copied"), 1)
            dve.wait_ge(S("squares"), 2 * NT)
            dve.tensor_scalar(sroot[:, 0, :], ssq[:, 0, :], 1.0 / QL, 1e-6, ALU.mult, ALU.add).then_inc(S("msq"), 1)
            dve.tensor_scalar(sroot[:, 1, :], ssq[:, 1, :], 1.0 / KVL, 1e-6, ALU.mult, ALU.add).then_inc(S("msq"), 1)
            dve.wait_ge(S("rms"), 1)
            dve.reciprocal(srec[:], sroot[:]).then_inc(S("rrms"), 1)
            dve.wait_ge(S("rrms"), 1)
            dve.wait_ge(S("lat_copied"), NT)
            dve.tensor_tensor(zq[:], z[:, :, 0:QL], srec[:, 0, :].unsqueeze(2).to_broadcast([P, NT, QL]),
                              ALU.mult).then_inc(S("zq"), 1)
            dve.tensor_tensor(zk[:, :, ROPE:], z[:, :, QL:QL + KVL],
                              srec[:, 1, :].unsqueeze(2).to_broadcast([P, NT, KVL]), ALU.mult).then_inc(S("zk"), 1)
            kr = QL + KVL
            n = 0
            for b in range(B):
                tt = slice(TB * b, TB * (b + 1))
                x1, x2 = z[:, tt, kr:kr + HALF], z[:, tt, kr + HALF:kr + ROPE]
                for o, (u, v, op) in enumerate([(x1, x2, ALU.subtract), (x2, x1, ALU.add)]):
                    if n:
                        dve.wait_ge(S("kr_rot"), n)
                    dve.scalar_tensor_tensor(out=ra[:], in0=u, scalar=1.0 / H, in1=cosn[:], op0=ALU.mult, op1=ALU.mult).then_inc(S("kr_terms"), 1)
                    dve.scalar_tensor_tensor(out=rb[:], in0=v, scalar=1.0 / H, in1=sinn[:], op0=ALU.mult, op1=ALU.mult).then_inc(S("kr_terms"), 1)
                    n += 1
                    dve.wait_ge(S("kr_terms"), 2 * n)
                    dve.tensor_tensor(zk[:, tt, HALF * o:HALF * (o + 1)], ra[:], rb[:], op).then_inc(S("kr_rot"), 1)
            dve.wait_ge(S("imp_copied"), 4)
            cur = sc[:]
            for r in range(4):
                if r:
                    dve.wait_ge(S("top_round"), r)
                dve.max(top[:, r, :], cur).then_inc(S("top_found"), 1)
                dve.wait_ge(S("top_found"), r + 1)
                dve.match_replace(scw[:, r % 2, :], top[:, r, :], cur, -3.0e38).then_inc(S("top_round"), 1)
                cur = scw[:, r % 2, :]
            dve.wait_ge(S("top_round"), 4)
            dve.tensor_tensor(selm[:], cur, sc[:], ALU.not_equal).then_inc(S("selm"), 1)
            dve.wait_ge(S("selm"), 1)
            dve.wait_ge(S("misc_const"), 3)
            dve.tensor_tensor_scan(rank[:], K["ones"][0:33, 0:1].to_broadcast([33, T]), selm[:], 0.0,
                                   ALU.mult, ALU.add).then_inc(S("rank0"), 1)
            dve.wait_ge(S("rank0"), 1)
            dve.tensor_tensor(selm[:], rank[:], selm[:], ALU.mult).then_inc(S("rank1"), 1)
            dve.wait_ge(S("rank1"), 1)
            dve.tensor_scalar(rank[:], selm[:], -1.0, None, ALU.add).then_inc(S("rank2"), 1)
            dve.wait_ge(S("rankn_full"), 1)
            for b in range(B):
                tt = slice(TB * b, TB * (b + 1))
                dve.tensor_copy(rkn[:, tt], ps[:, 6 - 2 * b, tt]).then_inc(S("rankn"), 1)
            dve.wait_ge(S("rankn"), 2)
            for t in range(NT):
                dve.tensor_scalar(hot[:, t, :], iota[:], rkn[:, t:t + 1], None, ALU.is_equal).then_inc(S("hot"), 1)
            dve.wait_ge(S("sel_full"), 1)
            dve.tensor_copy(K["selT"][:], ps[:, 7, 0:B * KEEP]).then_inc(S("selT"), 1)
            dve.wait_ge(S("gate_full"), 1)
            dve.tensor_scalar(gl[:], ps[0:96, 5, 0:B * 3].rearrange("p (b g) -> p b g", b=B), 1.0 / T, None,
                              ALU.mult).then_inc(S("gl"), 1)
            dve.wait_ge(S("gl"), 1)
            dve.tensor_reduce(gm[:], gl[:], AX.X, ALU.max).then_inc(S("gm"), 1)
            dve.wait_ge(S("gm"), 1)
            dve.tensor_tensor(ge[:], gl[:], gm[:].unsqueeze(2).to_broadcast([96, B, 3]), ALU.subtract).then_inc(S("gd"), 1)
            dve.wait_ge(S("gexp"), 1)
            dve.tensor_reduce(gs[:], gl[:], AX.X, ALU.add).then_inc(S("gs"), 1)
            dve.wait_ge(S("gs"), 1)
            dve.reciprocal(gr[:], gs[:]).then_inc(S("gr"), 1)
            dve.wait_ge(S("gr"), 1)
            for n, g in enumerate((0, 2, 1)):
                rows = slice(32 * n, 32 * n + 32)
                dve.tensor_tensor(K["gcol"][rows, :], gl[rows, :, g], gr[rows, :], ALU.mult).then_inc(S("gcol"), 1)
            for i in range(4):
                b, c = i // 2, i % 2
                cols = slice(BANK * c, BANK * (c + 1))
                dve.wait_ge(S("krH"), i + 1)
                dve.tensor_tensor(K["kL1"][b][0:ROPE, cols], ps[0:ROPE, i, :], K["kH1"][b][0:ROPE, cols].bitcast(F32),
                                  ALU.subtract).then_inc(S("krL"), 1)
            for b in range(B):
                for n, k in enumerate(("kH1", "kHw", "kH2")):
                    w = KEEP if k == "kH2" else T
                    dve.tensor_copy(K[k][b][96:99, :], onehot3[96:99, n:n + 1].to_broadcast([3, w])).then_inc(S("aug"), 1)

        @block.scalar
        def _(act):
            act.wait_ge(S("ln_var"), 1)
            act.activation(std[:], rstd[:], ACT.Sqrt).then_inc(S("ln_std"), 1)
            for g in range(4):
                act.wait_ge(S("yT_full"), g + 1)
                act.activation(yT[:, BANK * g:BANK * (g + 1)], ps[:, g, :], ACT.Copy).then_inc(S("yT"), 1)
            for t in range(NT):
                act.wait_ge(S("lat_copied"), t + 1)
                for n, (o, w) in enumerate(((0, QL), (QL, KVL))):
                    if 2 * t + n:
                        act.wait_ge(S("squares"), 2 * t + n)
                    act.activation(sqj[:, 0:w], z[:, t, o:o + w], ACT.Square,
                                   accum_out=ssq[:, n, t:t + 1]).then_inc(S("squares"), 1)
            act.wait_ge(S("msq"), 2)
            act.activation(sroot[:], sroot[:], ACT.Sqrt).then_inc(S("rms"), 1)
            act.wait_ge(S("gqs"), 1)
            for g in range(4):
                act.wait_ge(S("nq_full"), g + 1)
                act.activation(nqT[:, BANK * g:BANK * (g + 1)], ps[0:QL, g, :], ACT.Copy, scale=gqs[:]).then_inc(S("nqT"), 1)
            for i in range(4):
                b, c = i // 2, i % 2
                act.wait_ge(S("kc_full"), i + 1)
                act.activation(kcT[64:96, BANK * i:BANK * (i + 1)], ps[64:96, i, :], ACT.Copy, scale=gkv[64:96, :]).then_inc(S("kcT"), 1)
                act.activation(K["kH1"][b][0:ROPE, BANK * c:BANK * (c + 1)], ps[0:ROPE, i, :], ACT.Copy).then_inc(S("krH"), 1)
            act.wait_ge(S("gd"), 1)
            act.activation(gl[:], ge[:], ACT.Exp).then_inc(S("gexp"), 1)

        @block.tensor
        def _(pe):
            ident = K["ident"]
            pe.wait_ge(S("consts_loaded"), ALLC)
            for t in range(NT):
                pe.wait_ge(S("y_ready"), t + 1)
                mm = pe.transpose(ps[:, t // 4, P * (t % 4):P * (t % 4 + 1)], y[:, t, :], ident[:])
                if t % 4 == 3:
                    mm.then_inc(S("yT_full"), 1)
            for t in range(NT):
                if t % 4 == 0:
                    pe.wait_ge(S("yT"), t // 4 + 1)
                if t >= 2:
                    pe.wait_ge(S("lat_copied"), t - 1)
                pe.matmul(ps[:, 4 + t % 2, 0:QL + KVL + ROPE], yT[:, P * t:P * (t + 1)], wc[:],
                          start=True, stop=True).then_inc(S("lat_full"), 1)
            for i in range(4):
                b, c = i // 2, i % 2
                if b:
                    pe.wait_ge(S("imp_copied"), i - 1)
                pe.matmul(ps[32 * b:32 * b + 1, 6 + c, :], wimp[:], yT[:, BANK * i:BANK * (i + 1)],
                          start=True, stop=True).then_inc(S("imp_full"), 1)
            pe.wait_ge(S("ysum"), 2)
            pe.wait_ge(S("lat_copied"), NT)
            for b in range(B):
                mm = pe.matmul(ps[0:96, 5, 3 * b:3 * b + 3], ysum[:, b:b + 1].to_broadcast([P, 96]), wgate[:],
                               start=True, stop=True)
            mm.then_inc(S("gate_full"), 1)
            pe.wait_ge(S("zq"), 1)
            for t in range(NT):
                mm = pe.transpose(ps[0:QL, t // 4, P * (t % 4):P * (t % 4 + 1)], zq[:, t, :], ident[:])
                if t % 4 == 3:
                    mm.then_inc(S("nq_full"), 1)
            pe.wait_ge(S("zk"), 1)
            pe.wait_ge(S("kr_rot"), 2 * B)
            for t in range(NT):
                if t % 4 == 0:
                    pe.wait_ge(S("nqT"), t // 4 + 1)
                mm = pe.transpose(ps[0:96, t // 4, P * (t % 4):P * (t % 4 + 1)], zk[:, t, :], ident[:])
                if t % 4 == 3:
                    mm.then_inc(S("kc_full"), 1)
            pe.wait_ge(S("rank2"), 1)
            pe.wait_ge(S("one1"), 1)
            for t in range(NT):
                b, r = t // TB, 32 * (t // TB)
                mm = pe.matmul(ps[:, 6 - 2 * b, t:t + 1], rank[r:r + 1, P * (t % TB):P * (t % TB + 1)], one1[r:r + 1, :],
                               start=True, stop=True)
            mm.then_inc(S("rankn_full"), 1)
            for t in range(NT):
                b = t // TB
                pe.wait_ge(S("hot"), t + 1)
                mm = pe.matmul(ps[:, 7, KEEP * b:KEEP * (b + 1)], y[:, t, :], hot[:, t, :],
                               start=(t % TB == 0), stop=(t % TB == TB - 1))
            mm.then_inc(S("sel_full"), 1)


class Ring:

    def __init__(self, first, loop, last, first_loop_slots):
        self.per = [sum(1 for i in range(len(loop)) if i % 2 == k) for k in (0, 1)]
        self.head = [sum(1 for i in range(len(first)) if i % 2 == k) for k in (0, 1)]
        self.place = {"first": {n: i for i, n in enumerate(first)}, "loop": {n: i for i, n in enumerate(loop)},
                      "last": {n: i for i, n in enumerate(last)}}

    def at(self, kind, slot, item):
        i = self.place[kind][item]
        k = i % 2
        return k, (i // 2 if kind == "first" else self.head[k] + self.per[k] * slot + i // 2)


COMING = {"q", "qh", "k", "kh", "n", "v", "k2", "mt"}


def score_tiles():
    return [(a, j, c) for a in (0, 1) for j in range(TB) for c in range(1 + (j >= 4))]


def timeline():
    mx = [("mx", *x) for x in score_tiles()]
    steps = [("q",), ("B", 0), ("k",), ("qh",), ("n",), ("B", 1), ("kh",), ("v",), ("a2s",), ("k2",), ("B", 2)]
    steps += mx[0:4] + [("a2o",), ("B", 3)] + mx[4:8] + [("B", 4)] + mx[8:12] + [("B", 5)]
    steps += mx[12:15] + [("B", 6)] + mx[15:17] + [("B", 7), ("mx2",)] + mx[17:19] + [("B", 8), ("norm",)]
    steps += mx[19:] + [("mt",), ("wp",)]
    return steps


def is_coming(step):
    return step[0] in COMING or step[0] in ("mx", "mx2")


def items_of(steps):
    out = []
    for s in steps:
        if s[0] in ("q", "k", "n", "a2o", "wp"):
            out += [(s[0], 0), (s[0], 1)]
        elif s[0] in ("v", "k2", "mx", "mx2", "mt"):
            out.append(s)
    return out


def latent_attention(nc, ins, K, ps, S, before):
    steps = timeline()
    first = [s for s in steps if is_coming(s)]
    last = [s for s in steps if not is_coming(s)]
    assert len(items_of(steps)) % 2 == 0
    ring = Ring(items_of(first), items_of(steps), items_of(last), 0)
    which = {"first": first, "loop": steps, "last": last}

    with ExitStack() as ctx:
        def sb(name, shape, dt=F32):
            return ctx.enter_context(nc.sbuf_tensor(name, shape, dt))

        wq = sb("wq", [QL, QK])
        wk = sb("wk", [P, QK])
        wks = sb("wks", [P, QK])
        wdk = sb("wdk", [96, NOPE])
        wdv = sb("wdv", [96, VD])
        wvw = sb("wvw", [P, VD])
        wvs = sb("wvs", [P, VD])
        wp = sb("wp", [96, C])
        wpg = [sb(f"wpg{b}", [96, C]) for b in range(B)]
        qf = sb("qf", [QK, T])
        qt = sb("qt", [ROPE, T])
        kf = sb("kf", [QK, T])
        kt = sb("kt", [ROPE, T])
        k2f = sb("k2f", [QK, KEEP])
        k2t = sb("k2t", [ROPE, KEEP])
        qH = [sb(f"qH{b}", [99, T], F32R) for b in range(B)]
        qL_ = [sb(f"qL{b}", [QK, T], F32R) for b in range(B)]
        kH = [K["kH1"], K["kHw"], K["kH2"]]
        kL = [K["kL1"], [sb(f"kLw{b}", [QK, T], F32R) for b in range(B)], [sb(f"kL2{b}", [QK, KEEP], F32R) for b in range(B)]]
        V = [sb(f"V{b}", [P, 2, TB, VD]) for b in range(B)]
        V2 = [sb(f"V2{b}", [KEEP, 2 * VD]) for b in range(B)]
        mpart = sb("mpart", [P, 2, 4])
        mneg = sb("mneg", [P, NBR, TB])
        mT = sb("mT", [NBR * TB, P], F32R)
        pr = [[sb(f"pr{a}{n}", [P, T]) for n in range(2)] for a in range(2)]
        p2 = sb("p2", [KEEP, T])
        lnD = sb("lnD", [96, T])
        rD = sb("rD", [96, T])
        tO = [sb(f"tO{b}", [96, T]) for b in range(B)]
        res, yT, nqT, kcT, ones = K["res"], K["yT"], K["nqT"], K["kcT"], K["ones"]
        cosT, sinT, ident, selT = K["cosT"], K["sinT"], K["ident"], K["selT"]

        def st(a, lo, hi):
            return ps[:, 2 * a:2 * a + 2, :].rearrange("p a n -> p (a n)")[:, lo:hi]

        out_ps = ps[:, 4:6, :].rearrange("p a n -> p (a n)")

        def bank(k):
            return ps[:, 6 + k, :]

        def pieces(i):
            return [(max(P * i, BANK * c), BANK * (c + 1)) for c in range(2) if P * i < BANK * (c + 1)]

        block = ctx.enter_context(nc.Block())
        full = [S("spare0_filled"), S("spare1_filled")]
        free = [S("spare0_read"), S("spare1_read")]

        w_q_nope, w_q_rope = ins["L0_attn_w_dq_nope"], ins["L0_attn_w_dq_rope"]
        w_wink, w_selk = ins["L0_attn_w_wink"], ins["L0_attn_w_selk"]

        def per_head(ap, width):
            return ap.rearrange("k (h d) -> h k d", d=width)

        def head_loads(h):
            nope, rope = slice(ROPE, QK), slice(0, ROPE)
            return [
                (wq[:, rope], per_head(w_q_rope, ROPE)[h]), (wq[:, nope], per_head(w_q_nope, NOPE)[h]),
                (wk[:, nope], per_head(w_wink, QK)[h, :, 0:NOPE]), (wk[:, rope], per_head(w_wink, QK)[h, :, NOPE:QK]),
                (wks[:, nope], per_head(w_selk, QK)[h, :, 0:NOPE]), (wks[:, rope], per_head(w_selk, QK)[h, :, NOPE:QK]),
                (wdk[64:96, :], per_head(ins["L0_attn_w_dk_nope"], NOPE)[h]),
                (wdv[64:96, :], per_head(ins["L0_attn_w_dv"], VD)[h]),
                (wvw[:], per_head(ins["L0_attn_w_winv"], VD)[h]), (wvs[:], per_head(ins["L0_attn_w_selv"], VD)[h]),
            ]

        NLOAD = 16 * 10
        wproj = ins["L0_attn_w_proj"].rearrange("(h d) c -> h d c", d=VD)

        def run_slots(eng, slot):
            slot("first", -1, -1, 1)
            with eng.Fori(0, H - 1) as h:
                slot("loop", 2 * h, h, 0)
                slot("loop", 2 * h + 1, h, 1)
            slot("loop", 2 * (H - 1), H - 1, 0)
            slot("last", 2 * H - 1, H - 1, 1)

        @block.sync
        def _(sp):
            before.clear(sp)
            for dst, src in head_loads(0):
                sp.dma_start(dst, src).then_inc(S("head_loaded"), 16)
            for n in range(NBR):
                sp.dma_start(wp[32 * n:32 * n + 32, :], wproj[0]).then_inc(S("wp_loaded"), 16)

            def slot(kind, s, h, b):
                u, ub = s + 1, 1 - b
                if kind != "first" and b == 1 and kind != "last":
                    sp.wait_ge(S("wpg_done"), 2 * h + 2)
                    for n in range(NBR):
                        sp.dma_start(wp[32 * n:32 * n + 32, :], wproj[h + 1]).then_inc(S("wp_loaded"), 16)
                if kind == "loop" and b == 0 and not (isinstance(h, int) and h == H - 1):
                    k, n = ring.at(kind, s, ("k2",))
                    sp.wait_ge(full[k], n + 1)
                    for dst, src in head_loads(h + 1):
                        sp.dma_start(dst, src).then_inc(S("head_loaded"), 16)
                if kind != "last":
                    k, n = ring.at(kind, s, ("mt",))
                    sp.wait_ge(free[k], n + 1)
                    for n in range(NBR):
                        sp.dma_start(qH[ub][96 + n:97 + n, :].bitcast(F32).rearrange("a (j p) -> a j p", p=P),
                                     mT[TB * n:TB * (n + 1), :].bitcast(F32)).then_inc(S(f"maxrows{ub}"), 16)

            run_slots(sp, slot)

        @block.tensor
        def _(pe):
            def slot(kind, s, h, b):
                u, ub = s + 1, 1 - b
                hu = h + 1 if b == 1 else h

                def take(item):
                    k, n = ring.at(kind, s, item)
                    wait_past(pe, free[k], n)
                    return k

                def product(k, out, lhsT, rhs, start=True, stop=True):
                    return pe.matmul(out, lhsT, rhs, start=start, stop=stop)

                def scores(a, i):
                    n = TB * s + i if a else (TB + 1) * s + i + (i >= 2)
                    wait_past(pe, S(f"st{a}_read"), n)
                    ks = slice(P * i, P * (i + 1))
                    for m, (lo, hi) in enumerate(pieces(i)):
                        pe.matmul(st(a, lo, hi), kH[a][b][0:QK, ks], qL_[b][:, lo:hi], start=True, stop=False)
                        pe.matmul(st(a, lo, hi), kL[a][b][:, ks], qH[b][0:QK, lo:hi], start=False, stop=False)
                        mm = pe.matmul(st(a, lo, hi), kH[a][b][0:99, ks], qH[b][0:99, lo:hi], start=False, stop=True)
                    mm.then_inc(S(f"st{a}_filled"), 1)

                def weighted(i):
                    for a in range(2):
                        pe.wait_ge(S(f"probs{a}"), TB * s + i + 1)
                    if i == 0:
                        wait_past(pe, S("out_read"), s)
                    for lo, hi in pieces(i):
                        stop = (i == TB - 1) or (i == 3 and hi == BANK)
                        for g, (a, lhsT) in enumerate(((0, V[b][:, 0, i, :]), (1, V[b][:, 1, i, :]),
                                                       (0, ones[:]), (1, ones[:]))):
                            mm = pe.matmul(out_ps[32 * g:32 * g + 32, lo:hi], lhsT, pr[a][i % 2][:, lo:hi],
                                           start=(i == 0), stop=stop)
                    mm.then_inc(S("weighted"), 1)

                for step in which[kind]:
                    op = step[0]
                    if op == "q":
                        pe.wait_ge(S("head_loaded"), NLOAD * (hu + 1))
                        for c in range(2):
                            k = take((op, c))
                            pe.matmul(bank(k)[0:QK, :], wq[:], nqT[:, T * ub + BANK * c:T * ub + BANK * (c + 1)],
                                      start=True, stop=True).then_inc(full[k], 1)
                    elif op == "k":
                        for c in range(2):
                            k = take((op, c))
                            pe.matmul(bank(k)[0:QK, :], wk[:], yT[:, T * ub + BANK * c:T * ub + BANK * (c + 1)],
                                      start=True, stop=True).then_inc(full[k], 1)
                    elif op == "n":
                        for c in range(2):
                            k, m = ring.at(kind, s, (op, c))
                            wait_apart(pe, S, free[k], m)
                            pe.matmul(bank(k)[64:96, :], wdk[64:96, :],
                                      kcT[64:96, T * ub + BANK * c:T * ub + BANK * (c + 1)],
                                      start=True, stop=True).then_inc(full[k], 1)
                    elif op == "v":
                        k = take(step)
                        for t in range(TB):
                            tok = slice(T * ub + P * t, T * ub + P * (t + 1))
                            pe.matmul(bank(k)[:, VD * t:VD * (t + 1)], kcT[64:96, tok], wdv[64:96, :], start=True, stop=True)
                        for t in range(TB):
                            tok = slice(T * ub + P * t, T * ub + P * (t + 1))
                            mm = pe.matmul(bank(k)[:, 256 + VD * t:256 + VD * (t + 1)], yT[:, tok], wvw[:], start=True, stop=True)
                        mm.then_inc(full[k], 1)
                    elif op == "k2":
                        k = take(step)
                        sel = selT[:, KEEP * ub:KEEP * (ub + 1)]
                        pe.matmul(bank(k)[0:QK, 0:KEEP], wks[:], sel, start=True, stop=True)
                        pe.matmul(bank(k)[0:KEEP, 64:64 + VD], sel, wvs[:], start=True, stop=True).then_inc(full[k], 1)
                    elif op == "mx":
                        _, a, j, c = step
                        k = take(step)
                        if j == 0:
                            pe.wait_ge(S("qH_done"), 2 * (u + 1))
                            pe.wait_ge(S("kHw_done") if a else S("kH1_done"), 2 * (u + 1))
                        hi = min(P * (j + 1), BANK * (c + 1))
                        w = hi - BANK * c
                        diag = hi == P * (j + 1)
                        mm = pe.matmul(bank(k)[:, 0:w], qH[ub][0:QK, P * j:P * (j + 1)], kH[a][ub][0:QK, BANK * c:hi],
                                       start=True, stop=not diag)
                        if diag:
                            mm = pe.matmul(bank(k)[:, w - P:w], K["identb"][:], K["maskb"][:], start=False, stop=True)
                        mm.then_inc(full[k], 1)
                    elif op == "mx2":
                        k = take(step)
                        pe.wait_ge(S("k2_done"), u + 1)
                        for j in range(TB):
                            mm = pe.matmul(bank(k)[:, KEEP * j:KEEP * (j + 1)], qH[ub][0:QK, P * j:P * (j + 1)],
                                           kH[2][ub][0:QK, :], start=True, stop=True)
                        mm.then_inc(full[k], 1)
                    elif op == "mt":
                        k = take(step)
                        pe.wait_ge(S("mneg"), u + 1)
                        pe.transpose(bank(k)[0:NBR * TB, 0:P], mneg[:].rearrange("p a j -> p (a j)"), ident[:]).then_inc(full[k], 1)
                    elif op == "B":
                        i = step[1]
                        if i == 0:
                            pe.wait_ge(S(f"maxrows{b}"), 48 * (h + 1))
                            pe.wait_ge(S("qL_done"), s + 1)
                            pe.wait_ge(S("kLw_done"), s + 1)
                        if i < TB:
                            scores(0, i)
                            scores(1, i)
                        if i:
                            weighted(i - 1)
                    elif op == "a2s":
                        wait_past(pe, S("st0_read"), (TB + 1) * s + 2)
                        pe.wait_ge(S("k2_done"), s + 1)
                        for lo, hi in pieces(0):
                            o = st(0, lo, hi)[0:KEEP, :]
                            pe.matmul(o, kH[2][b][0:QK, :], qL_[b][:, lo:hi], start=True, stop=False)
                            pe.matmul(o, kL[2][b][:], qH[b][0:QK, lo:hi], start=False, stop=False)
                            mm = pe.matmul(o, kH[2][b][0:99, :], qH[b][0:99, lo:hi], start=False, stop=True)
                        mm.then_inc(S("st0_filled"), 1)
                    elif op == "a2o":
                        pe.wait_ge(S("st0_read"), (TB + 1) * s + 3)
                        for c in range(2):
                            k = take((op, c))
                            cols = slice(BANK * c, BANK * (c + 1))
                            pe.matmul(bank(k)[64:128, :], V2[b][:], p2[:, cols], start=True, stop=True).then_inc(full[k], 1)
                    elif op == "wp":
                        pe.wait_ge(S("out_read"), s + 1)
                        pe.wait_ge(S("wpg_done"), s + 1)
                        for c in range(2):
                            k = take((op, c))
                            for t in range(4):
                                j = 4 * c + t
                                mm = pe.matmul(bank(k)[:, P * t:P * (t + 1)], tO[b][:, P * j:P * (j + 1)], wpg[b][:],
                                               start=True, stop=True)
                            mm.then_inc(full[k], 1)

            run_slots(pe, slot)

        @block.scalar
        def _(act):
            def slot(kind, s, h, b):
                u, ub = s + 1, 1 - b

                def filled(item):
                    k, n = ring.at(kind, s, item)
                    act.wait_ge(full[k], n + 1)
                    return k

                def exponentials(a, i):
                    n = TB * s + i if a else (TB + 1) * s + i + (i >= 2)
                    act.wait_ge(S(f"st{a}_filled"), n + 1)
                    wait_past(act, S("weighted"), TB * s + max(i - 1, 0))
                    act.activation(pr[a][i % 2][:, P * i:T], st(a, P * i, T), ACT.Exp).then_inc(S(f"st{a}_read"), 1)

                for step in which[kind]:
                    op = step[0]
                    if op in ("q", "k"):
                        dst = qf if op == "q" else kf
                        wait_past(act, S("qL_done" if op == "q" else "kLw_done"), u)
                        for c in range(2):
                            k = filled((op, c))
                            act.activation(dst[64:96, BANK * c:BANK * (c + 1)], bank(k)[64:96, :], ACT.Copy).then_inc(S(f"{op}plain"), 1)
                    elif op in ("qh", "kh"):
                        o, src, dst = ("q", qf, qH[ub]) if op == "qh" else ("k", kf, kH[1][ub])
                        name = "qH_done" if op == "qh" else "kHw_done"
                        act.wait_ge(S(f"{o}plain"), 2 * (u + 1))
                        act.wait_ge(S(f"{o}rot"), u + 1)
                        for c in range(2):
                            act.activation(dst[0:QK, BANK * c:BANK * (c + 1)], src[:, BANK * c:BANK * (c + 1)], ACT.Copy).then_inc(S(name), 1)
                    elif op == "n":
                        for c in range(2):
                            k = filled((op, c))
                            act.activation(kH[0][ub][64:96, BANK * c:BANK * (c + 1)], bank(k)[64:96, :], ACT.Copy).then_inc(S("kH1_done"), 1)
                    elif op == "v":
                        k = filled(step)
                        act.activation(V[ub][:].rearrange("p a t d -> p (a t d)"), bank(k), ACT.Copy).then_inc(free[k], 1)
                    elif op == "mt":
                        k = filled(step)
                        if kind == "first":
                            pass
                        elif b == 0:
                            act.wait_ge(S("maxrows0"), 48 * (h + 1))
                        else:
                            act.wait_ge(S("maxrows1"), 48 * (h + 1))
                        act.activation(mT[:], bank(k)[0:NBR * TB, 0:P], ACT.Copy).then_inc(free[k], 1)
                    elif op == "B":
                        i = step[1]
                        if i < TB:
                            exponentials(0, i)
                            exponentials(1, i)
                    elif op == "a2s":
                        act.wait_ge(S("st0_filled"), (TB + 1) * s + 3)
                        act.activation(p2[:], st(0, 0, T)[0:KEEP, :], ACT.Exp).then_inc(S("st0_read"), 1)
                    elif op == "a2o":
                        for c in range(2):
                            k = filled((op, c))
                            cols = slice(BANK * c, BANK * (c + 1))
                            act.activation(lnD[64:96, cols], bank(k)[96:128, :], ACT.Ln).then_inc(S("ln2"), 1)
                            act.wait_ge(S("ln2"), 2 * s + c + 1)
                            act.activation(rD[64:96, cols], lnD[64:96, cols], ACT.Exp, scale=-1.0).then_inc(S("rD2"), 1)
                    elif op == "norm":
                        act.wait_ge(S("weighted"), TB * (s + 1))
                        act.activation(lnD[0:64, :], out_ps[64:128, :], ACT.Ln).then_inc(S("ln01"), 1)
                        act.wait_ge(S("ln01"), s + 1)
                        act.activation(rD[0:64, :], lnD[0:64, :], ACT.Exp, scale=-1.0).then_inc(S("rD01"), 1)

            run_slots(act, slot)

        @block.gpsimd
        def _(pool):
            def slot(kind, s, h, b):
                u, ub = s + 1, 1 - b
                for step in which[kind]:
                    op = step[0]
                    if op in ("qh", "kh"):
                        o, f, t, hi, lo = ("q", qf, qt, qH[ub], qL_[ub]) if op == "qh" else ("k", kf, kt, kH[1][ub], kL[1][ub])
                        pool.wait_ge(S(f"{o}terms"), 4 * (u + 1))
                        for c in range(2):
                            k, n = ring.at(kind, s, (o, c))
                            pool.wait_ge(free[k], n + 1)
                        pool.tensor_tensor(f[0:ROPE, :], f[0:ROPE, :], t[:], ALU.add).then_inc(S(f"{o}rot"), 1)
                        pool.wait_ge(S("qH_done" if op == "qh" else "kHw_done"), 2 * (u + 1))
                        pool.tensor_tensor(lo[:], f[:], hi[0:QK, :].bitcast(F32), ALU.subtract).then_inc(
                            S("qL_done" if op == "qh" else "kLw_done"), 1)
                    elif op == "B" and step[1] < TB:
                        i = step[1]
                        for a in range(2):
                            n = TB * s + i if a else (TB + 1) * s + i + (i >= 2)
                            wait_apart(pool, S, S(f"st{a}_read"), n + 1)
                            d = pr[a][i % 2][:, P * i:P * (i + 1)]
                            pool.affine_select(out=d, in_=d, pattern=[[1, P]], compare_op=ALU.is_ge, fill=0.0, base=0,
                                               channel_multiplier=-1).then_inc(S(f"probs{a}"), 1)
                    elif op == "a2o":
                        wait_apart(pool, S, S("wp_loaded"), 48 * (h + 1))
                        pool.tensor_scalar(wpg[b][:], wp[:], K["gcol"][:, b:b + 1], None, ALU.mult).then_inc(S("wpg_done"), 1)

            run_slots(pool, slot)

        @block.vector
        def _(dve):
            def slot(kind, s, h, b):
                u, ub = s + 1, 1 - b

                def filled(item):
                    k, n = ring.at(kind, s, item)
                    dve.wait_ge(full[k], n + 1)
                    return k

                for step in which[kind]:
                    op = step[0]
                    if op in ("q", "k"):
                        f, t = (qf, qt) if op == "q" else (kf, kt)
                        wait_past(dve, S("qL_done" if op == "q" else "kLw_done"), u)
                        for c in range(2):
                            k = filled((op, c))
                            cols = slice(BANK * c, BANK * (c + 1))
                            dve.tensor_tensor(f[0:ROPE, cols], bank(k)[0:ROPE, :], cosT[:, cols], ALU.mult).then_inc(S(f"{op}terms"), 1)
                            dve.tensor_tensor(t[0:HALF, cols], bank(k)[HALF:ROPE, :], sinT[HALF:ROPE, cols], ALU.mult).then_inc(S(f"{op}terms"), 1)
                            dve.wait_ge(S(f"{op}plain"), 2 * u + c + 1)
                            dve.tensor_tensor(t[HALF:ROPE, cols], bank(k)[0:HALF, :], sinT[0:HALF, cols], ALU.mult).then_inc(free[k], 1)
                    elif op == "n":
                        for c in range(2):
                            k = filled((op, c))
                            cols = slice(BANK * c, BANK * (c + 1))
                            dve.wait_ge(S("kH1_done"), 2 * u + c + 1)
                            dve.tensor_tensor(kL[0][ub][64:96, cols], bank(k)[64:96, :], kH[0][ub][64:96, cols].bitcast(F32),
                                              ALU.subtract).then_inc(free[k], 1)
                    elif op == "k2":
                        k = filled(step)
                        kk = bank(k)[:, 0:KEEP]
                        x = S("k2_chain")
                        dve.tensor_tensor(k2f[0:ROPE, :], kk[0:ROPE, :], cosT[:, 0:KEEP], ALU.mult).then_inc(x, 1)
                        dve.tensor_tensor(k2t[0:HALF, :], kk[HALF:ROPE, :], sinT[HALF:ROPE, 0:KEEP], ALU.mult).then_inc(x, 1)
                        dve.tensor_tensor(k2t[HALF:ROPE, :], kk[0:HALF, :], sinT[0:HALF, 0:KEEP], ALU.mult).then_inc(x, 1)
                        dve.tensor_copy(k2f[64:96, :], kk[64:96, :]).then_inc(x, 1)
                        dve.tensor_copy(V2[ub][:, 0:VD], bank(k)[0:KEEP, 64:64 + VD]).then_inc(x, 1)
                        dve.wait_ge(x, 6 * u + 5)
                        dve.tensor_tensor(k2f[0:ROPE, :], k2f[0:ROPE, :], k2t[:], ALU.add).then_inc(free[k], 1)
                        dve.wait_ge(free[k], ring.at(kind, s, step)[1] + 1)
                        dve.tensor_copy(kH[2][ub][0:QK, :], k2f[:]).then_inc(x, 1)
                        dve.wait_ge(x, 6 * u + 6)
                        dve.tensor_tensor(kL[2][ub][:], k2f[:], kH[2][ub][0:QK, :].bitcast(F32), ALU.subtract).then_inc(S("k2_done"), 1)
                    elif op == "mx":
                        _, a, j, c = step
                        k = filled(step)
                        hi = min(P * (j + 1), BANK * (c + 1))
                        w = hi - BANK * c
                        dst = mneg[:, a, j:j + 1] if c == 0 else mpart[:, a, j - 4:j - 3]
                        dve.tensor_reduce(dst, bank(k)[:, 0:w], AX.X, ALU.max, negate=True).then_inc(free[k], 1)
                    elif op == "mx2":
                        k = filled(step)
                        dve.tensor_reduce(mneg[:, 2, :], bank(k)[:, 0:KEEP * TB].rearrange("p (j n) -> p j n", n=KEEP),
                                          AX.X, ALU.max, negate=True).then_inc(free[k], 1)
                    elif op == "mt":
                        for item in (("mx", 1, 7, 0), ("mx", 1, 7, 1), ("mx2",)):
                            k, n = ring.at(kind, s, item)
                            dve.wait_ge(free[k], n + 1)
                        dve.tensor_tensor(mneg[:, 0:2, 4:8], mneg[:, 0:2, 4:8], mpart[:], ALU.min).then_inc(S("mneg"), 1)
                    elif op == "a2o":
                        for c in range(2):
                            k = filled((op, c))
                            cols = slice(BANK * c, BANK * (c + 1))
                            dve.wait_ge(S("rD2"), 2 * s + c + 1)
                            dve.tensor_tensor(tO[b][64:96, cols], bank(k)[64:96, :], rD[64:96, cols], ALU.mult).then_inc(free[k], 1)
                    elif op == "norm":
                        dve.wait_ge(S("rD01"), s + 1)
                        dve.tensor_tensor(tO[b][0:64, :], out_ps[0:64, :], rD[0:64, :], ALU.mult).then_inc(S("out_read"), 1)
                    elif op == "wp":
                        for c in range(2):
                            k = filled((op, c))
                            rows = res[:, TB * b + 4 * c:TB * b + 4 * (c + 1), :].rearrange("p t c -> p (t c)")
                            dve.tensor_tensor(rows, bank(k), rows, ALU.add).then_inc(free[k], 1)

            for b in range(B):
                dve.memset(V2[b][:, VD:], 1.0).then_inc(S("v2_ones"), 1)
            run_slots(dve, slot)


def bank_uses(steps_of_kind, uses):
    table, totals = {}, {}
    for kind, steps in steps_of_kind.items():
        count = {}
        for s in steps:
            for n, k in enumerate(uses.get(s, ())):
                table[kind, s, n] = (k, count.get(k, 0))
                count[k] = count.get(k, 0) + 1
        totals[kind] = count

    def at(kind, slot, step, nth=0):
        k, i = table[kind, step, nth]
        return k, (i if kind == "first" else totals["first"].get(k, 0) + totals["loop"].get(k, 0) * slot + i)

    return at


def ffn_begin(nc, ins, F, ps, S, before):
    with ExitStack() as ctx:
        def sb(name, shape, dt=F32):
            return ctx.enter_context(nc.sbuf_tensor(name, shape, dt))

        raw = sb("raw_tables", [P, 4, TB, FD])
        gains = sb("gains", [P, DEPTH, 4, FD])
        stats = sb("f_stats", [P, NT, 6])
        mv = sb("f_mv", [P, NT, 2])
        va = sb("f_va", [P, NT])
        sd = sb("f_sd", [P, NT])
        rs = sb("f_rs", [P, NT])
        res, xf, tabs = F["res"], F["xf"], F["tabs"]
        loads = [(raw[:, n], ins[name].rearrange("(t p) d -> p t d", p=P))
                 for n, name in enumerate(("c_qcos", "c_qsin", "c_kcos", "c_ksin"))]
        for l in range(DEPTH):
            for n, name in ((0, "L0_ffn_q_scale"), (2, "L0_ffn_k_scale")):
                row = ins[name][l:l + 1, :]
                loads.append((gains[:, l, n, :], row.to_broadcast([P, FD])))
                loads.append((gains[:, l, n + 1, 0:HALF], row[:, HALF:FD].to_broadcast([P, HALF])))
                loads.append((gains[:, l, n + 1, HALF:FD], row[:, 0:HALF].to_broadcast([P, HALF])))
        others = [(F["shift"][:], ins["c_shift"]), (F["edge"][:], ins["c_edge"]), (F["masks"][:], ins["c_masks"]),
                  (F["flags"][:], ins["c_flags"]),
                  (F["wqkv"][:], ins["L0_ffn_wqkv"].rearrange("l c n -> c l n")),
                  (F["wo"][:], ins["L0_ffn_wo"].rearrange("l (m p) c -> p l m c", p=P)),
                  (F["w1"][:], ins["L0_ffn_w1"].rearrange("l c n -> c l n")),
                  ]
        for l in range(DEPTH):
            others.append((F["lg"][:, l:l + 1], ins["L0_ffn_ln_g"][l].rearrange("(p a) -> p a", a=1)))
            others.append((F["lb"][:, l:l + 1], ins["L0_ffn_ln_b"][l].rearrange("(p a) -> p a", a=1)))
            others.append((F["b2"][:, l, :], ins["L0_ffn_b2"][l:l + 1, :].to_broadcast([P, C])))
            for c, (o, w) in enumerate(HCH):
                others.append((F["w2"][0:w, l, c, :], ins["L0_ffn_w2"][l, o:o + w, :]))
                for half in range(2):
                    others.append((F["b1"][0:w, l, 3 * half + c:3 * half + c + 1],
                                   ins["L0_ffn_b1"][l, HID * half + o:HID * half + o + w].rearrange("(p a) -> p a", a=1)))
        block = ctx.enter_context(nc.Block())

        @block.sync
        def _(sp):
            before.clear(sp)
            for dst, src in loads:
                sp.dma_start(dst, src).then_inc(S("tables_loaded"), 16)
            for dst, src in others:
                sp.dma_start(dst, src).then_inc(S("weights_loaded"), 16)
            sp.wait_ge(S("weights_loaded"), 16 * len(others))

        @block.gpsimd
        def _(pool):
            pool.memset(F["ln256"][:], float(np.log(256.0))).then_inc(S("zeroed"), 1)
            pool.memset(F["kT"][3][:], 0.0).then_inc(S("zeroed"), 1)
            pool.memset(F["vN"][3][:], 0.0).then_inc(S("zeroed"), 1)
            pool.memset(F["sm"][:], 0.0).then_inc(S("zeroed"), 1)
            pool.memset(xf[:, 0, :], 0.0).then_inc(S("zeroed"), 1)
            pool.wait_ge(S("tables_loaded"), 16 * len(loads))
            for l in (1,):
                for n in range(4):
                    for b in range(B):
                        pool.tensor_tensor(tabs[:, l, n, TB * b:TB * (b + 1), :], raw[:, n],
                                           gains[:, l, n:n + 1, :].to_broadcast([P, TB, FD]), ALU.mult).then_inc(S("tabs"), 1)

        @block.scalar
        def _(act):
            act.wait_ge(S("f_var"), 1)
            act.activation(sd[:], va[:], ACT.Sqrt).then_inc(S("f_std"), 1)

        @block.vector
        def _(dve):
            for t in range(NT):
                dve.bn_stats(stats[:, t, :], res[:, t, :]).then_inc(S("f_stats"), 1)
            for t in range(NT):
                dve.wait_ge(S("f_stats"), t + 1)
                dve.bn_aggr(mv[:, t, :], stats[:, t, :]).then_inc(S("f_aggr"), 1)
            dve.wait_ge(S("f_aggr"), NT)
            dve.tensor_scalar(va[:], mv[:, :, 1], 1e-5, None, ALU.add).then_inc(S("f_var"), 1)
            dve.wait_ge(S("f_std"), 1)
            dve.reciprocal(rs[:], sd[:]).then_inc(S("f_rstd"), 1)
            dve.wait_ge(S("f_rstd"), 1)
            for t in range(NT):
                dve.tensor_scalar(xf[:, t + 1, :], res[:, t, :], mv[:, t, 0:1], rs[:, t:t + 1],
                                  ALU.subtract, ALU.mult).then_inc(S("xf"), 1)
            dve.wait_ge(S("tables_loaded"), 16 * len(loads))
            for n in range(4):
                for b in range(B):
                    dve.tensor_tensor(tabs[:, 0, n, TB * b:TB * (b + 1), :], raw[:, n],
                                      gains[:, 0, n:n + 1, :].to_broadcast([P, TB, FD]), ALU.mult).then_inc(S("tabs"), 1)


def window_attention(nc, F, ps, l, S):
    steps = ["ax", "ah", "bs0", "aq", "bs1", "as", "bt0", "bt1", "an", "bt2", "bt3", "bo", "at", "bw", "bx"]
    kinds = {"first": [s for s in steps if s[0] == "a"], "loop": steps, "last": [s for s in steps if s[0] == "b"]}
    at = bank_uses(kinds, {"ah": (0,), "bw": (0,), "bx": (0,), "aq": (1, 2, 3), "at": (1, 2), "bt0": (6, 3),
                           "bs0": (4, 5), "bs1": (4, 5), "bt1": (7,), "bt2": (6,), "bt3": (7,)})
    with ExitStack() as ctx:
        def sb(name, shape, dt=F32):
            return ctx.enter_context(nc.sbuf_tensor(f"{name}_l{l}", shape, dt))

        xa = sb("xa", [P, C])
        xb = sb("xb", [P, FD])
        hT = sb("hT", [P, P])
        sq = sb("sq", [P, 2, INNER])
        ss = sb("ss", [P, 2 * FH])
        sl = sb("sl", [P, 2 * FH])
        rn = sb("rn", [P, 2 * FH])
        qk = [sb(f"qk{n}", [P, INNER]) for n in range(2)]
        qs = [sb(f"qs{n}", [P, INNER]) for n in range(2)]
        qT = [sb(f"qT{n}", [P, 4, P]) for n in range(2)]
        band = sb("band", [P, P + WIN])
        mx = sb("mx", [P, FH])
        ng = sb("ng", [P, FH])
        rs = sb("rs", [P, FH])
        rr = sb("rr", [P, FH])
        pT = [sb(f"pT{n}", [P, 4, P]) for n in range(2)]
        oN = sb("oN", [P, INNER])
        oT = sb("oT", [P, 4, P])
        xf, tabs, masks, flags, ident, shift, edge = (F[k] for k in ("xf", "tabs", "masks", "flags", "ident", "shift", "edge"))
        kT, vN, sm, wqkv, wo = F["kT"], F["vN"], F["sm"], F["wqkv"], F["wo"]
        block = ctx.enter_context(nc.Block())
        full = [S(f"bank{k}_filled") for k in range(8)]
        free = [S(f"bank{k}_read") for k in range(8)]

        def heads(ap):
            return ap.rearrange("p (h d) -> p h d", h=FH)

        def run_slots(eng, slot):
            slot("first", 0, 0)
            with eng.Fori(0, 3) as i:
                for r in range(4):
                    slot("loop", 4 * i + r + 1, (r + 1) % 4)
            for t in range(13, NT):
                slot("loop", t, t % 4)
            slot("last", NT, 0)

        def prev(kind, t, step, nth=0):
            k, n = at(kind, 0 if kind == "first" else t - 1, step, nth)
            return k, n

        @block.tensor
        def _(pe):
            def slot(kind, t, r):
                g = t - 1
                rg, rp = (r - 1) % 4, (r - 2) % 4

                def take(step, nth=0):
                    k, n = prev(kind, t, step, nth)
                    wait_past(pe, free[k], n)
                    return k

                for step in kinds[kind]:
                    if step == "ah":
                        k = take(step)
                        pe.wait_ge(S("x_copied"), 2 * (t + 1))
                        pe.matmul(ps[0:64, k, 0:P], xa[:, 0:FD], ident[:], start=True, stop=True)
                        pe.matmul(ps[64:128, k, 0:P], xa[:, FD:C], shift[:], start=True, stop=False)
                        pe.matmul(ps[64:128, k, 0:P], xb[:], edge[:], start=False, stop=True).then_inc(full[k], 1)
                    elif step == "aq":
                        k, n = prev(kind, t, "ah")
                        pe.wait_ge(free[k], n + 1)
                        for n in range(3):
                            k = take(step, n)
                            pe.matmul(ps[:, k, :], hT[:], wqkv[:, l, INNER * n:INNER * (n + 1)],
                                      start=True, stop=True).then_inc(full[k], 1)
                    elif step == "at":
                        for n in range(2):
                            k = take(step, n)
                            pe.wait_ge(S("qk_scaled"), 2 * t + n + 1)
                            for m in range(4):
                                mm = pe.transpose(ps[:, k, P * m:P * (m + 1)], qk[n][:, P * m:P * (m + 1)], ident[:])
                            mm.then_inc(full[k], 1)
                    elif step in ("bs0", "bs1"):
                        gr = int(step[2])
                        if gr == 0:
                            for n in range(2):
                                pk, pn = at("first", 0, "at", n) if isinstance(t, int) and t == 1 else at("loop", t - 2, "at", n)
                                pe.wait_ge(free[pk], pn + 1)
                        for o in range(2):
                            k = take(step, o)
                            rows = slice(FD * o, FD * (o + 1))
                            for e in range(2):
                                hp = 2 * gr + e
                                q = qT[rg % 2][rows, hp, :]
                                pe.matmul(ps[:, k, 192 * e:192 * e + 64], q, kT[rp][rows, hp, 64:128], start=True, stop=True)
                                mm = pe.matmul(ps[:, k, 192 * e + 64:192 * e + 192], q, kT[rg][rows, hp, :], start=True, stop=True)
                            mm.then_inc(full[k], 1)
                    elif step[0:2] == "bt":
                        m = int(step[2])
                        k = take(step)
                        pe.wait_ge(S("probs"), FH * g + 2 * m + 2)
                        for j in range(4):
                            mm = pe.transpose(ps[:, k, P * j:P * (j + 1)], sm[:, 2 * m + j // 2, P * (j % 2):P * (j % 2 + 1)], ident[:])
                        mm.then_inc(full[k], 1)
                        if m:
                            weighted(kind, t, m - 1, rg, rp)
                    elif step == "bo":
                        weighted(kind, t, 3, rg, rp)
                    elif step == "bw":
                        k = take(step)
                        pe.wait_ge(S("oN"), g + 1)
                        for m in range(4):
                            mm = pe.transpose(ps[:, k, P * m:P * (m + 1)], oN[:, P * m:P * (m + 1)], ident[:])
                        mm.then_inc(full[k], 1)
                    elif step == "bx":
                        k = take(step)
                        for m in range(4):
                            mm = pe.matmul(ps[:, k, 0:P], oT[:, m, :], wo[:, l, m, :], start=(m == 0), stop=(m == 3))
                        mm.then_inc(full[k], 1)

            def weighted(kind, t, m, rg, rp):
                k6, n6 = prev(kind, t, f"bt{m}")
                pe.wait_ge(free[k6], n6 + 1)
                k, n = prev(kind, t, "bt0", 1)
                if m == 0:
                    wait_past(pe, free[k], n)
                for j in range(2):
                    hh = 2 * m + j
                    cols = slice(FD * hh, FD * (hh + 1))
                    pe.matmul(ps[:, k, cols], pT[m % 2][:, 2 * j + 1, :], vN[rg][:, cols], start=True, stop=False)
                    mm = pe.matmul(ps[:, k, cols], pT[m % 2][64:128, 2 * j, :], vN[rp][64:128, cols], start=False, stop=True)
                mm.then_inc(S("weighted") if m < 3 else full[k], 1)

            run_slots(pe, slot)

        @block.scalar
        def _(act):
            def slot(kind, t, r):
                g = t - 1

                def filled(step, nth=0):
                    k, n = prev(kind, t, step, nth)
                    act.wait_ge(full[k], n + 1)
                    return k

                for step in kinds[kind]:
                    if step == "ah":
                        k = filled(step)
                        act.activation(hT[:], ps[:, k, 0:P], ACT.Copy).then_inc(free[k], 1)
                    elif step == "aq":
                        wait_past(act, S("sums"), t)
                        for n in range(2):
                            k = filled(step, n)
                            act.activation(sq[:, n, :], ps[:, k, :], ACT.Square).then_inc(S("squares"), 1)
                        k = filled(step, 2)
                        act.activation(vN[r][:], ps[:, k, :], ACT.Copy).then_inc(free[k], 1)
                    elif step == "as":
                        act.wait_ge(S("clipped"), t + 1)
                        act.activation(sl[:], ss[:], ACT.Ln, scale=65536.0).then_inc(S("ln_norm"), 1)
                        act.wait_ge(S("ln_norm"), t + 1)
                        act.activation(rn[:], sl[:], ACT.Exp, scale=-0.5, bias=F["ln256"][:, 0:1]).then_inc(S("rn"), 1)
                    elif step == "at":
                        for n, dst in enumerate((qT[r % 2], kT[r])):
                            k = filled(step, n)
                            act.activation(dst[:].rearrange("p a n -> p (a n)"), ps[:, k, :], ACT.Copy).then_inc(free[k], 1)
                    elif step in ("bs0", "bs1"):
                        gr = int(step[2])
                        act.wait_ge(S("neg_max"), 2 * g + gr + 1)
                        for hh in range(4 * gr, 4 * gr + 4):
                            act.activation(sm[:, hh, 64:256], sm[:, hh, 64:256], ACT.Exp, bias=ng[:, hh:hh + 1],
                                           accum_out=rs[:, hh:hh + 1]).then_inc(S("probs"), 1)
                    elif step in ("bt1", "bt3"):
                        k = filled(step)
                        act.activation(pT[1][:].rearrange("p a n -> p (a n)"), ps[:, k, :], ACT.Copy).then_inc(free[k], 1)
                    elif step == "bw":
                        k = filled(step)
                        act.activation(oT[:].rearrange("p a n -> p (a n)"), ps[:, k, :], ACT.Copy).then_inc(free[k], 1)

            run_slots(act, slot)

        @block.gpsimd
        def _(pool):
            def slot(kind, t, r):
                for step in kinds[kind]:
                    if step == "as":
                        for n in range(2):
                            pool.wait_ge(S("cos_terms"), 2 * t + n + 1)
                            k, m = prev(kind, t, "aq", n)
                            pool.wait_ge(free[k], m + 1)
                            pool.tensor_tensor(qk[n][:], qk[n][:], qs[n][:], ALU.add).then_inc(S("rotated"), 1)

            run_slots(pool, slot)

        @block.vector
        def _(dve):
            def slot(kind, t, r):
                g = t - 1

                def filled(step, nth=0):
                    k, n = prev(kind, t, step, nth)
                    dve.wait_ge(full[k], n + 1)
                    return k

                for step in kinds[kind]:
                    if step == "ax":
                        dve.tensor_copy(xa[:], xf[:, t + 1, :]).then_inc(S("x_copied"), 1)
                        dve.tensor_scalar(xb[:], xf[:, t, FD:C], flags[:, bass.ds(t, 1)], None, ALU.mult).then_inc(S("x_copied"), 1)
                    elif step == "as":
                        dve.wait_ge(S("squares"), 2 * (t + 1))
                        dve.tensor_reduce(ss[:], sq[:].rearrange("p a (h d) -> p (a h) d", h=FH), AX.X, ALU.add).then_inc(S("sums"), 1)
                        dve.wait_ge(S("sums"), t + 1)
                        dve.tensor_scalar(ss[:], ss[:], 1e-24, None, ALU.max).then_inc(S("clipped"), 1)
                        for n in range(2):
                            k = filled("aq", n)
                            dve.tensor_tensor(heads(qk[n][:]), heads(ps[:, k, :]),
                                              tabs[:, l, 2 * n, bass.ds(t, 1), :].to_broadcast([P, FH, FD]), ALU.mult).then_inc(S("cos_terms"), 1)
                            for o in range(2):
                                src = heads(ps[:, k, :])[:, :, HALF * (1 - o):HALF * (2 - o)]
                                dst = heads(qs[n][:])[:, :, HALF * o:HALF * (o + 1)]
                                tab = tabs[:, l, 2 * n + 1, bass.ds(t, 1), HALF * o:HALF * (o + 1)].to_broadcast([P, FH, HALF])
                                ins_ = dve.tensor_tensor(dst, src, tab, ALU.mult)
                                ins_.then_inc(free[k] if o else S("sin_terms"), 1)
                    elif step == "an":
                        dve.wait_ge(S("rn"), t + 1)
                        for n in range(2):
                            dve.wait_ge(S("rotated"), 2 * t + n + 1)
                            dve.tensor_tensor(heads(qk[n][:]), heads(qk[n][:]),
                                              rn[:, FH * n:FH * (n + 1)].unsqueeze(2).to_broadcast([P, FH, FD]),
                                              ALU.mult).then_inc(S("qk_scaled"), 1)
                    elif step in ("bs0", "bs1"):
                        gr = int(step[2])
                        if gr == 0:
                            wait_past(dve, S("weighted"), 3 * g)
                        k4, k5 = filled(step, 0), filled(step, 1)
                        dve.sem_inc(S("passed_DVE"), 1)
                        dve.tensor_copy(band[:], masks[:, g, :]).then_inc(S("band"), 1)
                        dve.wait_ge(S("band"), 2 * g + gr + 1)
                        dve.sem_inc(S("passed_DVE"), 1)
                        for o, k in enumerate((k4, k5)):
                            for e in range(2):
                                hh = 4 * gr + 2 * e + o
                                dve.tensor_tensor_reduce(sm[:, hh, 64:256], ps[:, k, 192 * e:192 * e + 192], band[:], 1.0,
                                                         -3.0e38, ALU.add, ALU.max, mx[:, hh:hh + 1]).then_inc(free[k] if e else S("maxed"), 1)
                        dve.wait_ge(S("maxed"), 4 * g + 2 * gr + 2)
                        for o in range(2):
                            k, n = prev(kind, t, step, o)
                            dve.wait_ge(free[k], n + 1)
                        dve.tensor_scalar(ng[:, 4 * gr:4 * gr + 4], mx[:, 4 * gr:4 * gr + 4], -1.0, None, ALU.mult).then_inc(S("neg_max"), 1)
                    elif step in ("bt0", "bt2"):
                        k = filled(step)
                        dve.tensor_copy(pT[0][:].rearrange("p a n -> p (a n)"), ps[:, k, :]).then_inc(free[k], 1)
                    elif step == "bo":
                        dve.wait_ge(S("probs"), FH * (g + 1))
                        dve.reciprocal(rr[:], rs[:]).then_inc(S("rr"), 1)
                        dve.wait_ge(S("rr"), g + 1)
                        k = filled("bt0", 1)
                        dve.tensor_tensor(heads(oN[:]), heads(ps[:, k, :]), rr[:].unsqueeze(2).to_broadcast([P, FH, FD]),
                                          ALU.mult).then_inc(S("oN"), 1)
                        dve.wait_ge(S("oN"), g + 1)
                        dve.sem_inc(free[k], 1)
                    elif step == "bx":
                        k = filled(step)
                        dve.tensor_tensor(xf[:, t, :], ps[:, k, 0:P], xf[:, t, :], ALU.add).then_inc(free[k], 1)

            run_slots(dve, slot)


def gated_mlp(nc, F, ps, l, S, out_ap=None):
    NC4, W = NT // 4, BANK
    with ExitStack() as ctx:
        def sb(name, shape, dt=F32):
            return ctx.enter_context(nc.sbuf_tensor(f"{name}_m{l}", shape, dt))

        xp = sb("xp", [P, NT, FD])
        hn = sb("hn", [P, NT, C])
        stats = sb("stats", [P, NT, 6])
        mv = sb("mv", [P, NT, 2])
        va = sb("va", [P, NT])
        sd = sb("sd", [P, NT])
        rs = sb("rs", [P, NT])
        hT = sb("hTm", [P, NT * P])
        gg = sb("gg", [P, 3, W])
        hid = sb("hid", [P, 3, W])
        xf, res, flags, ident, shift, edge = (F[k] for k in ("xf", "res", "flags", "ident", "shift", "edge"))
        w1, w2, b1, b2, lg, lb = (F[k] for k in ("w1", "w2", "b1", "b2", "lg", "lb"))
        block = ctx.enter_context(nc.Block())
        last = l == DEPTH - 1

        @block.vector
        def _(dve):
            for m in range(NC4):
                s = slice(4 * m, 4 * m + 4)
                dve.tensor_tensor(xp[:, s, :], xf[:, s, FD:C], flags[:, s].unsqueeze(2).to_broadcast([P, 4, FD]),
                                  ALU.mult).then_inc(S("xp"), 1)
            for m in range(NC4):
                s = slice(4 * m, 4 * m + 4)
                dve.tensor_copy(hn[:, s, 0:FD], xf[:, 4 * m + 1:4 * m + 5, 0:FD]).then_inc(S("lower"), 1)
                dve.wait_ge(S("shifted"), m + 1)
                dve.tensor_copy(hn[:, s, FD:C], ps[:, m, 0:4 * FD].rearrange("p (t d) -> p t d", t=4)).then_inc(S("upper"), 1)
            dve.wait_ge(S("lower"), NC4)
            for t in range(NT):
                dve.wait_ge(S("upper"), t // 4 + 1)
                dve.bn_stats(stats[:, t, :], hn[:, t, :]).then_inc(S("stats"), 1)
            for t in range(NT):
                dve.wait_ge(S("stats"), t + 1)
                dve.bn_aggr(mv[:, t, :], stats[:, t, :]).then_inc(S("aggr"), 1)
            dve.wait_ge(S("aggr"), NT)
            dve.tensor_scalar(va[:], mv[:, :, 1], 1e-5, None, ALU.add).then_inc(S("var"), 1)
            dve.wait_ge(S("std"), 1)
            dve.reciprocal(rs[:], sd[:]).then_inc(S("rstd"), 1)
            dve.wait_ge(S("rstd"), 1)
            for t in range(NT):
                dve.tensor_scalar(hn[:, t, :], hn[:, t, :], mv[:, t, 0:1], rs[:, t:t + 1], ALU.subtract, ALU.mult).then_inc(S("normed"), 1)
            for m in range(NC4):
                s = slice(4 * m + 1, 4 * m + 5)
                dve.tensor_tensor(xf[:, s, :], xf[:, s, :], b2[:, l:l + 1, :].to_broadcast([P, 4, C]), ALU.add).then_inc(S("biased"), 1)
            if last:
                for m in range(NC4):
                    s = slice(4 * m + 1, 4 * m + 5)
                    dve.wait_ge(S("biased"), m + 1)
                    dve.tensor_tensor(xf[:, s, :], xf[:, s, :], res[:, 4 * m:4 * m + 4, :], ALU.add).then_inc(S("biased"), 1)
            dve.wait_ge(S("biased"), NC4 * (1 + last))
            with dve.Fori(0, NC4) as m:
                dve.wait_ge(S("out_done"), m)
                for c, (o, w) in enumerate(HCH):
                    dve.wait_ge(S("a_filled"), 3 * m + c + 1)
                    dve.wait_ge(S("gelu"), 3 * m + c + 1)
                    dve.scalar_tensor_tensor(out=hid[0:w, c, :], in0=ps[0:w, 3 + c, :], scalar=b1[0:w, l, c:c + 1],
                                             in1=gg[0:w, c, :], op0=ALU.add, op1=ALU.mult).then_inc(S("hidden"), 1)
                dve.wait_ge(S("out_filled"), m + 1)
                rows = xf[:, bass.ds(4 * m + 1, 4), :]
                dve.tensor_tensor(rows, ps[:, 7, :].rearrange("p (t c) -> p t c", t=4), rows, ALU.add).then_inc(S("out_done"), 1)

        @block.scalar
        def _(act):
            act.wait_ge(S("var"), 1)
            act.activation(sd[:], va[:], ACT.Sqrt).then_inc(S("std"), 1)

            for g in range(NC4):
                act.wait_ge(S("turned"), g + 1)
                act.activation(hT[:, W * g:W * (g + 1)], ps[:, g, :], ACT.Identity, scale=lg[:, l:l + 1],
                               bias=lb[:, l:l + 1]).then_inc(S("hT"), 1)
            with act.Fori(0, NC4) as m:
                act.wait_ge(S("hidden"), 3 * m)
                for c, (o, w) in enumerate(HCH):
                    act.wait_ge(S("g_filled"), 3 * m + c + 1)
                    act.activation(gg[0:w, c, :], ps[0:w, c, :], ACT.Gelu, bias=b1[0:w, l, 3 + c:4 + c]).then_inc(S("gelu"), 1)

        @block.tensor
        def _(pe):
            for m in range(NC4):
                pe.wait_ge(S("xp"), m + 1)
                o = ps[:, m, 0:4 * FD].rearrange("p (t d) -> p t d", t=4)
                pe.matmul(o, shift[:], xf[:, 4 * m + 1:4 * m + 5, FD:C], start=True, stop=False)
                pe.matmul(o, edge[:], xp[:, 4 * m:4 * m + 4, :], start=False, stop=True).then_inc(S("shifted"), 1)
            pe.wait_ge(S("upper"), NC4)
            for t in range(NT):
                pe.wait_ge(S("normed"), t + 1)
                mm = pe.transpose(ps[:, t // 4, P * (t % 4):P * (t % 4 + 1)], hn[:, t, :], ident[:])
                if t % 4 == 3:
                    mm.then_inc(S("turned"), 1)
            pe.wait_ge(S("hT"), NC4)
            with pe.Fori(0, NC4) as m:
                h = hT[:, bass.ds(W * m, W)]
                pe.wait_ge(S("gelu"), 3 * m)
                for c, (o, w) in enumerate(HCH):
                    pe.matmul(ps[0:w, c, :], w1[:, l, HID + o:HID + o + w], h, start=True, stop=True).then_inc(S("g_filled"), 1)
                pe.wait_ge(S("hidden"), 3 * m)
                for c, (o, w) in enumerate(HCH):
                    pe.matmul(ps[0:w, 3 + c, :], w1[:, l, o:o + w], h, start=True, stop=True).then_inc(S("a_filled"), 1)
                pe.wait_ge(S("out_done"), m)
                pe.wait_ge(S("hidden"), 3 * m + 3)
                for t in range(4):
                    for c, (o, w) in enumerate(HCH):
                        mm = pe.matmul(ps[:, 7, P * t:P * (t + 1)], hid[0:w, c, P * t:P * (t + 1)], w2[0:w, l, c, :],
                                       start=(c == 0), stop=(c == 2))
                mm.then_inc(S("out_filled"), 1)

        if last:
            @block.sync
            def _(sp):
                o_v = out_ap.rearrange("b (t p) c -> p (b t) c", p=P)
                for m in range(NC4):
                    sp.wait_ge(S("out_done"), m + 1)
                    sp.dma_start(o_v[:, 4 * m:4 * m + 4, :], xf[:, 4 * m + 1:4 * m + 5, :]).then_inc(S("stored"), 16)
                sp.wait_ge(S("stored"), 16 * NC4)


def build(nc, ins, out):
    with ExitStack() as ctx:
        def sb(name, shape, dt=F32):
            return ctx.enter_context(nc.sbuf_tensor(name, shape, dt))

        ps = ctx.enter_context(nc.psum_tensor("ps", [P, 8, BANK], F32))
        res = sb("res", [P, NT, C])
        ident = sb("ident", [P, P])
        SA = Sems(nc, ctx, "att_")
        with ExitStack() as actx:
            def sba(name, shape, dt=F32):
                return actx.enter_context(nc.sbuf_tensor(name, shape, dt))
            K = dict(res=res, ident=ident, identb=sba("identb", [P, P], BF16), maskb=sba("maskb", [P, P], BF16),
                     maskf=sba("maskf", [P, P]), cosT=sba("cosT", [ROPE, T]), sinT=sba("sinT", [ROPE, T]),
                     yT=sba("yT", [P, B * T]), nqT=sba("nqT", [QL, B * T]), kcT=sba("kcT", [96, B * T]),
                     ones=sba("ones", [P, VD]), selT=sba("selT", [P, B * KEEP]), gcol=sba("gcol", [96, B]),
                     kH1=[sba(f"kH1{b}", [99, T], F32R) for b in range(B)],
                     kL1=[sba(f"kL1{b}", [QK, T], F32R) for b in range(B)],
                     kHw=[sba(f"kHw{b}", [99, T], F32R) for b in range(B)],
                     kH2=[sba(f"kH2{b}", [99, KEEP], F32R) for b in range(B)])
            with ExitStack() as pctx:
                SP_ = Sems(nc, pctx, "prep_")
                prepare(nc, ins, K, ps, SP_)
                latent_attention(nc, ins, K, ps, SA, SP_)
        with ExitStack() as fctx:
            def sbf(name, shape, dt=F32):
                return fctx.enter_context(nc.sbuf_tensor(name, shape, dt))
            F = dict(res=res, ident=ident, xf=sbf("xf", [P, NT + 1, C]), shift=sbf("shift", [P, P]), edge=sbf("edge", [P, P]),
                     masks=sbf("masks", [P, NT, P + WIN]), flags=sbf("flags", [P, NT]), ln256=sbf("ln256", [P, 1]),
                     tabs=sbf("tabs", [P, DEPTH, 4, NT, FD]), wqkv=sbf("wqkv", [P, DEPTH, 3 * INNER]),
                     wo=sbf("wo", [P, DEPTH, 4, C]), w1=sbf("w1", [P, DEPTH, 2 * HID]), w2=sbf("w2", [HCH[0][1], DEPTH, 3, C]),
                     b1=sbf("b1", [HCH[0][1], DEPTH, 6]), b2=sbf("b2", [P, DEPTH, C]), lg=sbf("lg", [P, DEPTH]),
                     lb=sbf("lb", [P, DEPTH]), sm=sbf("sm", [P, FH, 2 * P]),
                     kT=[sbf(f"kT{n}", [P, 4, P]) for n in range(4)], vN=[sbf(f"vN{n}", [P, INNER]) for n in range(4)])
            with ExitStack() as bctx:
                ffn_begin(nc, ins, F, ps, Sems(nc, bctx, "start_"), SA)
            SW, SM = Sems(nc, fctx, "win_"), Sems(nc, fctx, "mlp_")
            for l in range(DEPTH):
                window_attention(nc, F, ps, l, SW)
                gated_mlp(nc, F, ps, l, SM, out)
                if l < DEPTH - 1:
                    with nc.Block() as between:
                        @between.sync
                        def _(sp):
                            SW.clear(sp)
                            SM.clear(sp)


def _constants():
    f32 = np.float32
    f = (f32(1.0) / f32(10000.0) ** (np.arange(0, ROPE, 2, dtype=f32) / f32(ROPE))).astype(f32)
    a = np.outer(np.arange(T, dtype=f32), f).astype(f32)
    cos, sin = np.cos(a).astype(f32), np.sin(a).astype(f32)
    i, j = np.arange(P)[:, None], np.arange(P)[None, :]
    out = {
        "c_ident": np.eye(P, dtype=f32),
        "c_causal": np.where(j > i, f32(NEG), f32(0.0)).astype(f32),
        "c_cosT": np.ascontiguousarray(np.concatenate([cos, cos], 1).T),
        "c_sinT": np.ascontiguousarray(np.concatenate([sin, -sin], 1).T),
        "c_cosN": cos, "c_sinN": sin,
        "c_iota": np.tile(np.arange(KEEP, dtype=f32), (P, 1)),
    }
    half = np.arange(0, FD, 2, dtype=f32)
    inv = (f32(1.0) / f32(10000.0) ** (half / f32(FD))).astype(f32)
    ang = (np.arange(T, dtype=f32)[:, None] * inv[None, :]).astype(f32)
    base = ((half + f32(0.4 * FD)) / f32(1.4 * FD)).astype(f32)
    power = ((np.arange(T, dtype=f32) - T // 2) / f32(WIN // 2)).astype(f32)
    scale = (base[None, :] ** power[:, None]).astype(f32)
    both = lambda a: np.concatenate([a, a], 1)
    sgn = np.concatenate([-np.ones(FD // 2, f32), np.ones(FD // 2, f32)])[None, :]
    out["c_qcos"] = both(np.cos(ang) * scale * f32(8.0)).astype(f32)
    out["c_qsin"] = (both(np.sin(ang) * scale * f32(8.0)) * sgn).astype(f32)
    out["c_kcos"] = both(np.cos(ang) / scale).astype(f32)
    out["c_ksin"] = (both(np.sin(ang) / scale) * sgn).astype(f32)
    out["c_shift"] = np.eye(P, k=1, dtype=f32)
    edge = np.zeros((P, P), f32)
    edge[P - 1, 0] = 1.0
    out["c_edge"] = edge
    q, k = np.arange(P)[:, None], np.arange(P + WIN)[None, :] - WIN
    near = (q - k >= 0) & (q - k <= WIN)
    masks = np.empty((P, NT, P + WIN), f32)
    for t in range(NT):
        masks[:, t] = np.where(near & ((k >= 0) | (t % TB != 0)), f32(0.0), f32(NEG))
    out["c_masks"] = masks
    out["c_flags"] = np.tile((np.arange(NT) % TB != 0).astype(f32), (P, 1))
    return out


_INS = ['L0_attn_x', 'L0_attn_w_cq', 'L0_attn_g_qnorm', 'L0_attn_w_dq_nope', 'L0_attn_w_dq_rope', 'L0_attn_w_ckv',
        'L0_attn_g_kvnorm', 'L0_attn_w_dk_nope', 'L0_attn_w_dv', 'L0_attn_w_krope', 'L0_attn_w_imp', 'L0_attn_w_selk',
        'L0_attn_w_selv', 'L0_attn_w_wink', 'L0_attn_w_winv', 'L0_attn_w_gate', 'L0_attn_w_proj', 'L0_ffn_wqkv',
        'L0_ffn_q_scale', 'L0_ffn_k_scale', 'L0_ffn_wo', 'L0_ffn_ln_g', 'L0_ffn_ln_b', 'L0_ffn_w1', 'L0_ffn_b1',
        'L0_ffn_w2', 'L0_ffn_b2']


def kernel(**inputs):
    import concourse.bacc as _bacc
    from concourse.bass_utils import run_bass_kernel_spmd as _run

    nc = _bacc.Bacc("TRN2", target_bir_lowering=False, num_devices=1)
    arrays, aps = {}, {}
    given = {n: np.ascontiguousarray(inputs[n]) for n in _INS}
    given.update(_constants())
    for name, a in given.items():
        arrays[f"in_{name}_dram"] = a
        aps[name] = nc.dram_tensor(f"in_{name}_dram", a.shape, mybir.dt.from_np(a.dtype), kind="ExternalInput").ap()
    out = nc.dram_tensor("out_0_dram", (B, T, C), F32, kind="ExternalOutput").ap()
    build(nc, aps, out)
    r = _run(nc, [arrays], core_ids=[0])
    return r.results[0]["out_0_dram"]
```

```python
from contextlib import ExitStack

import numpy as np

import concourse.bass as bass
from concourse import mybir
from concourse.alu_op_type import AluOpType as ALU

F32 = mybir.dt.float32
F32R = mybir.dt.float32r
BF16 = mybir.dt.bfloat16
ACT = mybir.ActivationFunctionType
AX = mybir.AxisListType

P = 128
B, T, C = 2, 1024, 128
NT = B * T // P
TB = T // P
H = 16
HEADS = H
NOPE, ROPE, VD = 32, 64, 32
QK = NOPE + ROPE
HALF = ROPE // 2
KEEP = 32
QL, KVL = 96, 32
NBR = 3
BANK = 512
NEG = -1.0e30

DEPTH, FH, FD, WIN = 2, 8, 64, 64
INNER = FH * FD
LOOPS = NT // 4 - 1
HID = int(C * 4 * 2 / 3)
HCH = [(0, 114), (114, 114), (228, 113)]


class Sems:

    def __init__(self, nc, ctx, stage):
        self.nc, self.ctx, self.stage, self.made = nc, ctx, stage, {}

    def __call__(self, name):
        if name not in self.made:
            self.made[name] = self.ctx.enter_context(self.nc.semaphore(self.stage + name))
        return self.made[name]

    def clear(self, eng):
        for made in self.made.values():
            eng.sem_clear(made)


def wait_past(eng, sem, value):
    if not (isinstance(value, int) and value <= 0):
        eng.wait_ge(sem, value)


def wait_apart(eng, S, sem, value):
    wait_past(eng, sem, value)
    eng.sem_inc(S(f"passed_{eng.engine.name}"), 1)


def prepare(nc, ins, K, ps, S):
    with ExitStack() as ctx:
        def sb(name, shape, dt=F32):
            return ctx.enter_context(nc.sbuf_tensor(name, shape, dt))

        stats = sb("stats", [P, NT, 6])
        mv = sb("mv", [P, NT, 2])
        rstd = sb("rstd", [P, NT])
        std = sb("std", [P, NT])
        y = sb("y", [P, NT, C])
        wc = sb("wc", [P, QL + KVL + ROPE])
        wimp = sb("wimp", [P, 1])
        wgate = sb("wgate", [P, 3])
        gq = sb("gq", [QL, 1])
        gqs = sb("gqs", [QL, 1])
        gkv = sb("gkv", [96, 1])
        gkv0 = sb("gkv0", [KVL, 1])
        wdv = sb("wdv", [KVL, H * VD])
        wpr = sb("wpr", [P, H // 4, C])
        wdvT = sb("wdvT", [P, H // 4, KVL])
        cosn = sb("cosn", [P, TB, HALF])
        sinn = sb("sinn", [P, TB, HALF])
        iota = sb("iota", [P, KEEP])
        onehot3 = sb("onehot3", [99, 3])
        z = sb("z", [P, NT, QL + KVL + ROPE])
        ssq = sb("ssq", [P, 2, NT])
        sroot = sb("sroot", [P, 2, NT])
        srec = sb("srec", [P, 2, NT])
        sqj = sb("sqj", [P, QL])
        zq = sb("zq", [P, NT, QL])
        zk = sb("zk", [P, NT, ROPE + KVL])
        ra = sb("ra", [P, TB, HALF])
        rb = sb("rb", [P, TB, HALF])
        sc = sb("sc", [33, T])
        scw = sb("scw", [33, 2, T])
        top = sb("top", [33, 4, 8])
        selm = sb("selm", [33, T])
        rank = sb("rank", [33, T])
        one1 = sb("one1", [33, 1])
        rkn = sb("rkn", [P, NT])
        hot = sb("hot", [P, NT, KEEP])
        ysum = sb("ysum", [P, B])
        gl = sb("gl", [96, B, 3])
        gm = sb("gm", [96, B])
        ge = sb("ge", [96, B, 3])
        gs = sb("gs", [96, B])
        gr = sb("gr", [96, B])

        block = ctx.enter_context(nc.Block())
        res, yT, nqT, kcT = K["res"], K["yT"], K["nqT"], K["kcT"]

        x_v = ins["L0_attn_x"].rearrange("b (t p) c -> p (b t) c", p=P)
        consts = [
            (K["ident"][:], ins["c_ident"]), (K["maskf"][:], ins["c_causal"]),
            (K["cosT"][:], ins["c_cosT"]), (K["sinT"][:], ins["c_sinT"]),
            (cosn[:], ins["c_cosN"].rearrange("(t p) d -> p t d", p=P)),
            (sinn[:], ins["c_sinN"].rearrange("(t p) d -> p t d", p=P)),
            (iota[:], ins["c_iota"]), (onehot3[96:99, :], ins["c_ident"][0:3, 0:3]),
            (wc[:, 0:QL], ins["L0_attn_w_cq"]), (wc[:, QL:QL + KVL], ins["L0_attn_w_ckv"]),
            (wc[:, QL + KVL:], ins["L0_attn_w_krope"]),
            (wimp[:], ins["L0_attn_w_imp"]), (wgate[:], ins["L0_attn_w_gate"]),
            (gq[:], ins["L0_attn_g_qnorm"].rearrange("(a o) -> a o", o=1)),
            (gkv[64:96, :], ins["L0_attn_g_kvnorm"].rearrange("(a o) -> a o", o=1)),
            (gkv0[:], ins["L0_attn_g_kvnorm"].rearrange("(a o) -> a o", o=1)),
            (wdv[:], ins["L0_attn_w_dv"]), (wpr[:], ins["L0_attn_w_proj"].rearrange("(g p) c -> p g c", p=P)),
        ]

        @block.sync
        def _(sp):
            for c in range(4):
                sp.dma_start(res[:, 4 * c:4 * c + 4, :], x_v[:, 4 * c:4 * c + 4, :]).then_inc(S(f"x_loaded{c}"), 16)
            for dst, src in consts:
                sp.dma_start(dst, src).then_inc(S("consts_loaded"), 16)

        ALLC = 16 * len(consts)

        @block.vector
        def _(dve):
            for t in range(NT):
                if t % 4 == 0:
                    dve.wait_ge(S(f"x_loaded{t // 4}"), 16)
                dve.bn_stats(stats[:, t, :], res[:, t, :]).then_inc(S("ln_stats"), 1)
            for t in range(NT):
                dve.wait_ge(S("ln_stats"), t + 1)
                dve.bn_aggr(mv[:, t, :], stats[:, t, :]).then_inc(S("ln_aggr"), 1)
            dve.wait_ge(S("ln_aggr"), NT)
            dve.tensor_scalar(rstd[:], mv[:, :, 1], 1e-5, None, ALU.add).then_inc(S("ln_var"), 1)
            dve.wait_ge(S("ln_std"), 1)
            dve.reciprocal(rstd[:], std[:]).then_inc(S("ln_rstd"), 1)
            dve.wait_ge(S("ln_rstd"), 1)
            for t in range(NT):
                dve.tensor_scalar(y[:, t, :], res[:, t, :], mv[:, t, 0:1], rstd[:, t:t + 1],
                                  ALU.subtract, ALU.mult).then_inc(S("y_ready"), 1)
            dve.wait_ge(S("consts_loaded"), ALLC)
            dve.tensor_copy(K["identb"][:], K["ident"][:]).then_inc(S("misc_const"), 1)
            dve.tensor_copy(K["maskb"][:], K["maskf"][:]).then_inc(S("misc_const"), 1)
            dve.memset(K["ones"][:], 1.0).then_inc(S("misc_const"), 1)
            dve.memset(sc[:], 0.0).then_inc(S("sc_zero"), 1)
            dve.memset(one1[:], 1.0).then_inc(S("one1"), 1)
            dve.tensor_scalar(gqs[:], gq[:], float(QK) ** -0.5, None, ALU.mult).then_inc(S("gqs"), 1)
            for t in range(NT):
                dve.wait_ge(S("lat_full"), t + 1)
                dve.tensor_copy(z[:, t, :], ps[:, 4 + t % 2, 0:QL + KVL + ROPE]).then_inc(S("lat_copied"), 1)
            for b in range(B):
                dve.wait_ge(S("yT"), 2 * b + 2)
                dve.tensor_reduce(ysum[:, b:b + 1], yT[:, T * b:T * (b + 1)], AX.X, ALU.add).then_inc(S("ysum"), 1)
            for b in range(B):
                for c in range(2):
                    i = 2 * b + c
                    dve.wait_ge(S("imp_full"), i + 1)
                    if i == 0:
                        dve.wait_ge(S("sc_zero"), 1)
                    dve.tensor_copy(sc[32 * b:32 * b + 1, BANK * c:BANK * (c + 1)],
                                    ps[32 * b:32 * b + 1, 6 + c, :]).then_inc(S("imp_copied"), 1)
            dve.wait_ge(S("squares"), 2 * NT)
            dve.tensor_scalar(sroot[:, 0, :], ssq[:, 0, :], 1.0 / QL, 1e-6, ALU.mult, ALU.add).then_inc(S("msq"), 1)
            dve.tensor_scalar(sroot[:, 1, :], ssq[:, 1, :], 1.0 / KVL, 1e-6, ALU.mult, ALU.add).then_inc(S("msq"), 1)
            dve.wait_ge(S("rms"), 1)
            dve.reciprocal(srec[:], sroot[:]).then_inc(S("rrms"), 1)
            dve.wait_ge(S("rrms"), 1)
            dve.wait_ge(S("lat_copied"), NT)
            dve.tensor_tensor(zq[:], z[:, :, 0:QL], srec[:, 0, :].unsqueeze(2).to_broadcast([P, NT, QL]),
                              ALU.mult).then_inc(S("zq"), 1)
            dve.tensor_tensor(zk[:, :, ROPE:], z[:, :, QL:QL + KVL],
                              srec[:, 1, :].unsqueeze(2).to_broadcast([P, NT, KVL]), ALU.mult).then_inc(S("zk"), 1)
            dve.tensor_tensor(K["cN"][:], z[:, :, QL:QL + KVL],
                              srec[:, 1, :].unsqueeze(2).to_broadcast([P, NT, KVL]), ALU.mult).then_inc(S("cN"), 1)
            kr = QL + KVL
            n = 0
            for b in range(B):
                tt = slice(TB * b, TB * (b + 1))
                x1, x2 = z[:, tt, kr:kr + HALF], z[:, tt, kr + HALF:kr + ROPE]
                for o, (u, v, op) in enumerate([(x1, x2, ALU.subtract), (x2, x1, ALU.add)]):
                    if n:
                        dve.wait_ge(S("kr_rot"), n)
                    dve.scalar_tensor_tensor(out=ra[:], in0=u, scalar=1.0 / H, in1=cosn[:], op0=ALU.mult, op1=ALU.mult).then_inc(S("kr_terms"), 1)
                    dve.scalar_tensor_tensor(out=rb[:], in0=v, scalar=1.0 / H, in1=sinn[:], op0=ALU.mult, op1=ALU.mult).then_inc(S("kr_terms"), 1)
                    n += 1
                    dve.wait_ge(S("kr_terms"), 2 * n)
                    dve.tensor_tensor(zk[:, tt, HALF * o:HALF * (o + 1)], ra[:], rb[:], op).then_inc(S("kr_rot"), 1)
            dve.wait_ge(S("imp_copied"), 4)
            cur = sc[:]
            for r in range(4):
                if r:
                    dve.wait_ge(S("top_round"), r)
                dve.max(top[:, r, :], cur).then_inc(S("top_found"), 1)
                dve.wait_ge(S("top_found"), r + 1)
                dve.match_replace(scw[:, r % 2, :], top[:, r, :], cur, -3.0e38).then_inc(S("top_round"), 1)
                cur = scw[:, r % 2, :]
            dve.wait_ge(S("top_round"), 4)
            dve.tensor_tensor(selm[:], cur, sc[:], ALU.not_equal).then_inc(S("selm"), 1)
            dve.wait_ge(S("selm"), 1)
            dve.wait_ge(S("misc_const"), 3)
            dve.tensor_tensor_scan(rank[:], K["ones"][0:33, 0:1].to_broadcast([33, T]), selm[:], 0.0,
                                   ALU.mult, ALU.add).then_inc(S("rank0"), 1)
            dve.wait_ge(S("rank0"), 1)
            dve.tensor_tensor(selm[:], rank[:], selm[:], ALU.mult).then_inc(S("rank1"), 1)
            dve.wait_ge(S("rank1"), 1)
            dve.tensor_scalar(rank[:], selm[:], -1.0, None, ALU.add).then_inc(S("rank2"), 1)
            dve.wait_ge(S("rankn_full"), 1)
            for b in range(B):
                tt = slice(TB * b, TB * (b + 1))
                dve.tensor_copy(rkn[:, tt], ps[:, 6 - 2 * b, tt]).then_inc(S("rankn"), 1)
            dve.wait_ge(S("rankn"), 2)
            for t in range(NT):
                dve.tensor_scalar(hot[:, t, :], iota[:], rkn[:, t:t + 1], None, ALU.is_equal).then_inc(S("hot"), 1)
            dve.wait_ge(S("sel_full"), 1)
            dve.tensor_copy(K["selT"][:], ps[:, 7, 0:B * KEEP]).then_inc(S("selT"), 1)
            dve.wait_ge(S("gate_full"), 1)
            dve.tensor_scalar(gl[:], ps[0:96, 5, 0:B * 3].rearrange("p (b g) -> p b g", b=B), 1.0 / T, None,
                              ALU.mult).then_inc(S("gl"), 1)
            dve.wait_ge(S("gl"), 1)
            dve.tensor_reduce(gm[:], gl[:], AX.X, ALU.max).then_inc(S("gm"), 1)
            dve.wait_ge(S("gm"), 1)
            dve.tensor_tensor(ge[:], gl[:], gm[:].unsqueeze(2).to_broadcast([96, B, 3]), ALU.subtract).then_inc(S("gd"), 1)
            dve.wait_ge(S("gexp"), 1)
            dve.tensor_reduce(gs[:], gl[:], AX.X, ALU.add).then_inc(S("gs"), 1)
            dve.wait_ge(S("gs"), 1)
            dve.reciprocal(gr[:], gs[:]).then_inc(S("gr"), 1)
            dve.wait_ge(S("gr"), 1)
            for n, g in enumerate((0, 2, 1)):
                rows = slice(32 * n, 32 * n + 32)
                dve.tensor_tensor(K["gcol"][rows, :], gl[rows, :, g], gr[rows, :], ALU.mult).then_inc(S("gcol"), 1)
            for i in range(4):
                b, c = i // 2, i % 2
                cols = slice(BANK * c, BANK * (c + 1))
                dve.wait_ge(S("krH"), i + 1)
                dve.tensor_tensor(K["kL1"][b][0:ROPE, cols], ps[0:ROPE, i, :], K["kH1"][b][0:ROPE, cols].bitcast(F32),
                                  ALU.subtract).then_inc(S("krL"), 1)
            for b in range(B):
                for n, k in enumerate(("kH1", "kHw", "kH2")):
                    w = KEEP if k == "kH2" else T
                    dve.tensor_copy(K[k][b][96:99, :], onehot3[96:99, n:n + 1].to_broadcast([3, w])).then_inc(S("aug"), 1)

        @block.scalar
        def _(act):
            act.wait_ge(S("ln_var"), 1)
            act.activation(std[:], rstd[:], ACT.Sqrt).then_inc(S("ln_std"), 1)
            for g in range(4):
                act.wait_ge(S("yT_full"), g + 1)
                act.activation(yT[:, BANK * g:BANK * (g + 1)], ps[:, g, :], ACT.Copy).then_inc(S("yT"), 1)
            for t in range(NT):
                act.wait_ge(S("lat_copied"), t + 1)
                for n, (o, w) in enumerate(((0, QL), (QL, KVL))):
                    if 2 * t + n:
                        act.wait_ge(S("squares"), 2 * t + n)
                    act.activation(sqj[:, 0:w], z[:, t, o:o + w], ACT.Square,
                                   accum_out=ssq[:, n, t:t + 1]).then_inc(S("squares"), 1)
            act.wait_ge(S("wdvT_full"), 1)
            act.activation(wdvT[:].rearrange("p g d -> p (g d)"), ps[:, 0, 0:H // 4 * KVL], ACT.Copy).then_inc(S("wdvT"), 1)
            for r in range(4):
                act.wait_ge(S("wvo_full"), r + 1)
                act.activation(K["wvo"][:, :, r, :], ps[0:KVL, r, :].rearrange("p (g c) -> p g c", c=C), ACT.Copy,
                               scale=gkv0[:]).then_inc(S("wvo"), 1)
            act.wait_ge(S("msq"), 2)
            act.activation(sroot[:], sroot[:], ACT.Sqrt).then_inc(S("rms"), 1)
            act.wait_ge(S("gqs"), 1)
            for g in range(4):
                act.wait_ge(S("nq_full"), g + 1)
                act.activation(nqT[:, BANK * g:BANK * (g + 1)], ps[0:QL, g, :], ACT.Copy, scale=gqs[:]).then_inc(S("nqT"), 1)
            for i in range(4):
                b, c = i // 2, i % 2
                act.wait_ge(S("kc_full"), i + 1)
                act.activation(kcT[64:96, BANK * i:BANK * (i + 1)], ps[64:96, i, :], ACT.Copy, scale=gkv[64:96, :]).then_inc(S("kcT"), 1)
                act.activation(K["kH1"][b][0:ROPE, BANK * c:BANK * (c + 1)], ps[0:ROPE, i, :], ACT.Copy).then_inc(S("krH"), 1)
            act.wait_ge(S("gd"), 1)
            act.activation(gl[:], ge[:], ACT.Exp).then_inc(S("gexp"), 1)

        @block.tensor
        def _(pe):
            ident = K["ident"]
            pe.wait_ge(S("consts_loaded"), ALLC)
            for t in range(NT):
                pe.wait_ge(S("y_ready"), t + 1)
                mm = pe.transpose(ps[:, t // 4, P * (t % 4):P * (t % 4 + 1)], y[:, t, :], ident[:])
                if t % 4 == 3:
                    mm.then_inc(S("yT_full"), 1)
            for t in range(NT):
                if t % 4 == 0:
                    pe.wait_ge(S("yT"), t // 4 + 1)
                if t >= 2:
                    pe.wait_ge(S("lat_copied"), t - 1)
                pe.matmul(ps[:, 4 + t % 2, 0:QL + KVL + ROPE], yT[:, P * t:P * (t + 1)], wc[:],
                          start=True, stop=True).then_inc(S("lat_full"), 1)
            for i in range(4):
                b, c = i // 2, i % 2
                if b:
                    pe.wait_ge(S("imp_copied"), i - 1)
                pe.matmul(ps[32 * b:32 * b + 1, 6 + c, :], wimp[:], yT[:, BANK * i:BANK * (i + 1)],
                          start=True, stop=True).then_inc(S("imp_full"), 1)
            for g in range(H // 4):
                mm = pe.transpose(ps[:, 0, KVL * g:KVL * (g + 1)], wdv[:, P * g:P * (g + 1)], ident[0:KVL, 0:KVL])
            mm.then_inc(S("wdvT_full"), 1)
            pe.wait_ge(S("wdvT"), 1)
            for r in range(4):
                rows = slice(32 * r, 32 * r + 32)
                for g in range(H // 4):
                    mm = pe.matmul(ps[0:KVL, r, C * g:C * (g + 1)], wdvT[rows, g, :], wpr[rows, g, :], start=True, stop=True)
                mm.then_inc(S("wvo_full"), 1)
            pe.wait_ge(S("ysum"), 2)
            pe.wait_ge(S("lat_copied"), NT)
            for b in range(B):
                mm = pe.matmul(ps[0:96, 5, 3 * b:3 * b + 3], ysum[:, b:b + 1].to_broadcast([P, 96]), wgate[:],
                               start=True, stop=True)
            mm.then_inc(S("gate_full"), 1)
            pe.wait_ge(S("zq"), 1)
            pe.wait_ge(S("wvo"), 4)
            for t in range(NT):
                mm = pe.transpose(ps[0:QL, t // 4, P * (t % 4):P * (t % 4 + 1)], zq[:, t, :], ident[:])
                if t % 4 == 3:
                    mm.then_inc(S("nq_full"), 1)
            pe.wait_ge(S("zk"), 1)
            pe.wait_ge(S("kr_rot"), 2 * B)
            for t in range(NT):
                if t % 4 == 0:
                    pe.wait_ge(S("nqT"), t // 4 + 1)
                mm = pe.transpose(ps[0:96, t // 4, P * (t % 4):P * (t % 4 + 1)], zk[:, t, :], ident[:])
                if t % 4 == 3:
                    mm.then_inc(S("kc_full"), 1)
            pe.wait_ge(S("rank2"), 1)
            pe.wait_ge(S("one1"), 1)
            for t in range(NT):
                b, r = t // TB, 32 * (t // TB)
                mm = pe.matmul(ps[:, 6 - 2 * b, t:t + 1], rank[r:r + 1, P * (t % TB):P * (t % TB + 1)], one1[r:r + 1, :],
                               start=True, stop=True)
            mm.then_inc(S("rankn_full"), 1)
            for t in range(NT):
                b = t // TB
                pe.wait_ge(S("hot"), t + 1)
                mm = pe.matmul(ps[:, 7, KEEP * b:KEEP * (b + 1)], y[:, t, :], hot[:, t, :],
                               start=(t % TB == 0), stop=(t % TB == TB - 1))
            mm.then_inc(S("sel_full"), 1)


class Ring:

    def __init__(self, first, loop, last):
        self.head = [len(first[k::RING]) for k in range(RING)]
        self.per = [len(loop[k::RING]) for k in range(RING)]
        self.place = {"first": {n: i for i, n in enumerate(first)}, "loop": {n: i for i, n in enumerate(loop)},
                      "last": {n: i for i, n in enumerate(last)}}

    def at(self, kind, slot, item):
        i = self.place[kind][item]
        k = i % RING
        return k, (i // RING if kind == "first" else self.head[k] + self.per[k] * slot + i // RING)


RING = 6
NPR = 3
CREDIT = 1
COMING = {"q", "qh", "k", "kh", "n", "v", "k2", "mt"}


def score_tiles():
    pairs = [((0, 1), 4 * c + j, c) for c in range(2) for j in range(2)]
    return pairs + [((a,), j, c) for a in (0, 1) for j in range(TB) for c in range(1 + (j >= 4))
                    if ((0, 1), j, c) not in pairs]


def timeline():
    return [
        ('q',), ('S', 0), ('S', 1), ('k',), ('qh',), ('n',), ('v',), ('S', 2), ('W', 0), ('k2',), ('mx', (0,), 7, 1),
        ('mx', (0,), 7, 0), ('mx', (0,), 4, 0), ('kh',), ('a2s',), ('W', 1), ('mx', (1,), 7, 0), ('S', 3), ('a2o',),
        ('mx', (0,), 6, 1), ('S', 4), ('W', 2), ('mx', (1,), 6, 0), ('W', 3), ('S', 5), ('mx', (0,), 5, 0), ('W', 4),
        ('mx', (1,), 7, 1), ('S', 6), ('S', 7), ('mx', (0,), 6, 0), ('mx', (0, 1), 1, 0), ('mx', (0,), 2, 0),
        ('mx', (0, 1), 5, 1), ('W', 5), ('mx', (1,), 5, 0), ('mx', (1,), 2, 0), ('mx', (0, 1), 0, 0),
        ('mx', (0,), 3, 0), ('mx', (0, 1), 4, 1), ('mx', (1,), 3, 0), ('W', 6), ('W', 7), ('mx', (1,), 4, 0), ('mx2',),
        ('invert',), ('mx', (1,), 6, 1), ('mt',), ('norm',), ('wp',),
    ]


def is_coming(step):
    return step[0] in COMING or step[0] in ("mx", "mx2")


def pieces(i):
    return [(c, max(P * i, BANK * c), BANK * (c + 1)) for c in range(2) if P * i < BANK * (c + 1)]


def items_of(steps):
    out = []
    for s in steps:
        if s[0] in ("q", "k", "n", "a2o", "wp"):
            out += [(s[0], 0), (s[0], 1)]
        elif s[0] in ("v", "k2", "mx", "mx2", "mt"):
            out.append(s)
        elif s[0] == "S":
            out += [("S", a, s[1], c) for a in (0, 1) for c, _, _ in pieces(s[1])]
        elif s[0] == "a2s":
            out += [("a2s", 0), ("a2s", 1)]
    return out


def latent_attention(nc, ins, K, ps, S, before, later):
    steps = timeline()
    first = [s for s in steps if is_coming(s)]
    last = [s for s in steps if not is_coming(s)]
    ring = Ring(items_of(first), items_of(steps), items_of(last))
    which = {"first": first, "loop": steps, "last": last}

    with ExitStack() as ctx:
        def sb(name, shape, dt=F32):
            return ctx.enter_context(nc.sbuf_tensor(name, shape, dt))

        wq = sb("wq", [QL, QK])
        wk = sb("wk", [P, QK])
        wks = sb("wks", [P, QK])
        wdk = sb("wdk", [96, NOPE])
        wvw = sb("wvw", [P, VD])
        wvs = sb("wvs", [P, VD])
        wp = sb("wp", [96, C])
        wpg = [sb(f"wpg{b}", [96, C]) for b in range(B)]
        qf = sb("qf", [QK, T])
        qt = sb("qt", [ROPE, T])
        kf = sb("kf", [QK, T])
        kt = sb("kt", [ROPE, T])
        k2f = sb("k2f", [QK, KEEP])
        k2t = sb("k2t", [ROPE, KEEP])
        qH = [sb(f"qH{b}", [99, T], F32R) for b in range(B)]
        qL_ = [sb(f"qL{b}", [QK, T], F32R) for b in range(B)]
        kH = [K["kH1"], K["kHw"], K["kH2"]]
        kL = [K["kL1"], [sb(f"kLw{b}", [QK, T], F32R) for b in range(B)], [sb(f"kL2{b}", [QK, KEEP], F32R) for b in range(B)]]
        V = [sb(f"V{b}", [P, TB, VD]) for b in range(B)]
        V2 = [sb(f"V2{b}", [KEEP, 2 * VD]) for b in range(B)]
        mpart = sb("mpart", [P, 2, 4])
        mneg = sb("mneg", [P, NBR, TB])
        mT = sb("mT", [NBR * TB, P], F32R)
        pr = [[sb(f"pr{a}{n}", [P, T]) for n in range(NPR)] for a in range(2)]
        p2 = sb("p2", [KEEP, T])
        lnD = sb("lnD", [96, T])
        rD = sb("rD", [96, T])
        tO = [sb(f"tO{b}", [96, T]) for b in range(B)]
        cN, wvo = K["cN"], K["wvo"].rearrange("p g r c -> p (g r) c")
        res, yT, nqT, kcT, ones = K["res"], K["yT"], K["nqT"], K["kcT"], K["ones"]
        cosT, sinT, ident, selT = K["cosT"], K["sinT"], K["ident"], K["selT"]

        out_ps = ps[:, RING:RING + 2, :].rearrange("p a n -> p (a n)")

        def bank(k):
            return ps[:, k, :]

        block = ctx.enter_context(nc.Block())
        full = [S(f"bank{k}_filled") for k in range(RING)]
        free = [S(f"bank{k}_read") for k in range(RING)]

        w_q_nope, w_q_rope = ins["L0_attn_w_dq_nope"], ins["L0_attn_w_dq_rope"]
        w_wink, w_selk = ins["L0_attn_w_wink"], ins["L0_attn_w_selk"]

        def per_head(ap, width):
            return ap.rearrange("k (h d) -> h k d", d=width)

        def head_loads(h):
            nope, rope = slice(ROPE, QK), slice(0, ROPE)
            return [
                (wq[:, rope], per_head(w_q_rope, ROPE)[h]), (wq[:, nope], per_head(w_q_nope, NOPE)[h]),
                (wk[:, nope], per_head(w_wink, QK)[h, :, 0:NOPE]), (wk[:, rope], per_head(w_wink, QK)[h, :, NOPE:QK]),
                (wks[:, nope], per_head(w_selk, QK)[h, :, 0:NOPE]), (wks[:, rope], per_head(w_selk, QK)[h, :, NOPE:QK]),
                (wdk[64:96, :], per_head(ins["L0_attn_w_dk_nope"], NOPE)[h]),
                (wvw[:], per_head(ins["L0_attn_w_winv"], VD)[h]), (wvs[:], per_head(ins["L0_attn_w_selv"], VD)[h]),
            ]

        NLOAD = 16 * 9
        wproj = ins["L0_attn_w_proj"].rearrange("(h d) c -> h d c", d=VD)

        def output_weights(h):
            return [(wp[0:KVL, :], wvo[:, bass.ds(h, 1), :].rearrange("p a c -> p (a c)")),
                    (wp[32:64, :], wproj[h]), (wp[64:96, :], wproj[h])]

        def run_slots(eng, slot):
            slot("first", -1, -1, 1)
            with eng.Fori(0, HEADS - 1) as h:
                slot("loop", 2 * h, h, 0)
                slot("loop", 2 * h + 1, h, 1)
            slot("loop", 2 * (HEADS - 1), HEADS - 1, 0)
            slot("last", 2 * HEADS - 1, HEADS - 1, 1)

        @block.sync
        def _(sp):
            for name in ("weighted", "out_read"):
                sp.sem_inc(S(name), CREDIT)
            before.clear(sp)
            for dst, src in head_loads(0):
                sp.dma_start(dst, src).then_inc(S("head_loaded"), 16)
            for dst, src in output_weights(0):
                sp.dma_start(dst, src).then_inc(S("wp_loaded"), 16)
            for dst, src in later:
                sp.dma_start(dst, src).then_inc(S("later_loaded"), 16)

            def slot(kind, s, h, b):
                u, ub = s + 1, 1 - b
                if kind != "first" and b == 1 and kind != "last":
                    sp.wait_ge(S("wpg_done"), 2 * h + 2)
                    for dst, src in output_weights(h + 1):
                        sp.dma_start(dst, src).then_inc(S("wp_loaded"), 16)
                if kind == "loop" and b == 0 and not (isinstance(h, int) and h == HEADS - 1):
                    k, n = ring.at(kind, s, ("k2",))
                    sp.wait_ge(full[k], n + 1)
                    for dst, src in head_loads(h + 1):
                        sp.dma_start(dst, src).then_inc(S("head_loaded"), 16)
                if kind != "last":
                    k, n = ring.at(kind, s, ("mt",))
                    sp.wait_ge(free[k], n + 1)
                    for n in range(NBR):
                        sp.dma_start(qH[ub][96 + n:97 + n, :].bitcast(F32).rearrange("a (j p) -> a j p", p=P),
                                     mT[TB * n:TB * (n + 1), :].bitcast(F32)).then_inc(S(f"maxrows{ub}"), 16)

            run_slots(sp, slot)
            if later:
                sp.wait_ge(S("later_loaded"), 16 * len(later))

        @block.tensor
        def _(pe):
            def slot(kind, s, h, b):
                u, ub = s + 1, 1 - b
                hu = h + 1 if b == 1 else h

                def take(item):
                    k, n = ring.at(kind, s, item)
                    wait_past(pe, free[k], n)
                    return k

                def product(k, out, lhsT, rhs, start=True, stop=True):
                    return pe.matmul(out, lhsT, rhs, start=start, stop=stop)

                def scores(a, i):
                    ks = slice(P * i, P * (i + 1))
                    for c, lo, hi in pieces(i):
                        k = take(("S", a, i, c))
                        o = bank(k)[:, lo - BANK * c:hi - BANK * c]
                        pe.matmul(o, kH[a][b][0:QK, ks], qL_[b][:, lo:hi], start=True, stop=False)
                        pe.matmul(o, kL[a][b][:, ks], qH[b][0:QK, lo:hi], start=False, stop=False)
                        pe.matmul(o, kH[a][b][0:99, ks], qH[b][0:99, lo:hi], start=False, stop=True).then_inc(full[k], 1)

                def weighted(i):
                    k, n = ring.at(kind, s, ("S", 1, i, 1))
                    pe.wait_ge(free[k], n + 1)
                    pe.wait_ge(S("probs"), 2 * (TB * s + i + 1))
                    if i == 0:
                        pe.wait_ge(S("out_read"), CREDIT + s)
                    for c, lo, hi in pieces(i):
                        stop = (i == TB - 1) or (i == 3 and hi == BANK)
                        for g, (a, lhsT) in enumerate(((0, cN[:, TB * b + i, :]), (1, V[b][:, i, :]),
                                                       (0, ones[:]), (1, ones[:]))):
                            mm = pe.matmul(out_ps[32 * g:32 * g + 32, lo:hi], lhsT, pr[a][i % NPR][:, lo:hi],
                                           start=(i == 0), stop=stop)
                    mm.then_inc(S("weighted"), 1)

                for step in which[kind]:
                    op = step[0]
                    if op == "q":
                        pe.wait_ge(S("head_loaded"), NLOAD * (hu + 1))
                        for c in range(2):
                            k = take((op, c))
                            pe.matmul(bank(k)[0:QK, :], wq[:], nqT[:, T * ub + BANK * c:T * ub + BANK * (c + 1)],
                                      start=True, stop=True).then_inc(full[k], 1)
                    elif op == "k":
                        for c in range(2):
                            k = take((op, c))
                            pe.matmul(bank(k)[0:QK, :], wk[:], yT[:, T * ub + BANK * c:T * ub + BANK * (c + 1)],
                                      start=True, stop=True).then_inc(full[k], 1)
                    elif op == "n":
                        for c in range(2):
                            k, m = ring.at(kind, s, (op, c))
                            wait_apart(pe, S, free[k], m)
                            pe.matmul(bank(k)[64:96, :], wdk[64:96, :],
                                      kcT[64:96, T * ub + BANK * c:T * ub + BANK * (c + 1)],
                                      start=True, stop=True).then_inc(full[k], 1)
                    elif op == "v":
                        k = take(step)
                        for t in range(TB):
                            tok = slice(T * ub + P * t, T * ub + P * (t + 1))
                            mm = pe.matmul(bank(k)[:, VD * t:VD * (t + 1)], yT[:, tok], wvw[:], start=True, stop=True)
                        mm.then_inc(full[k], 1)
                    elif op == "k2":
                        k = take(step)
                        sel = selT[:, KEEP * ub:KEEP * (ub + 1)]
                        pe.matmul(bank(k)[0:QK, 0:KEEP], wks[:], sel, start=True, stop=True)
                        pe.matmul(bank(k)[0:KEEP, 64:64 + VD], sel, wvs[:], start=True, stop=True).then_inc(full[k], 1)
                    elif op == "mx":
                        _, branches, j, c = step
                        k = take(step)
                        hi = min(P * (j + 1), BANK * (c + 1))
                        w = hi - BANK * c
                        diag = hi == P * (j + 1)
                        for n, a in enumerate(branches):
                            if step == next(x for x in steps if x[0] == "mx" and a in x[1]):
                                pe.wait_ge(S("qH_done"), 2 * (u + 1))
                                pe.wait_ge(S("kHw_done") if a else S("kH1_done"), 2 * (u + 1))
                            mm = pe.matmul(bank(k)[:, w * n:w * (n + 1)], qH[ub][0:QK, P * j:P * (j + 1)],
                                           kH[a][ub][0:QK, BANK * c:hi], start=True, stop=not diag)
                            if diag:
                                mm = pe.matmul(bank(k)[:, w * (n + 1) - P:w * (n + 1)], K["identb"][:], K["maskb"][:],
                                               start=False, stop=True)
                        mm.then_inc(full[k], 1)
                    elif op == "mx2":
                        k = take(step)
                        pe.wait_ge(S("k2_done"), u + 1)
                        for j in range(TB):
                            mm = pe.matmul(bank(k)[:, KEEP * j:KEEP * (j + 1)], qH[ub][0:QK, P * j:P * (j + 1)],
                                           kH[2][ub][0:QK, :], start=True, stop=True)
                        mm.then_inc(full[k], 1)
                    elif op == "mt":
                        k = take(step)
                        pe.wait_ge(S("mneg"), u + 1)
                        pe.transpose(bank(k)[0:NBR * TB, 0:P], mneg[:].rearrange("p a j -> p (a j)"), ident[:]).then_inc(full[k], 1)
                    elif op == "S":
                        i = step[1]
                        if i == 0:
                            pe.wait_ge(S(f"maxrows{b}"), 48 * (h + 1))
                            pe.wait_ge(S("qL_done"), s + 1)
                            pe.wait_ge(S("kLw_done"), s + 1)
                        scores(0, i)
                        scores(1, i)
                    elif op == "W":
                        weighted(step[1])
                    elif op == "a2s":
                        pe.wait_ge(S("k2_done"), s + 1)
                        for c, lo, hi in pieces(0):
                            k = take((op, c))
                            o = bank(k)[0:KEEP, :]
                            pe.matmul(o, kH[2][b][0:QK, :], qL_[b][:, lo:hi], start=True, stop=False)
                            pe.matmul(o, kL[2][b][:], qH[b][0:QK, lo:hi], start=False, stop=False)
                            pe.matmul(o, kH[2][b][0:99, :], qH[b][0:99, lo:hi], start=False, stop=True).then_inc(full[k], 1)
                    elif op == "a2o":
                        for c in range(2):
                            k, n = ring.at(kind, s, ("a2s", c))
                            pe.wait_ge(free[k], n + 1)
                            k = take((op, c))
                            cols = slice(BANK * c, BANK * (c + 1))
                            pe.matmul(bank(k)[64:128, :], V2[b][:], p2[:, cols], start=True, stop=True).then_inc(full[k], 1)
                    elif op == "wp":
                        pe.wait_ge(S("out_read"), CREDIT + s + 1)
                        pe.wait_ge(S("wpg_done"), s + 1)
                        for c in range(2):
                            k = take((op, c))
                            for t in range(4):
                                j = 4 * c + t
                                mm = pe.matmul(bank(k)[:, P * t:P * (t + 1)], tO[b][:, P * j:P * (j + 1)], wpg[b][:],
                                               start=True, stop=True)
                            mm.then_inc(full[k], 1)

            run_slots(pe, slot)

        @block.scalar
        def _(act):
            act.preload_act_table_set("natural_log_exp_and_others")

            def slot(kind, s, h, b):
                u, ub = s + 1, 1 - b

                def filled(item):
                    k, n = ring.at(kind, s, item)
                    act.wait_ge(full[k], n + 1)
                    return k

                def exponentials(a, i):
                    act.wait_ge(S("weighted"), CREDIT + TB * s + max(i - NPR + 1, 0))
                    for c, lo, hi in pieces(i):
                        k = filled(("S", a, i, c))
                        act.activation(pr[a][i % NPR][:, lo:hi], bank(k)[:, lo - BANK * c:hi - BANK * c],
                                       ACT.Exp).then_inc(free[k], 1)

                for step in which[kind]:
                    op = step[0]
                    if op in ("q", "k"):
                        dst = qf if op == "q" else kf
                        wait_past(act, S("qL_done" if op == "q" else "kLw_done"), u)
                        for c in range(2):
                            k = filled((op, c))
                            act.activation(dst[64:96, BANK * c:BANK * (c + 1)], bank(k)[64:96, :], ACT.Copy).then_inc(S(f"{op}plain"), 1)
                    elif op in ("qh", "kh"):
                        o, src, dst = ("q", qf, qH[ub]) if op == "qh" else ("k", kf, kH[1][ub])
                        name = "qH_done" if op == "qh" else "kHw_done"
                        act.wait_ge(S(f"{o}plain"), 2 * (u + 1))
                        act.wait_ge(S(f"{o}rot"), u + 1)
                        for c in range(2):
                            act.activation(dst[0:QK, BANK * c:BANK * (c + 1)], src[:, BANK * c:BANK * (c + 1)], ACT.Copy).then_inc(S(name), 1)
                    elif op == "n":
                        for c in range(2):
                            k = filled((op, c))
                            act.activation(kH[0][ub][64:96, BANK * c:BANK * (c + 1)], bank(k)[64:96, :], ACT.Copy).then_inc(S("kH1_done"), 1)
                    elif op == "v":
                        k = filled(step)
                        act.activation(V[ub][:].rearrange("p t d -> p (t d)"), bank(k)[:, 0:TB * VD], ACT.Copy).then_inc(free[k], 1)
                    elif op == "mt":
                        k = filled(step)
                        if kind == "first":
                            pass
                        elif b == 0:
                            act.wait_ge(S("maxrows0"), 48 * (h + 1))
                        else:
                            act.wait_ge(S("maxrows1"), 48 * (h + 1))
                        act.activation(mT[:], bank(k)[0:NBR * TB, 0:P], ACT.Copy).then_inc(free[k], 1)
                    elif op == "S":
                        exponentials(0, step[1])
                        exponentials(1, step[1])
                    elif op == "a2s":
                        for c, lo, hi in pieces(0):
                            k = filled((op, c))
                            act.activation(p2[:, lo:hi], bank(k)[0:KEEP, :], ACT.Exp).then_inc(free[k], 1)
                    elif op == "a2o":
                        for c in range(2):
                            k = filled((op, c))
                            cols = slice(BANK * c, BANK * (c + 1))
                            act.activation(lnD[64:96, cols], bank(k)[96:128, :], ACT.Ln).then_inc(S("ln2"), 1)
                            act.wait_ge(S("ln2"), 2 * s + c + 1)
                            act.activation(rD[64:96, cols], lnD[64:96, cols], ACT.Exp, scale=-1.0).then_inc(S("rD2"), 1)
                    elif op == "invert":
                        act.wait_ge(S("weighted"), CREDIT + TB * (s + 1))
                        act.activation(lnD[0:64, :], out_ps[64:128, :], ACT.Ln).then_inc(S("ln01"), 1)
                        act.wait_ge(S("ln01"), s + 1)
                        act.activation(rD[0:64, :], lnD[0:64, :], ACT.Exp, scale=-1.0).then_inc(S("rD01"), 1)

            run_slots(act, slot)

        @block.gpsimd
        def _(pool):
            def slot(kind, s, h, b):
                u, ub = s + 1, 1 - b
                for step in which[kind]:
                    op = step[0]
                    if op in ("qh", "kh"):
                        o, f, t, hi, lo = ("q", qf, qt, qH[ub], qL_[ub]) if op == "qh" else ("k", kf, kt, kH[1][ub], kL[1][ub])
                        pool.wait_ge(S(f"{o}terms"), 4 * (u + 1))
                        for c in range(2):
                            k, n = ring.at(kind, s, (o, c))
                            pool.wait_ge(free[k], n + 1)
                        pool.tensor_tensor(f[0:ROPE, :], f[0:ROPE, :], t[:], ALU.add).then_inc(S(f"{o}rot"), 1)
                        pool.wait_ge(S("qH_done" if op == "qh" else "kHw_done"), 2 * (u + 1))
                        pool.tensor_tensor(lo[:], f[:], hi[0:QK, :].bitcast(F32), ALU.subtract).then_inc(
                            S("qL_done" if op == "qh" else "kLw_done"), 1)
                    elif op == "S":
                        i = step[1]
                        for a in range(2):
                            k, n = ring.at(kind, s, ("S", a, i, pieces(i)[0][0]))
                            wait_apart(pool, S, free[k], n + 1)
                            d = pr[a][i % NPR][:, P * i:P * (i + 1)]
                            pool.affine_select(out=d, in_=d, pattern=[[1, P]], compare_op=ALU.is_ge, fill=0.0, base=0,
                                               channel_multiplier=-1).then_inc(S("probs"), 1)
                    elif op == "a2o":
                        wait_apart(pool, S, S("wp_loaded"), 48 * (h + 1))
                        pool.tensor_scalar(wpg[b][:], wp[:], K["gcol"][:, b:b + 1], None, ALU.mult).then_inc(S("wpg_done"), 1)

            run_slots(pool, slot)

        @block.vector
        def _(dve):
            def slot(kind, s, h, b):
                u, ub = s + 1, 1 - b

                def filled(item):
                    k, n = ring.at(kind, s, item)
                    dve.wait_ge(full[k], n + 1)
                    return k

                for step in which[kind]:
                    op = step[0]
                    if op in ("q", "k"):
                        f, t = (qf, qt) if op == "q" else (kf, kt)
                        wait_past(dve, S("qL_done" if op == "q" else "kLw_done"), u)
                        for c in range(2):
                            k = filled((op, c))
                            cols = slice(BANK * c, BANK * (c + 1))
                            dve.tensor_tensor(f[0:ROPE, cols], bank(k)[0:ROPE, :], cosT[:, cols], ALU.mult).then_inc(S(f"{op}terms"), 1)
                            dve.tensor_tensor(t[0:HALF, cols], bank(k)[HALF:ROPE, :], sinT[HALF:ROPE, cols], ALU.mult).then_inc(S(f"{op}terms"), 1)
                            dve.wait_ge(S(f"{op}plain"), 2 * u + c + 1)
                            dve.tensor_tensor(t[HALF:ROPE, cols], bank(k)[0:HALF, :], sinT[0:HALF, cols], ALU.mult).then_inc(free[k], 1)
                    elif op == "n":
                        for c in range(2):
                            k = filled((op, c))
                            cols = slice(BANK * c, BANK * (c + 1))
                            dve.wait_ge(S("kH1_done"), 2 * u + c + 1)
                            dve.tensor_tensor(kL[0][ub][64:96, cols], bank(k)[64:96, :], kH[0][ub][64:96, cols].bitcast(F32),
                                              ALU.subtract).then_inc(free[k], 1)
                    elif op == "k2":
                        k = filled(step)
                        kk = bank(k)[:, 0:KEEP]
                        x = S("k2_chain")
                        dve.tensor_tensor(k2f[0:ROPE, :], kk[0:ROPE, :], cosT[:, 0:KEEP], ALU.mult).then_inc(x, 1)
                        dve.tensor_tensor(k2t[0:HALF, :], kk[HALF:ROPE, :], sinT[HALF:ROPE, 0:KEEP], ALU.mult).then_inc(x, 1)
                        dve.tensor_tensor(k2t[HALF:ROPE, :], kk[0:HALF, :], sinT[0:HALF, 0:KEEP], ALU.mult).then_inc(x, 1)
                        dve.tensor_copy(k2f[64:96, :], kk[64:96, :]).then_inc(x, 1)
                        dve.tensor_copy(V2[ub][:, 0:VD], bank(k)[0:KEEP, 64:64 + VD]).then_inc(x, 1)
                        dve.wait_ge(x, 6 * u + 5)
                        dve.tensor_tensor(k2f[0:ROPE, :], k2f[0:ROPE, :], k2t[:], ALU.add).then_inc(free[k], 1)
                        dve.wait_ge(free[k], ring.at(kind, s, step)[1] + 1)
                        dve.tensor_copy(kH[2][ub][0:QK, :], k2f[:]).then_inc(x, 1)
                        dve.wait_ge(x, 6 * u + 6)
                        dve.tensor_tensor(kL[2][ub][:], k2f[:], kH[2][ub][0:QK, :].bitcast(F32), ALU.subtract).then_inc(S("k2_done"), 1)
                    elif op == "mx":
                        _, branches, j, c = step
                        k = filled(step)
                        na = len(branches)
                        a = slice(branches[0], branches[-1] + 1)
                        w = min(P * (j + 1), BANK * (c + 1)) - BANK * c
                        dst = mneg[:, a, j] if c == 0 else mpart[:, a, j - 4]
                        dve.tensor_reduce(dst, bank(k)[:, 0:na * w].rearrange("p (a n) -> p a n", a=na), AX.X, ALU.max, negate=True).then_inc(free[k], 1)
                    elif op == "mx2":
                        k = filled(step)
                        dve.tensor_reduce(mneg[:, 2, :], bank(k)[:, 0:KEEP * TB].rearrange("p (j n) -> p j n", n=KEEP),
                                          AX.X, ALU.max, negate=True).then_inc(free[k], 1)
                    elif op == "mt":
                        for item in [x for x in steps if x[0] in ("mx", "mx2")][-2:]:
                            k, n = ring.at(kind, s, item)
                            dve.wait_ge(free[k], n + 1)
                        dve.tensor_tensor(mneg[:, 0:2, 4:8], mneg[:, 0:2, 4:8], mpart[:], ALU.min).then_inc(S("mneg"), 1)
                    elif op == "a2o":
                        for c in range(2):
                            k = filled((op, c))
                            cols = slice(BANK * c, BANK * (c + 1))
                            dve.wait_ge(S("rD2"), 2 * s + c + 1)
                            dve.tensor_tensor(tO[b][64:96, cols], bank(k)[64:96, :], rD[64:96, cols], ALU.mult).then_inc(free[k], 1)
                    elif op == "norm":
                        dve.wait_ge(S("rD01"), s + 1)
                        dve.tensor_tensor(tO[b][0:64, :], out_ps[0:64, :], rD[0:64, :], ALU.mult).then_inc(S("out_read"), 1)
                    elif op == "wp":
                        for c in range(2):
                            k = filled((op, c))
                            rows = res[:, TB * b + 4 * c:TB * b + 4 * (c + 1), :].rearrange("p t c -> p (t c)")
                            dve.tensor_tensor(rows, bank(k), rows, ALU.add).then_inc(free[k], 1)

            for b in range(B):
                dve.memset(V2[b][:, VD:], 1.0).then_inc(S("v2_ones"), 1)
            run_slots(dve, slot)


def bank_uses(steps_of_kind, uses):
    table, totals = {}, {}
    for kind, steps in steps_of_kind.items():
        count = {}
        for s in steps:
            for n, k in enumerate(uses.get(s, ())):
                table[kind, s, n] = (k, count.get(k, 0))
                count[k] = count.get(k, 0) + 1
        totals[kind] = count

    def at(kind, slot, step, nth=0):
        k, i = table[kind, step, nth]
        return k, (i if kind == "first" else totals["first"].get(k, 0) + totals["loop"].get(k, 0) * slot + i)

    return at


def ffn_weights(ins, F):
    loads = [(F["shift"][:], ins["c_shift"]), (F["edge"][:], ins["c_edge"]), (F["near"][:], ins["c_near"]),
             (F["flags"][:], ins["c_flags"]), (F["starts"][:], ins["c_starts"]),
             (F["wqkv"][:], ins["L0_ffn_wqkv"].rearrange("l c n -> c l n")),
             (F["wo"][:], ins["L0_ffn_wo"].rearrange("l (m p) c -> p l m c", p=P)),
             (F["w1"][:], ins["L0_ffn_w1"].rearrange("l c n -> c l n"))]
    for l in range(DEPTH):
        loads.append((F["lg"][:, l:l + 1], ins["L0_ffn_ln_g"][l].rearrange("(p a) -> p a", a=1)))
        loads.append((F["lb"][:, l:l + 1], ins["L0_ffn_ln_b"][l].rearrange("(p a) -> p a", a=1)))
        loads.append((F["b2"][:, l, :], ins["L0_ffn_b2"][l:l + 1, :].to_broadcast([P, C])))
        for c, (o, w) in enumerate(HCH):
            loads.append((F["w2"][0:w, l, c, :], ins["L0_ffn_w2"][l, o:o + w, :]))
            for half in range(2):
                loads.append((F["b1"][0:w, l, 3 * half + c:3 * half + c + 1],
                              ins["L0_ffn_b1"][l, HID * half + o:HID * half + o + w].rearrange("(p a) -> p a", a=1)))
    return loads


def ffn_begin(nc, ins, F, ps, S, before):
    with ExitStack() as ctx:
        def sb(name, shape, dt=F32):
            return ctx.enter_context(nc.sbuf_tensor(name, shape, dt))

        raw = sb("raw_tables", [P, 4, TB, FD])
        gains = sb("gains", [P, DEPTH, 4, FD])
        stats = sb("f_stats", [P, NT, 6])
        mv = sb("f_mv", [P, NT, 2])
        va = sb("f_va", [P, NT])
        sd = sb("f_sd", [P, NT])
        rs = sb("f_rs", [P, NT])
        res, xf, tabs = F["res"], F["xf"], F["tabs"]
        loads = [(raw[:, n], ins[name].rearrange("(t p) d -> p t d", p=P))
                 for n, name in enumerate(("c_qcos", "c_qsin", "c_kcos", "c_ksin"))]
        for l in range(DEPTH):
            for n, name in ((0, "L0_ffn_q_scale"), (2, "L0_ffn_k_scale")):
                row = ins[name][l:l + 1, :]
                loads.append((gains[:, l, n, :], row.to_broadcast([P, FD])))
                loads.append((gains[:, l, n + 1, 0:HALF], row[:, HALF:FD].to_broadcast([P, HALF])))
                loads.append((gains[:, l, n + 1, HALF:FD], row[:, 0:HALF].to_broadcast([P, HALF])))
        block = ctx.enter_context(nc.Block())

        @block.sync
        def _(sp):
            before.clear(sp)
            for dst, src in loads:
                sp.dma_start(dst, src).then_inc(S("tables_loaded"), 16)

        @block.gpsimd
        def _(pool):
            pool.memset(F["minus_half"][:], -0.5).then_inc(S("zeroed"), 1)
            pool.memset(F["kT"][3][:], 0.0).then_inc(S("zeroed"), 1)
            pool.memset(F["vN"][3][:], 0.0).then_inc(S("zeroed"), 1)
            pool.memset(F["sm"][:], 0.0).then_inc(S("zeroed"), 1)
            pool.memset(xf[:, 0, :], 0.0).then_inc(S("zeroed"), 1)
            pool.wait_ge(S("tables_loaded"), 16 * len(loads))
            for l in (1,):
                for n in range(4):
                    for b in range(B):
                        pool.tensor_tensor(tabs[:, l, n, TB * b:TB * (b + 1), :], raw[:, n],
                                           gains[:, l, n:n + 1, :].to_broadcast([P, TB, FD]), ALU.mult).then_inc(S("tabs"), 1)

        @block.scalar
        def _(act):
            act.wait_ge(S("f_var"), 1)
            act.activation(sd[:], va[:], ACT.Sqrt).then_inc(S("f_std"), 1)

        @block.vector
        def _(dve):
            for t in range(NT):
                dve.bn_stats(stats[:, t, :], res[:, t, :]).then_inc(S("f_stats"), 1)
            for t in range(NT):
                dve.wait_ge(S("f_stats"), t + 1)
                dve.bn_aggr(mv[:, t, :], stats[:, t, :]).then_inc(S("f_aggr"), 1)
            dve.wait_ge(S("f_aggr"), NT)
            dve.tensor_scalar(va[:], mv[:, :, 1], 1e-5, None, ALU.add).then_inc(S("f_var"), 1)
            dve.wait_ge(S("f_std"), 1)
            dve.reciprocal(rs[:], sd[:]).then_inc(S("f_rstd"), 1)
            dve.wait_ge(S("f_rstd"), 1)
            for t in range(NT):
                dve.tensor_scalar(xf[:, t + 1, :], res[:, t, :], mv[:, t, 0:1], rs[:, t:t + 1],
                                  ALU.subtract, ALU.mult).then_inc(S("xf"), 1)
            dve.wait_ge(S("tables_loaded"), 16 * len(loads))
            for n in range(4):
                for b in range(B):
                    dve.tensor_tensor(tabs[:, 0, n, TB * b:TB * (b + 1), :], raw[:, n],
                                      gains[:, 0, n:n + 1, :].to_broadcast([P, TB, FD]), ALU.mult).then_inc(S("tabs"), 1)


def window_order():
    return ["ax", "ah", "bs0", "aq0", "bs1", "bt0", "bt1", "aq1", "ar0", "bt2", "as", "bv0", "bt3", "ar1",
            "bv1", "bv2", "bv3", "bo", "bw", "an0", "aq2", "an1", "at0", "bx", "at1"]


def window_attention(nc, F, ps, l, S):
    steps = window_order()
    kinds = {"first": [s for s in steps if s[0] == "a"], "loop": steps, "last": [s for s in steps if s[0] == "b"]}
    at = bank_uses(kinds, {"ah": (0,), "bw": (0,), "bx": (0,), "aq0": (1,), "aq1": (2,), "aq2": (3,), "at0": (1,),
                           "at1": (2,), "bs0": (4, 5), "bs1": (4, 5), "bt0": (6,), "bt1": (7,), "bt2": (6,), "bt3": (7,),
                           "bv0": (3,)})
    with ExitStack() as ctx:
        def sb(name, shape, dt=F32):
            return ctx.enter_context(nc.sbuf_tensor(f"{name}_l{l}", shape, dt))

        xa = sb("xa", [P, C])
        xb = sb("xb", [P, FD])
        hT = sb("hT", [P, P])
        sq = sb("sq", [P, 2, INNER])
        ss = sb("ss", [P, 2 * FH])
        rn = sb("rn", [P, 2 * FH])
        qk = [sb(f"qk{n}", [P, INNER]) for n in range(2)]
        qs = [sb(f"qs{n}", [P, INNER]) for n in range(2)]
        qT = [sb(f"qT{n}", [P, 4, P]) for n in range(2)]
        band = sb("band", [P, P + WIN])
        mx = sb("mx", [P, FH])
        ng = sb("ng", [P, FH])
        rs = sb("rs", [P, FH])
        rr = sb("rr", [P, FH])
        pT = [sb(f"pT{n}", [P, 4, P]) for n in range(4)]
        oN = sb("oN", [P, INNER])
        oT = sb("oT", [P, 4, P])
        xf, tabs, flags, ident, shift, edge = (F[k] for k in ("xf", "tabs", "flags", "ident", "shift", "edge"))
        near, starts = F["near"], F["starts"]
        kT, vN, sm, wqkv, wo = F["kT"], F["vN"], F["sm"], F["wqkv"], F["wo"]
        block = ctx.enter_context(nc.Block())
        full = [S(f"bank{k}_filled") for k in range(8)]
        free = [S(f"bank{k}_read") for k in range(8)]

        def heads(ap):
            return ap.rearrange("p (h d) -> p h d", h=FH)

        def run_slots(eng, slot):
            slot("first", 0, 0)
            with eng.Fori(0, LOOPS) as i:
                for r in range(4):
                    slot("loop", 4 * i + r + 1, (r + 1) % 4)
            for t in range(4 * LOOPS + 1, 4 * LOOPS + 4):
                slot("loop", t, t % 4)
            slot("last", 4 * LOOPS + 4, 0)

        def prev(kind, t, step, nth=0):
            k, n = at(kind, 0 if kind == "first" else t - 1, step, nth)
            return k, n

        @block.sync
        def _(sp):
            for k in range(8):
                sp.sem_inc(free[k], CREDIT)

        @block.tensor
        def _(pe):
            def slot(kind, t, r):
                g = t - 1
                rg, rp = (r - 1) % 4, (r - 2) % 4

                def take(step, nth=0):
                    k, n = prev(kind, t, step, nth)
                    pe.wait_ge(free[k], CREDIT + n)
                    return k

                for step in kinds[kind]:
                    if step == "ah":
                        k = take(step)
                        pe.wait_ge(S("x_copied"), 2 * (t + 1))
                        pe.matmul(ps[0:64, k, 0:P], xa[:, 0:FD], ident[:], start=True, stop=True)
                        pe.matmul(ps[64:128, k, 0:P], xa[:, FD:C], shift[:], start=True, stop=False)
                        pe.matmul(ps[64:128, k, 0:P], xb[:], edge[:], start=False, stop=True).then_inc(full[k], 1)
                    elif step[0:2] == "aq":
                        n = int(step[2])
                        if n == 0:
                            hk, hn = prev(kind, t, "ah")
                            pe.wait_ge(free[hk], CREDIT + hn + 1)
                        k = take(step)
                        pe.matmul(ps[:, k, :], hT[:], wqkv[:, l, INNER * n:INNER * (n + 1)],
                                  start=True, stop=True).then_inc(full[k], 1)
                    elif step in ("at0", "at1"):
                        n = int(step[2])
                        k = take(step)
                        pe.wait_ge(S("qk_scaled"), 2 * t + n + 1)
                        for m in range(4):
                            mm = pe.transpose(ps[:, k, P * m:P * (m + 1)], qk[n][:, P * m:P * (m + 1)], ident[:])
                        mm.then_inc(full[k], 1)
                    elif step in ("bs0", "bs1"):
                        gr = int(step[2])
                        if gr == 0:
                            for n in range(2):
                                pk, pn = at("loop", t - 2, f"at{n}")
                                pe.wait_ge(free[pk], CREDIT + pn + 1)
                        for o in range(2):
                            k = take(step, o)
                            rows = slice(FD * o, FD * (o + 1))
                            for e in range(2):
                                hp = 2 * gr + e
                                q = qT[rg % 2][rows, hp, :]
                                pe.matmul(ps[:, k, 192 * e:192 * e + 64], q, kT[rp][rows, hp, 64:128], start=True, stop=True)
                                mm = pe.matmul(ps[:, k, 192 * e + 64:192 * e + 192], q, kT[rg][rows, hp, :], start=True, stop=True)
                            mm.then_inc(full[k], 1)
                    elif step[0:2] == "bt":
                        m = int(step[2])
                        k = take(step)
                        pe.wait_ge(S("probs"), FH * g + 2 * m + 2)
                        for j in range(4):
                            mm = pe.transpose(ps[:, k, P * j:P * (j + 1)], sm[:, 2 * m + j // 2, P * (j % 2):P * (j % 2 + 1)], ident[:])
                        mm.then_inc(full[k], 1)
                    elif step[0:2] == "bv":
                        weighted(kind, t, int(step[2]), rg, rp)
                    elif step == "bw":
                        k = take(step)
                        pe.wait_ge(S("oN"), g + 1)
                        for m in range(4):
                            mm = pe.transpose(ps[:, k, P * m:P * (m + 1)], oN[:, P * m:P * (m + 1)], ident[:])
                        mm.then_inc(full[k], 1)
                    elif step == "bx":
                        wk, wn = prev(kind, t, "bw")
                        pe.wait_ge(free[wk], CREDIT + wn + 1)
                        k = take(step)
                        for m in range(4):
                            mm = pe.matmul(ps[:, k, 0:P], oT[:, m, :], wo[:, l, m, :], start=(m == 0), stop=(m == 3))
                        mm.then_inc(full[k], 1)

            def weighted(kind, t, m, rg, rp):
                k6, n6 = prev(kind, t, f"bt{m}")
                pe.wait_ge(free[k6], CREDIT + n6 + 1)
                k, n = prev(kind, t, "bv0")
                if m == 0:
                    pe.wait_ge(free[k], CREDIT + n)
                for j in range(2):
                    hh = 2 * m + j
                    cols = slice(FD * hh, FD * (hh + 1))
                    pe.matmul(ps[:, k, cols], pT[m][:, 2 * j + 1, :], vN[rg][:, cols], start=True, stop=False)
                    mm = pe.matmul(ps[:, k, cols], pT[m][64:128, 2 * j, :], vN[rp][64:128, cols], start=False, stop=True)
                if m == 3:
                    mm.then_inc(full[k], 1)

            run_slots(pe, slot)

        @block.scalar
        def _(act):
            def slot(kind, t, r):
                g = t - 1

                def filled(step, nth=0):
                    k, n = prev(kind, t, step, nth)
                    act.wait_ge(full[k], n + 1)
                    return k

                for step in kinds[kind]:
                    if step == "ah":
                        k = filled(step)
                        act.activation(hT[:], ps[:, k, 0:P], ACT.Copy).then_inc(free[k], 1)
                    elif step in ("aq0", "aq1"):
                        n = int(step[2])
                        if n == 0:
                            wait_past(act, S("sums"), t)
                        k = filled(step)
                        act.activation(sq[:, n, :], ps[:, k, :], ACT.Square).then_inc(S("squares"), 1)
                    elif step == "aq2":
                        k = filled(step)
                        act.activation(vN[r][:], ps[:, k, :], ACT.Copy).then_inc(free[k], 1)
                    elif step in ("at0", "at1"):
                        dst = (qT[r % 2], kT[r])[int(step[2])]
                        k = filled(step)
                        act.activation(dst[:].rearrange("p a n -> p (a n)"), ps[:, k, :], ACT.Copy).then_inc(free[k], 1)
                    elif step in ("bs0", "bs1"):
                        gr = int(step[2])
                        act.wait_ge(S("neg_max"), 2 * g + gr + 1)
                        for hh in range(4 * gr, 4 * gr + 4):
                            act.activation(sm[:, hh, 64:256], sm[:, hh, 64:256], ACT.Exp, bias=ng[:, hh:hh + 1],
                                           accum_out=rs[:, hh:hh + 1]).then_inc(S("probs"), 1)
                    elif step in ("bt1", "bt3"):
                        k = filled(step)
                        act.activation(pT[int(step[2])][:].rearrange("p a n -> p (a n)"), ps[:, k, :], ACT.Copy).then_inc(free[k], 1)
                    elif step == "bw":
                        k = filled(step)
                        act.activation(oT[:].rearrange("p a n -> p (a n)"), ps[:, k, :], ACT.Copy).then_inc(free[k], 1)

            run_slots(act, slot)

        @block.gpsimd
        def _(pool):
            def slot(kind, t, r):
                for step in kinds[kind]:
                    if step == "as":
                        pool.wait_ge(S("clipped"), t + 1)
                        pool.tensor_tensor(rn[:], ss[:], F["minus_half"][:], ALU.pow).then_inc(S("rn"), 1)
                    elif step in ("ar0", "ar1"):
                        n = int(step[2])
                        pool.wait_ge(S("cos_terms"), 2 * t + n + 1)
                        k, m = prev(kind, t, f"aq{n}")
                        pool.wait_ge(free[k], CREDIT + m + 1)
                        pool.tensor_tensor(qk[n][:], qk[n][:], qs[n][:], ALU.add).then_inc(S("rotated"), 1)

            run_slots(pool, slot)

        @block.vector
        def _(dve):
            def slot(kind, t, r):
                g = t - 1

                def filled(step, nth=0):
                    k, n = prev(kind, t, step, nth)
                    dve.wait_ge(full[k], n + 1)
                    return k

                for step in kinds[kind]:
                    if step == "ax":
                        dve.tensor_copy(xa[:], xf[:, t + 1, :]).then_inc(S("x_copied"), 1)
                        dve.tensor_scalar(xb[:], xf[:, t, FD:C], flags[:, bass.ds(t, 1)], None, ALU.mult).then_inc(S("x_copied"), 1)
                    elif step == "as":
                        dve.wait_ge(S("squares"), 2 * (t + 1))
                        dve.tensor_reduce(ss[:], sq[:].rearrange("p a (h d) -> p (a h) d", h=FH), AX.X, ALU.add).then_inc(S("sums"), 1)
                        dve.wait_ge(S("sums"), t + 1)
                        dve.tensor_scalar(ss[:], ss[:], 1e-24, None, ALU.max).then_inc(S("clipped"), 1)
                    elif step in ("ar0", "ar1"):
                        n = int(step[2])
                        k = filled(f"aq{n}")
                        dve.wait_ge(S("squares"), 2 * t + n + 1)
                        dve.tensor_tensor(heads(qk[n][:]), heads(ps[:, k, :]),
                                          tabs[:, l, 2 * n, bass.ds(t, 1), :].to_broadcast([P, FH, FD]), ALU.mult).then_inc(S("cos_terms"), 1)
                        for o in range(2):
                            src = heads(ps[:, k, :])[:, :, HALF * (1 - o):HALF * (2 - o)]
                            dst = heads(qs[n][:])[:, :, HALF * o:HALF * (o + 1)]
                            tab = tabs[:, l, 2 * n + 1, bass.ds(t, 1), HALF * o:HALF * (o + 1)].to_broadcast([P, FH, HALF])
                            dve.tensor_tensor(dst, src, tab, ALU.mult).then_inc(free[k] if o else S("sin_terms"), 1)
                    elif step in ("an0", "an1"):
                        n = int(step[2])
                        dve.wait_ge(S("rn"), t + 1)
                        dve.wait_ge(S("rotated"), 2 * t + n + 1)
                        dve.tensor_tensor(heads(qk[n][:]), heads(qk[n][:]),
                                          rn[:, FH * n:FH * (n + 1)].unsqueeze(2).to_broadcast([P, FH, FD]),
                                          ALU.mult).then_inc(S("qk_scaled"), 1)
                    elif step in ("bs0", "bs1"):
                        gr = int(step[2])
                        if gr == 0:
                            dve.tensor_scalar(band[:, 0:WIN], near[:, 0:WIN], starts[:, bass.ds(g, 1)], None,
                                              ALU.add).then_inc(S("band"), 1)
                            dve.wait_ge(S("band"), g + 2)
                            pk, pn = at("loop", t - 2, "bt3")
                            dve.wait_ge(free[pk], CREDIT + pn + 1)
                        k4, k5 = filled(step, 0), filled(step, 1)
                        dve.sem_inc(S("passed_DVE"), 1)
                        for o, k in enumerate((k4, k5)):
                            for e in range(2):
                                hh = 4 * gr + 2 * e + o
                                dve.tensor_tensor_reduce(sm[:, hh, 64:256], ps[:, k, 192 * e:192 * e + 192], band[:], 1.0,
                                                         -3.0e38, ALU.add, ALU.max, mx[:, hh:hh + 1]).then_inc(free[k] if e else S("maxed"), 1)
                        dve.wait_ge(S("maxed"), 4 * g + 2 * gr + 2)
                        for o in range(2):
                            k, n = prev(kind, t, step, o)
                            dve.wait_ge(free[k], CREDIT + n + 1)
                        dve.tensor_scalar(ng[:, 4 * gr:4 * gr + 4], mx[:, 4 * gr:4 * gr + 4], -1.0, None, ALU.mult).then_inc(S("neg_max"), 1)
                    elif step in ("bt0", "bt2"):
                        k = filled(step)
                        dve.tensor_copy(pT[int(step[2])][:].rearrange("p a n -> p (a n)"), ps[:, k, :]).then_inc(free[k], 1)
                    elif step == "bo":
                        dve.wait_ge(S("probs"), FH * (g + 1))
                        dve.reciprocal(rr[:], rs[:]).then_inc(S("rr"), 1)
                        dve.wait_ge(S("rr"), g + 1)
                        k = filled("bv0")
                        dve.tensor_tensor(heads(oN[:]), heads(ps[:, k, :]), rr[:].unsqueeze(2).to_broadcast([P, FH, FD]),
                                          ALU.mult).then_inc(S("oN"), 1)
                        dve.wait_ge(S("oN"), g + 1)
                        dve.sem_inc(free[k], 1)
                    elif step == "bx":
                        k = filled(step)
                        dve.tensor_tensor(xf[:, t, :], ps[:, k, 0:P], xf[:, t, :], ALU.add).then_inc(free[k], 1)

            dve.tensor_copy(band[:], near[:]).then_inc(S("band"), 1)
            run_slots(dve, slot)


def gated_mlp(nc, F, ps, l, S, out_ap=None):
    NC4, W = NT // 4, BANK
    with ExitStack() as ctx:
        def sb(name, shape, dt=F32):
            return ctx.enter_context(nc.sbuf_tensor(f"{name}_m{l}", shape, dt))

        xp = sb("xp", [P, NT, FD])
        hn = sb("hn", [P, NT, C])
        stats = sb("stats", [P, NT, 6])
        mv = sb("mv", [P, NT, 2])
        va = sb("va", [P, NT])
        sd = sb("sd", [P, NT])
        rs = sb("rs", [P, NT])
        hT = sb("hTm", [P, NT * P])
        gg = sb("gg", [P, 3, W])
        hid = sb("hid", [P, 3, W])
        xf, res, flags, ident, shift, edge = (F[k] for k in ("xf", "res", "flags", "ident", "shift", "edge"))
        w1, w2, b1, b2, lg, lb = (F[k] for k in ("w1", "w2", "b1", "b2", "lg", "lb"))
        block = ctx.enter_context(nc.Block())
        last = l == DEPTH - 1

        @block.vector
        def _(dve):
            for m in range(NC4):
                s = slice(4 * m, 4 * m + 4)
                dve.tensor_tensor(xp[:, s, :], xf[:, s, FD:C], flags[:, s].unsqueeze(2).to_broadcast([P, 4, FD]),
                                  ALU.mult).then_inc(S("xp"), 1)
            for m in range(NC4):
                s = slice(4 * m, 4 * m + 4)
                dve.tensor_copy(hn[:, s, 0:FD], xf[:, 4 * m + 1:4 * m + 5, 0:FD]).then_inc(S("lower"), 1)
                dve.wait_ge(S("shifted"), m + 1)
                dve.tensor_copy(hn[:, s, FD:C], ps[:, m, 0:4 * FD].rearrange("p (t d) -> p t d", t=4)).then_inc(S("upper"), 1)
            dve.wait_ge(S("lower"), NC4)
            for t in range(NT):
                dve.wait_ge(S("upper"), t // 4 + 1)
                dve.bn_stats(stats[:, t, :], hn[:, t, :]).then_inc(S("stats"), 1)
            for t in range(NT):
                dve.wait_ge(S("stats"), t + 1)
                dve.bn_aggr(mv[:, t, :], stats[:, t, :]).then_inc(S("aggr"), 1)
            dve.wait_ge(S("aggr"), NT)
            dve.tensor_scalar(va[:], mv[:, :, 1], 1e-5, None, ALU.add).then_inc(S("var"), 1)
            dve.wait_ge(S("std"), 1)
            dve.reciprocal(rs[:], sd[:]).then_inc(S("rstd"), 1)
            dve.wait_ge(S("rstd"), 1)
            for t in range(NT):
                dve.tensor_scalar(hn[:, t, :], hn[:, t, :], mv[:, t, 0:1], rs[:, t:t + 1], ALU.subtract, ALU.mult).then_inc(S("normed"), 1)
            for m in range(NC4):
                s = slice(4 * m + 1, 4 * m + 5)
                dve.tensor_tensor(xf[:, s, :], xf[:, s, :], b2[:, l:l + 1, :].to_broadcast([P, 4, C]), ALU.add).then_inc(S("biased"), 1)
            if last:
                for m in range(NC4):
                    s = slice(4 * m + 1, 4 * m + 5)
                    dve.wait_ge(S("biased"), m + 1)
                    dve.tensor_tensor(xf[:, s, :], xf[:, s, :], res[:, 4 * m:4 * m + 4, :], ALU.add).then_inc(S("biased"), 1)
            dve.wait_ge(S("biased"), NC4 * (1 + last))
            with dve.Fori(0, NC4) as m:
                for c, (o, w) in enumerate(HCH):
                    dve.wait_ge(S("a_filled"), 3 * m + c + 1)
                    dve.wait_ge(S("gelu"), CREDIT + 3 * m + c + 1)
                    dve.scalar_tensor_tensor(out=hid[0:w, c, :], in0=ps[0:w, 3 + c, :], scalar=b1[0:w, l, c:c + 1],
                                             in1=gg[0:w, c, :], op0=ALU.add, op1=ALU.mult).then_inc(S("hidden"), 1)
                dve.wait_ge(S("out_filled"), m + 1)
                rows = xf[:, bass.ds(4 * m + 1, 4), :]
                dve.tensor_tensor(rows, ps[:, 7, :].rearrange("p (t c) -> p t c", t=4), rows, ALU.add).then_inc(S("out_done"), 1)

        @block.scalar
        def _(act):
            act.wait_ge(S("var"), 1)
            act.activation(sd[:], va[:], ACT.Sqrt).then_inc(S("std"), 1)

            for g in range(NC4):
                act.wait_ge(S("turned"), g + 1)
                act.activation(hT[:, W * g:W * (g + 1)], ps[:, g, :], ACT.Identity, scale=lg[:, l:l + 1],
                               bias=lb[:, l:l + 1]).then_inc(S("hT"), 1)
            with act.Fori(0, NC4) as m:
                act.wait_ge(S("hidden"), CREDIT + 3 * m)
                for c, (o, w) in enumerate(HCH):
                    act.wait_ge(S("g_filled"), 3 * m + c + 1)
                    act.activation(gg[0:w, c, :], ps[0:w, c, :], ACT.Gelu, bias=b1[0:w, l, 3 + c:4 + c]).then_inc(S("gelu"), 1)

        @block.tensor
        def _(pe):
            for m in range(NC4):
                pe.wait_ge(S("xp"), m + 1)
                o = ps[:, m, 0:4 * FD].rearrange("p (t d) -> p t d", t=4)
                pe.matmul(o, shift[:], xf[:, 4 * m + 1:4 * m + 5, FD:C], start=True, stop=False)
                pe.matmul(o, edge[:], xp[:, 4 * m:4 * m + 4, :], start=False, stop=True).then_inc(S("shifted"), 1)
            pe.wait_ge(S("upper"), NC4)
            for t in range(NT):
                pe.wait_ge(S("normed"), t + 1)
                mm = pe.transpose(ps[:, t // 4, P * (t % 4):P * (t % 4 + 1)], hn[:, t, :], ident[:])
                if t % 4 == 3:
                    mm.then_inc(S("turned"), 1)
            pe.wait_ge(S("hT"), NC4)
            with pe.Fori(0, NC4) as m:
                h = hT[:, bass.ds(W * m, W)]
                pe.wait_ge(S("gelu"), CREDIT + 3 * m)
                for c, (o, w) in enumerate(HCH):
                    pe.matmul(ps[0:w, c, :], w1[:, l, HID + o:HID + o + w], h, start=True, stop=True).then_inc(S("g_filled"), 1)
                pe.wait_ge(S("hidden"), CREDIT + 3 * m)
                for c, (o, w) in enumerate(HCH):
                    pe.matmul(ps[0:w, 3 + c, :], w1[:, l, o:o + w], h, start=True, stop=True).then_inc(S("a_filled"), 1)
                pe.wait_ge(S("out_done"), CREDIT + m)
                pe.wait_ge(S("hidden"), CREDIT + 3 * m + 3)
                for t in range(4):
                    for c, (o, w) in enumerate(HCH):
                        mm = pe.matmul(ps[:, 7, P * t:P * (t + 1)], hid[0:w, c, P * t:P * (t + 1)], w2[0:w, l, c, :],
                                       start=(c == 0), stop=(c == 2))
                mm.then_inc(S("out_filled"), 1)

        @block.sync
        def _(sp):
            for name in ("hidden", "gelu", "out_done"):
                sp.sem_inc(S(name), CREDIT)
            if last:
                o_v = out_ap.rearrange("b (t p) c -> p (b t) c", p=P)
                for m in range(NC4):
                    sp.wait_ge(S("out_done"), CREDIT + m + 1)
                    sp.dma_start(o_v[:, 4 * m:4 * m + 4, :], xf[:, 4 * m + 1:4 * m + 5, :]).then_inc(S("stored"), 16)
                sp.wait_ge(S("stored"), 16 * NC4)


def build(nc, ins, out):
    with ExitStack() as ctx:
        def sb(name, shape, dt=F32):
            return ctx.enter_context(nc.sbuf_tensor(name, shape, dt))

        ps = ctx.enter_context(nc.psum_tensor("ps", [P, 8, BANK], F32))
        res = sb("res", [P, NT, C])
        ident = sb("ident", [P, P])
        F = dict(res=res, ident=ident, shift=sb("shift", [P, P]), edge=sb("edge", [P, P]), near=sb("near", [P, P + WIN]),
                 flags=sb("flags", [P, NT]), starts=sb("starts", [P, NT]), wqkv=sb("wqkv", [P, DEPTH, 3 * INNER]),
                 wo=sb("wo", [P, DEPTH, 4, C]), w1=sb("w1", [P, DEPTH, 2 * HID]), w2=sb("w2", [HCH[0][1], DEPTH, 3, C]),
                 b1=sb("b1", [HCH[0][1], DEPTH, 6]), b2=sb("b2", [P, DEPTH, C]), lg=sb("lg", [P, DEPTH]),
                 lb=sb("lb", [P, DEPTH]))
        SA = Sems(nc, ctx, "att_")
        with ExitStack() as actx:
            def sba(name, shape, dt=F32):
                return actx.enter_context(nc.sbuf_tensor(name, shape, dt))
            K = dict(res=res, ident=ident, identb=sba("identb", [P, P], BF16), maskb=sba("maskb", [P, P], BF16),
                     maskf=sba("maskf", [P, P]), cosT=sba("cosT", [ROPE, T]), sinT=sba("sinT", [ROPE, T]),
                     yT=sba("yT", [P, B * T]), nqT=sba("nqT", [QL, B * T]), kcT=sba("kcT", [96, B * T]),
                     ones=sba("ones", [P, VD]), cN=sba("cN", [P, NT, KVL]), wvo=sba("wvo", [KVL, H // 4, 4, C]), selT=sba("selT", [P, B * KEEP]), gcol=sba("gcol", [96, B]),
                     kH1=[sba(f"kH1{b}", [99, T], F32R) for b in range(B)],
                     kL1=[sba(f"kL1{b}", [QK, T], F32R) for b in range(B)],
                     kHw=[sba(f"kHw{b}", [99, T], F32R) for b in range(B)],
                     kH2=[sba(f"kH2{b}", [99, KEEP], F32R) for b in range(B)])
            with ExitStack() as pctx:
                SP_ = Sems(nc, pctx, "prep_")
                prepare(nc, ins, K, ps, SP_)
                latent_attention(nc, ins, K, ps, SA, SP_, ffn_weights(ins, F))
        with ExitStack() as fctx:
            def sbf(name, shape, dt=F32):
                return fctx.enter_context(nc.sbuf_tensor(name, shape, dt))
            F.update(xf=sbf("xf", [P, NT + 1, C]), minus_half=sbf("minus_half", [P, 2 * FH]), tabs=sbf("tabs", [P, DEPTH, 4, NT, FD]),
                     sm=sbf("sm", [P, FH, 2 * P]), kT=[sbf(f"kT{n}", [P, 4, P]) for n in range(4)],
                     vN=[sbf(f"vN{n}", [P, INNER]) for n in range(4)])
            with ExitStack() as bctx:
                ffn_begin(nc, ins, F, ps, Sems(nc, bctx, "start_"), SA)
            SW, SM = Sems(nc, fctx, "win_"), Sems(nc, fctx, "mlp_")
            for l in range(DEPTH):
                window_attention(nc, F, ps, l, SW)
                gated_mlp(nc, F, ps, l, SM, out)
                if l < DEPTH - 1:
                    with nc.Block() as between:
                        @between.sync
                        def _(sp):
                            SW.clear(sp)
                            SM.clear(sp)


def _constants():
    f32 = np.float32
    f = (f32(1.0) / f32(10000.0) ** (np.arange(0, ROPE, 2, dtype=f32) / f32(ROPE))).astype(f32)
    a = np.outer(np.arange(T, dtype=f32), f).astype(f32)
    cos, sin = np.cos(a).astype(f32), np.sin(a).astype(f32)
    i, j = np.arange(P)[:, None], np.arange(P)[None, :]
    out = {
        "c_ident": np.eye(P, dtype=f32),
        "c_causal": np.where(j > i, f32(NEG), f32(0.0)).astype(f32),
        "c_cosT": np.ascontiguousarray(np.concatenate([cos, cos], 1).T),
        "c_sinT": np.ascontiguousarray(np.concatenate([sin, -sin], 1).T),
        "c_cosN": cos, "c_sinN": sin,
        "c_iota": np.tile(np.arange(KEEP, dtype=f32), (P, 1)),
    }
    half = np.arange(0, FD, 2, dtype=f32)
    inv = (f32(1.0) / f32(10000.0) ** (half / f32(FD))).astype(f32)
    ang = (np.arange(T, dtype=f32)[:, None] * inv[None, :]).astype(f32)
    base = ((half + f32(0.4 * FD)) / f32(1.4 * FD)).astype(f32)
    power = ((np.arange(T, dtype=f32) - T // 2) / f32(WIN // 2)).astype(f32)
    scale = (base[None, :] ** power[:, None]).astype(f32)
    both = lambda a: np.concatenate([a, a], 1)
    sgn = np.concatenate([-np.ones(FD // 2, f32), np.ones(FD // 2, f32)])[None, :]
    out["c_qcos"] = both(np.cos(ang) * scale * f32(8.0)).astype(f32)
    out["c_qsin"] = (both(np.sin(ang) * scale * f32(8.0)) * sgn).astype(f32)
    out["c_kcos"] = both(np.cos(ang) / scale).astype(f32)
    out["c_ksin"] = (both(np.sin(ang) / scale) * sgn).astype(f32)
    out["c_shift"] = np.eye(P, k=1, dtype=f32)
    edge = np.zeros((P, P), f32)
    edge[P - 1, 0] = 1.0
    out["c_edge"] = edge
    q, k = np.arange(P)[:, None], np.arange(P + WIN)[None, :] - WIN
    near = (q - k >= 0) & (q - k <= WIN)
    out["c_near"] = np.where(near, f32(0.0), f32(NEG)).astype(f32)
    out["c_starts"] = np.tile(np.where(np.arange(NT) % TB == 0, f32(NEG), f32(0.0)).astype(f32), (P, 1))
    out["c_flags"] = np.tile((np.arange(NT) % TB != 0).astype(f32), (P, 1))
    return out


_INS = ['L0_attn_x', 'L0_attn_w_cq', 'L0_attn_g_qnorm', 'L0_attn_w_dq_nope', 'L0_attn_w_dq_rope', 'L0_attn_w_ckv',
        'L0_attn_g_kvnorm', 'L0_attn_w_dk_nope', 'L0_attn_w_dv', 'L0_attn_w_krope', 'L0_attn_w_imp', 'L0_attn_w_selk',
        'L0_attn_w_selv', 'L0_attn_w_wink', 'L0_attn_w_winv', 'L0_attn_w_gate', 'L0_attn_w_proj', 'L0_ffn_wqkv',
        'L0_ffn_q_scale', 'L0_ffn_k_scale', 'L0_ffn_wo', 'L0_ffn_ln_g', 'L0_ffn_ln_b', 'L0_ffn_w1', 'L0_ffn_b1',
        'L0_ffn_w2', 'L0_ffn_b2']


def kernel(**inputs):
    import concourse.bacc as _bacc
    from concourse.bass_utils import run_bass_kernel_spmd as _run

    nc = _bacc.Bacc("TRN2", target_bir_lowering=False, num_devices=1)
    arrays, aps = {}, {}
    given = {n: np.ascontiguousarray(inputs[n]) for n in _INS}
    given.update(_constants())
    for name, a in given.items():
        arrays[f"in_{name}_dram"] = a
        aps[name] = nc.dram_tensor(f"in_{name}_dram", a.shape, mybir.dt.from_np(a.dtype), kind="ExternalInput").ap()
    out = nc.dram_tensor("out_0_dram", (B, T, C), F32, kind="ExternalOutput").ap()
    build(nc, aps, out)
    r = _run(nc, [arrays], core_ids=[0])
    return r.results[0]["out_0_dram"]
```

```python
from contextlib import ExitStack

import numpy as np

import concourse.bass as bass
from concourse import mybir
from concourse.alu_op_type import AluOpType as ALU

F32 = mybir.dt.float32
F32R = mybir.dt.float32r
BF16 = mybir.dt.bfloat16
ACT = mybir.ActivationFunctionType
AX = mybir.AxisListType

P = 128
B, T, C = 2, 1024, 128
NT = B * T // P
TB = T // P
H = 16
HEADS = H
NOPE, ROPE, VD = 32, 64, 32
QK = NOPE + ROPE
HALF = ROPE // 2
KEEP = 32
QL, KVL = 96, 32
NBR = 3
BANK = 512
NEG = -1.0e30

DEPTH, FH, FD, WIN = 2, 8, 64, 64
INNER = FH * FD
LOOPS = NT // 4 - 1
HID = int(C * 4 * 2 / 3)
HCH = [(0, 114), (114, 114), (228, 113)]


class Sems:

    def __init__(self, nc, ctx, stage):
        self.nc, self.ctx, self.stage, self.made = nc, ctx, stage, {}

    def __call__(self, name):
        if name not in self.made:
            self.made[name] = self.ctx.enter_context(self.nc.semaphore(self.stage + name))
        return self.made[name]

    def clear(self, eng):
        for made in self.made.values():
            eng.sem_clear(made)


def wait_past(eng, sem, value):
    if not (isinstance(value, int) and value <= 0):
        eng.wait_ge(sem, value)


def wait_apart(eng, S, sem, value):
    wait_past(eng, sem, value)
    eng.sem_inc(S(f"passed_{eng.engine.name}"), 1)


def prepare(nc, ins, K, ps, S):
    with ExitStack() as ctx:
        def sb(name, shape, dt=F32):
            return ctx.enter_context(nc.sbuf_tensor(name, shape, dt))

        stats = sb("stats", [P, NT, 6])
        mv = sb("mv", [P, NT, 2])
        rstd = sb("rstd", [P, NT])
        std = sb("std", [P, NT])
        y = sb("y", [P, NT, C])
        wc = sb("wc", [P, QL + KVL + ROPE])
        wimp = sb("wimp", [P, 1])
        wgate = sb("wgate", [P, 3])
        gq = sb("gq", [QL, 1])
        gqs = sb("gqs", [QL, 1])
        gkv = sb("gkv", [96, 1])
        gkv0 = sb("gkv0", [KVL, 1])
        wdv = sb("wdv", [KVL, H * VD])
        wpr = sb("wpr", [P, H // 4, C])
        wdvT = sb("wdvT", [P, H // 4, KVL])
        cosn = sb("cosn", [P, TB, HALF])
        sinn = sb("sinn", [P, TB, HALF])
        iota = sb("iota", [P, KEEP])
        onehot3 = sb("onehot3", [99, 3])
        z = sb("z", [P, NT, QL + KVL + ROPE])
        ssq = sb("ssq", [P, 2, NT])
        sroot = sb("sroot", [P, 2, NT])
        srec = sb("srec", [P, 2, NT])
        sqj = sb("sqj", [P, QL])
        zq = sb("zq", [P, NT, QL])
        zk = sb("zk", [P, NT, ROPE + KVL])
        ra = sb("ra", [P, TB, HALF])
        rb = sb("rb", [P, TB, HALF])
        sc = sb("sc", [33, T])
        scw = sb("scw", [33, 2, T])
        top = sb("top", [33, 4, 8])
        selm = sb("selm", [33, T])
        rank = sb("rank", [33, T])
        one1 = sb("one1", [33, 1])
        rkn = sb("rkn", [P, NT])
        hot = sb("hot", [P, NT, KEEP])
        ysum = sb("ysum", [P, 4])
        gl = sb("gl", [96, B, 3])
        gm = sb("gm", [96, B])
        ge = sb("ge", [96, B, 3])
        gs = sb("gs", [96, B])
        gr = sb("gr", [96, B])

        block = ctx.enter_context(nc.Block())
        res, yT, nqT, kcT = K["res"], K["yT"], K["nqT"], K["kcT"]

        x_v = ins["L0_attn_x"].rearrange("b (t p) c -> p (b t) c", p=P)
        consts = [
            (K["maskf"][:], ins["c_causal"]),
            (K["cosT"][:], ins["c_cosT"]), (K["sinT"][:], ins["c_sinT"]),
            (cosn[:], ins["c_cosN"].rearrange("(t p) d -> p t d", p=P)),
            (sinn[:], ins["c_sinN"].rearrange("(t p) d -> p t d", p=P)),
            (iota[:], ins["c_iota"]), (onehot3[96:99, :], ins["c_ident"][0:3, 0:3]),
            (wc[:, 0:QL], ins["L0_attn_w_cq"]), (wc[:, QL:QL + KVL], ins["L0_attn_w_ckv"]),
            (wc[:, QL + KVL:], ins["L0_attn_w_krope"]),
            (wimp[:], ins["L0_attn_w_imp"]), (wgate[:], ins["L0_attn_w_gate"]),
            (gq[:], ins["L0_attn_g_qnorm"].rearrange("(a o) -> a o", o=1)),
            (gkv[64:96, :], ins["L0_attn_g_kvnorm"].rearrange("(a o) -> a o", o=1)),
            (gkv0[:], ins["L0_attn_g_kvnorm"].rearrange("(a o) -> a o", o=1)),
            (wdv[:], ins["L0_attn_w_dv"]), (wpr[:], ins["L0_attn_w_proj"].rearrange("(g p) c -> p g c", p=P)),
        ]

        @block.sync
        def _(sp):
            sp.dma_start(K["ident"][:], ins["c_ident"]).then_inc(S("ident_loaded"), 16)
            for c in range(4):
                sp.dma_start(res[:, 4 * c:4 * c + 4, :], x_v[:, 4 * c:4 * c + 4, :]).then_inc(S(f"x_loaded{c}"), 16)
            for dst, src in consts:
                sp.dma_start(dst, src).then_inc(S("consts_loaded"), 16)

        ALLC = 16 * len(consts)

        @block.vector
        def _(dve):
            def normalise(c):
                dve.wait_ge(S("ln_rstd"), c + 1)
                for t in range(4 * c, 4 * c + 4):
                    dve.tensor_scalar(y[:, t, :], res[:, t, :], mv[:, t, 0:1], rstd[:, t:t + 1],
                                      ALU.subtract, ALU.mult).then_inc(S("y_ready"), 1)

            for c in range(4):
                dve.wait_ge(S(f"x_loaded{c}"), 16)
                for t in range(4 * c, 4 * c + 4):
                    dve.bn_stats(stats[:, t, :], res[:, t, :]).then_inc(S("ln_stats"), 1)
                for t in range(4 * c, 4 * c + 4):
                    dve.wait_ge(S("ln_stats"), t + 1)
                    dve.bn_aggr(mv[:, t, :], stats[:, t, :]).then_inc(S("ln_aggr"), 1)
                dve.wait_ge(S("ln_aggr"), 4 * c + 4)
                dve.tensor_scalar(std[:, 4 * c:4 * c + 4], mv[:, 4 * c:4 * c + 4, 1], 1e-5, None, ALU.add).then_inc(S("ln_var"), 1)
                if c:
                    normalise(c - 1)
            normalise(3)
            dve.wait_ge(S("consts_loaded"), ALLC)
            dve.tensor_scalar(gqs[:], gq[:], float(QK) ** -0.5, None, ALU.mult).then_inc(S("gqs"), 1)
            for t in range(NT):
                dve.wait_ge(S("lat_full"), t + 1)
                dve.tensor_copy(z[:, t, :], ps[:, 4 + t % 2, 0:QL + KVL + ROPE]).then_inc(S("lat_copied"), 1)
            for b in range(B):
                for c in range(2):
                    i = 2 * b + c
                    dve.wait_ge(S("imp_full"), i + 1)
                    if i == 0:
                        dve.wait_ge(S("sc_zero"), 1)
                    dve.tensor_copy(sc[32 * b:32 * b + 1, BANK * c:BANK * (c + 1)],
                                    ps[32 * b:32 * b + 1, 6 + c, :]).then_inc(S("imp_copied"), 1)
            dve.wait_ge(S("squares"), 2 * NT)
            dve.tensor_scalar(sroot[:, 0, :], ssq[:, 0, :], 1.0 / QL, 1e-6, ALU.mult, ALU.add).then_inc(S("msq"), 1)
            dve.tensor_scalar(sroot[:, 1, :], ssq[:, 1, :], 1.0 / KVL, 1e-6, ALU.mult, ALU.add).then_inc(S("msq"), 1)
            dve.wait_ge(S("rrms"), 1)
            dve.wait_ge(S("lat_copied"), NT)
            dve.tensor_tensor(zq[:], z[:, :, 0:QL], srec[:, 0, :].unsqueeze(2).to_broadcast([P, NT, QL]),
                              ALU.mult).then_inc(S("zq"), 1)
            dve.wait_ge(S("rrms"), 2)
            dve.tensor_tensor(zk[:, :, ROPE:], z[:, :, QL:QL + KVL],
                              srec[:, 1, :].unsqueeze(2).to_broadcast([P, NT, KVL]), ALU.mult).then_inc(S("zk"), 1)
            dve.wait_ge(S("imp_copied"), 4)
            cur = sc[:]
            for r in range(4):
                if r:
                    dve.wait_ge(S("top_round"), r)
                dve.max(top[:, r, :], cur).then_inc(S("top_found"), 1)
                dve.wait_ge(S("top_found"), r + 1)
                dve.match_replace(scw[:, r % 2, :], top[:, r, :], cur, -3.0e38).then_inc(S("top_round"), 1)
                cur = scw[:, r % 2, :]
            dve.wait_ge(S("top_round"), 4)
            dve.tensor_tensor(selm[:], cur, sc[:], ALU.not_equal).then_inc(S("selm"), 1)
            dve.wait_ge(S("selm"), 1)
            dve.wait_ge(S("misc_const"), 1)
            dve.tensor_tensor_scan(rank[:], K["ones"][0:33, 0:1].to_broadcast([33, T]), selm[:], 0.0,
                                   ALU.mult, ALU.add).then_inc(S("rank0"), 1)
            dve.wait_ge(S("rank0"), 1)
            dve.tensor_tensor(selm[:], rank[:], selm[:], ALU.mult).then_inc(S("rank1"), 1)
            dve.wait_ge(S("rank1"), 1)
            dve.tensor_scalar(rank[:], selm[:], -1.0, None, ALU.add).then_inc(S("rank2"), 1)
            dve.wait_ge(S("rankn_full"), 1)
            for b in range(B):
                tt = slice(TB * b, TB * (b + 1))
                dve.tensor_copy(rkn[:, tt], ps[:, 6 - 2 * b, tt]).then_inc(S("rankn"), 1)
            dve.wait_ge(S("rankn"), 2)
            for t in range(NT):
                dve.tensor_scalar(hot[:, t, :], iota[:], rkn[:, t:t + 1], None, ALU.is_equal).then_inc(S("hot"), 1)
            dve.wait_ge(S("sel_full"), 1)
            dve.tensor_copy(K["selT"][:], ps[:, 7, 0:B * KEEP]).then_inc(S("selT"), 1)
            dve.wait_ge(S("gate_full"), 1)
            dve.tensor_scalar(gl[:], ps[0:96, 5, 0:B * 3].rearrange("p (b g) -> p b g", b=B), 1.0 / T, None,
                              ALU.mult).then_inc(S("gl"), 1)
            dve.wait_ge(S("gl"), 1)
            dve.tensor_reduce(gm[:], gl[:], AX.X, ALU.max).then_inc(S("gm"), 1)
            dve.wait_ge(S("gm"), 1)
            dve.tensor_tensor(ge[:], gl[:], gm[:].unsqueeze(2).to_broadcast([96, B, 3]), ALU.subtract).then_inc(S("gd"), 1)
            dve.wait_ge(S("gexp"), 1)
            dve.tensor_reduce(gs[:], gl[:], AX.X, ALU.add).then_inc(S("gs"), 1)
            dve.wait_ge(S("gs"), 1)
            dve.reciprocal(gr[:], gs[:]).then_inc(S("gr"), 1)
            dve.wait_ge(S("gr"), 1)
            for n, g in enumerate((0, 2, 1)):
                rows = slice(32 * n, 32 * n + 32)
                dve.tensor_tensor(K["gcol"][rows, :], gl[rows, :, g], gr[rows, :], ALU.mult).then_inc(S("gcol"), 1)
            for i in range(4):
                b, c = i // 2, i % 2
                cols = slice(BANK * c, BANK * (c + 1))
                dve.wait_ge(S("krH"), i + 1)
                dve.tensor_tensor(K["kL1"][b][0:ROPE, cols], ps[0:ROPE, i, :], K["kH1"][b][0:ROPE, cols].bitcast(F32),
                                  ALU.subtract).then_inc(S("krL"), 1)

        @block.gpsimd
        def _(pool):
            pool.memset(K["minus_half"][:], -0.5).then_inc(S("half"), 1)
            pool.wait_ge(S("half"), 1)
            for c in range(4):
                pool.wait_ge(S("ln_var"), c + 1)
                pool.tensor_tensor(rstd[:, 4 * c:4 * c + 4], std[:, 4 * c:4 * c + 4], K["minus_half"][:, 0:4],
                                   ALU.pow).then_inc(S("ln_rstd"), 1)
            pool.memset(sc[:], 0.0).then_inc(S("sc_zero"), 1)
            pool.memset(one1[:], 1.0).then_inc(S("one1"), 1)
            pool.memset(K["ones"][:], 1.0).then_inc(S("misc_const"), 1)
            pool.wait_ge(S("consts_loaded"), ALLC)
            pool.wait_ge(S("ident_loaded"), 16)
            pool.tensor_copy(K["identb"][:], K["ident"][:]).then_inc(S("misc_const"), 1)
            pool.tensor_copy(K["maskb"][:], K["maskf"][:]).then_inc(S("misc_const"), 1)
            for n in range(2):
                pool.wait_ge(S("msq"), n + 1)
                pool.tensor_tensor(srec[:, n, :], sroot[:, n, :], K["minus_half"][:, 0:NT], ALU.pow).then_inc(S("rrms"), 1)
            pool.wait_ge(S("lat_copied"), NT)
            pool.wait_ge(S("rrms"), 2)
            pool.tensor_tensor(K["cN"][:], z[:, :, QL:QL + KVL],
                              srec[:, 1, :].unsqueeze(2).to_broadcast([P, NT, KVL]), ALU.mult).then_inc(S("cN"), 1)
            kr = QL + KVL
            n = 0
            for b in range(B):
                tt = slice(TB * b, TB * (b + 1))
                x1, x2 = z[:, tt, kr:kr + HALF], z[:, tt, kr + HALF:kr + ROPE]
                for o, (u, v, op) in enumerate([(x1, x2, ALU.subtract), (x2, x1, ALU.add)]):
                    if n:
                        pool.wait_ge(S("kr_rot"), n)
                    pool.tensor_tensor(ra[:], u, cosn[:], ALU.mult).then_inc(S("kr_terms"), 1)
                    pool.tensor_tensor(rb[:], v, sinn[:], ALU.mult).then_inc(S("kr_terms"), 1)
                    n += 1
                    pool.wait_ge(S("kr_terms"), 2 * n)
                    pool.tensor_tensor(zk[:, tt, HALF * o:HALF * (o + 1)], ra[:], rb[:], op).then_inc(S("kr_rot"), 1)

        @block.scalar
        def _(act):
            for g in range(4):
                act.wait_ge(S("yT_full"), g + 1)
                act.activation(yT[:, BANK * g:BANK * (g + 1)], ps[:, g, :], ACT.Copy,
                               accum_out=ysum[:, g:g + 1]).then_inc(S("yT"), 1)
            for t in range(NT):
                act.wait_ge(S("lat_copied"), t + 1)
                for n, (o, w) in enumerate(((0, QL), (QL, KVL))):
                    if 2 * t + n:
                        act.wait_ge(S("squares"), 2 * t + n)
                    act.activation(sqj[:, 0:w], z[:, t, o:o + w], ACT.Square,
                                   accum_out=ssq[:, n, t:t + 1]).then_inc(S("squares"), 1)
            act.wait_ge(S("wdvT_full"), 1)
            act.activation(wdvT[:].rearrange("p g d -> p (g d)"), ps[:, 0, 0:H // 4 * KVL], ACT.Copy).then_inc(S("wdvT"), 1)
            for r in range(4):
                act.wait_ge(S("wvo_full"), r + 1)
                act.activation(K["wvo"][:, :, r, :], ps[0:KVL, r, :].rearrange("p (g c) -> p g c", c=C), ACT.Copy,
                               scale=gkv0[:]).then_inc(S("wvo"), 1)
            act.wait_ge(S("gqs"), 1)
            for g in range(4):
                act.wait_ge(S("nq_full"), g + 1)
                act.activation(nqT[:, BANK * g:BANK * (g + 1)], ps[0:QL, g, :], ACT.Copy, scale=gqs[:]).then_inc(S("nqT"), 1)
            for i in range(4):
                b, c = i // 2, i % 2
                act.wait_ge(S("kc_full"), i + 1)
                act.activation(kcT[64:96, BANK * i:BANK * (i + 1)], ps[64:96, i, :], ACT.Copy, scale=gkv[64:96, :]).then_inc(S("kcT"), 1)
                act.activation(K["kH1"][b][0:ROPE, BANK * c:BANK * (c + 1)], ps[0:ROPE, i, :], ACT.Copy).then_inc(S("krH"), 1)
            act.wait_ge(S("consts_loaded"), ALLC)
            for b in range(B):
                for n, k in enumerate(("kH1", "kHw", "kH2")):
                    w = KEEP if k == "kH2" else T
                    act.activation(K[k][b][96:99, :], onehot3[96:99, n:n + 1].to_broadcast([3, w]), ACT.Copy).then_inc(S("aug"), 1)
            act.wait_ge(S("gd"), 1)
            act.activation(gl[:], ge[:], ACT.Exp).then_inc(S("gexp"), 1)

        @block.tensor
        def _(pe):
            ident = K["ident"]
            pe.wait_ge(S("ident_loaded"), 16)
            for t in range(NT):
                pe.wait_ge(S("y_ready"), t + 1)
                mm = pe.transpose(ps[:, t // 4, P * (t % 4):P * (t % 4 + 1)], y[:, t, :], ident[:])
                if t % 4 == 3:
                    mm.then_inc(S("yT_full"), 1)
            pe.wait_ge(S("consts_loaded"), ALLC)
            for t in range(NT):
                if t % 4 == 0:
                    pe.wait_ge(S("yT"), t // 4 + 1)
                if t >= 2:
                    pe.wait_ge(S("lat_copied"), t - 1)
                pe.matmul(ps[:, 4 + t % 2, 0:QL + KVL + ROPE], yT[:, P * t:P * (t + 1)], wc[:],
                          start=True, stop=True).then_inc(S("lat_full"), 1)
            for i in range(4):
                b, c = i // 2, i % 2
                if b:
                    pe.wait_ge(S("imp_copied"), i - 1)
                pe.matmul(ps[32 * b:32 * b + 1, 6 + c, :], wimp[:], yT[:, BANK * i:BANK * (i + 1)],
                          start=True, stop=True).then_inc(S("imp_full"), 1)
            for g in range(H // 4):
                mm = pe.transpose(ps[:, 0, KVL * g:KVL * (g + 1)], wdv[:, P * g:P * (g + 1)], ident[0:KVL, 0:KVL])
            mm.then_inc(S("wdvT_full"), 1)
            pe.wait_ge(S("wdvT"), 1)
            for r in range(4):
                rows = slice(32 * r, 32 * r + 32)
                for g in range(H // 4):
                    mm = pe.matmul(ps[0:KVL, r, C * g:C * (g + 1)], wdvT[rows, g, :], wpr[rows, g, :], start=True, stop=True)
                mm.then_inc(S("wvo_full"), 1)
            pe.wait_ge(S("yT"), 4)
            pe.wait_ge(S("lat_copied"), NT)
            for g in range(4):
                b = g // 2
                mm = pe.matmul(ps[0:96, 5, 3 * b:3 * b + 3], ysum[:, g:g + 1].to_broadcast([P, 96]), wgate[:],
                               start=(g % 2 == 0), stop=(g % 2 == 1))
            mm.then_inc(S("gate_full"), 1)
            pe.wait_ge(S("zq"), 1)
            pe.wait_ge(S("wvo"), 4)
            for t in range(NT):
                mm = pe.transpose(ps[0:QL, t // 4, P * (t % 4):P * (t % 4 + 1)], zq[:, t, :], ident[:])
                if t % 4 == 3:
                    mm.then_inc(S("nq_full"), 1)
            pe.wait_ge(S("zk"), 1)
            pe.wait_ge(S("kr_rot"), 2 * B)
            for t in range(NT):
                if t % 4 == 0:
                    pe.wait_ge(S("nqT"), t // 4 + 1)
                mm = pe.transpose(ps[0:96, t // 4, P * (t % 4):P * (t % 4 + 1)], zk[:, t, :], ident[:])
                if t % 4 == 3:
                    mm.then_inc(S("kc_full"), 1)
            pe.wait_ge(S("rank2"), 1)
            pe.wait_ge(S("one1"), 1)
            for t in range(NT):
                b, r = t // TB, 32 * (t // TB)
                mm = pe.matmul(ps[:, 6 - 2 * b, t:t + 1], rank[r:r + 1, P * (t % TB):P * (t % TB + 1)], one1[r:r + 1, :],
                               start=True, stop=True)
            mm.then_inc(S("rankn_full"), 1)
            for t in range(NT):
                b = t // TB
                pe.wait_ge(S("hot"), t + 1)
                mm = pe.matmul(ps[:, 7, KEEP * b:KEEP * (b + 1)], y[:, t, :], hot[:, t, :],
                               start=(t % TB == 0), stop=(t % TB == TB - 1))
            mm.then_inc(S("sel_full"), 1)


class Ring:

    def __init__(self, items):
        self.place = {kind: {n: i for i, n in enumerate(of)} for kind, of in items.items()}
        self.uses = {kind: [len(of[k::RING]) for k in range(RING)] for kind, of in items.items()}
        self.before, total = {}, [0] * RING
        for kind, of in self.uses.items():
            self.before[kind] = total
            total = [t + n * (2 * HEADS - 2 if kind == "loop" else 1) for t, n in zip(total, of)]

    def at(self, kind, slot, item):
        i = self.place[kind][item]
        k = i % RING
        within = self.before[kind][k] + i // RING
        return k, (within + self.uses[kind][k] * (slot - 1) if kind == "loop" else within)


LATE = {"invert", "norm", "wp"}
RING = 6
NPR = 3
CREDIT = 1
PROJECTIONS = {"q", "k", "n", "v", "k2"}
COMING = {"q", "qh", "k", "kh", "n", "v", "k2", "mt"}


def score_tiles():
    pairs = [((0, 1), 4 * c + j, c) for c in range(2) for j in range(2)]
    return pairs + [((a,), j, c) for a in (0, 1) for j in range(TB) for c in range(1 + (j >= 4))
                    if ((0, 1), j, c) not in pairs]


def timeline():
    return [
        ('q',), ('k',), ('invert',), ('norm',), ('v',), ('qh',), ('S', 0), ('a2s',), ('S', 1), ('n',), ('k2',),
        ('W', 0), ('mx', (0,), 6, 1), ('mx', (0,), 3, 0), ('W', 1), ('mx', (0,), 6, 0), ('mx2',), ('mx', (0,), 4, 0),
        ('mx', (0,), 5, 0), ('kh',), ('S', 2), ('mx', (1,), 6, 0), ('mx', (1,), 5, 0), ('mx', (0, 1), 5, 1),
        ('mx', (1,), 2, 0), ('S', 3), ('mx', (0, 1), 4, 1), ('mx', (1,), 7, 0), ('mx', (0,), 7, 0),
        ('mx', (0, 1), 1, 0), ('a2o',), ('W', 2), ('mx', (1,), 6, 1), ('mx', (0,), 7, 1), ('mx', (1,), 4, 0),
        ('mx', (1,), 7, 1), ('W', 3), ('S', 4), ('S', 5), ('mx', (0,), 2, 0), ('mx', (1,), 3, 0), ('mx', (0, 1), 0, 0),
        ('S', 6), ('W', 4), ('mt',), ('S', 7), ('W', 5), ('W', 6), ('W', 7), ('wp',),
    ]


def is_coming(step):
    return step[0] in COMING or step[0] in ("mx", "mx2")


def pieces(i):
    return [(c, max(P * i, BANK * c), BANK * (c + 1)) for c in range(2) if P * i < BANK * (c + 1)]


def items_of(steps):
    out = []
    for s in steps:
        if s[0] in ("q", "k", "n", "a2o", "wp"):
            out += [(s[0], 0), (s[0], 1)]
        elif s[0] in ("v", "k2", "mx", "mx2", "mt"):
            out.append(s)
        elif s[0] == "S":
            out += [("S", a, s[1], c) for a in (0, 1) for c, _, _ in pieces(s[1])]
        elif s[0] == "a2s":
            out += [("a2s", 0), ("a2s", 1)]
    return out


def latent_attention(nc, ins, K, ps, S, before, later):
    steps = timeline()
    which = {"first": [s for s in steps if is_coming(s)], "second": [s for s in steps if s[0] not in LATE],
             "loop": steps, "last": [s for s in steps if not is_coming(s)], "end": [s for s in steps if s[0] in LATE]}
    ring = Ring({kind: items_of(of) for kind, of in which.items()})

    with ExitStack() as ctx:
        def sb(name, shape, dt=F32):
            return ctx.enter_context(nc.sbuf_tensor(name, shape, dt))

        wq = sb("wq", [QL, QK])
        wk = sb("wk", [P, QK])
        wks = sb("wks", [P, QK])
        wdk = sb("wdk", [96, NOPE])
        wvw = sb("wvw", [P, VD])
        wvs = sb("wvs", [P, VD])
        wp = sb("wp", [96, C])
        wpg = [sb(f"wpg{b}", [96, C]) for b in range(B)]
        qf = sb("qf", [QK, T])
        qt = sb("qt", [ROPE, T])
        kf = sb("kf", [QK, T])
        kt = sb("kt", [ROPE, T])
        k2f = sb("k2f", [QK, KEEP])
        k2t = sb("k2t", [ROPE, KEEP])
        qH = [sb(f"qH{b}", [99, T], F32R) for b in range(B)]
        qL_ = [sb(f"qL{b}", [QK, T], F32R) for b in range(B)]
        kH = [K["kH1"], K["kHw"], K["kH2"]]
        kL = [K["kL1"], [sb(f"kLw{b}", [QK, T], F32R) for b in range(B)], [sb(f"kL2{b}", [QK, KEEP], F32R) for b in range(B)]]
        V = [sb(f"V{b}", [P, TB, VD]) for b in range(B)]
        V2 = [sb(f"V2{b}", [KEEP, 2 * VD]) for b in range(B)]
        mpart = sb("mpart", [P, 2, 4])
        mneg = sb("mneg", [P, NBR, TB])
        mT = sb("mT", [NBR * TB, P], F32R)
        pr = [[sb(f"pr{a}{n}", [P, T]) for n in range(NPR)] for a in range(2)]
        p2 = sb("p2", [KEEP, T])
        lnD = sb("lnD", [96, T])
        rD = sb("rD", [96, T])
        tO = [sb(f"tO{b}", [96, T]) for b in range(B)]
        cN, wvo = K["cN"], K["wvo"].rearrange("p g r c -> p (g r) c")
        res, yT, nqT, kcT, ones = K["res"], K["yT"], K["nqT"], K["kcT"], K["ones"]
        cosT, sinT, ident, selT = K["cosT"], K["sinT"], K["ident"], K["selT"]

        out_ps = ps[:, RING:RING + 2, :].rearrange("p a n -> p (a n)")

        def bank(k):
            return ps[:, k, :]

        block = ctx.enter_context(nc.Block())
        full = [S(f"bank{k}_filled") for k in range(RING)]
        free = [S(f"bank{k}_read") for k in range(RING)]

        w_q_nope, w_q_rope = ins["L0_attn_w_dq_nope"], ins["L0_attn_w_dq_rope"]
        w_wink, w_selk = ins["L0_attn_w_wink"], ins["L0_attn_w_selk"]

        def per_head(ap, width):
            return ap.rearrange("k (h d) -> h k d", d=width)

        def head_loads(h):
            nope, rope = slice(ROPE, QK), slice(0, ROPE)
            return [
                (wq[:, rope], per_head(w_q_rope, ROPE)[h]), (wq[:, nope], per_head(w_q_nope, NOPE)[h]),
                (wk[:, nope], per_head(w_wink, QK)[h, :, 0:NOPE]), (wk[:, rope], per_head(w_wink, QK)[h, :, NOPE:QK]),
                (wks[:, nope], per_head(w_selk, QK)[h, :, 0:NOPE]), (wks[:, rope], per_head(w_selk, QK)[h, :, NOPE:QK]),
                (wdk[64:96, :], per_head(ins["L0_attn_w_dk_nope"], NOPE)[h]),
                (wvw[:], per_head(ins["L0_attn_w_winv"], VD)[h]), (wvs[:], per_head(ins["L0_attn_w_selv"], VD)[h]),
            ]

        NLOAD = 16 * 9
        wproj = ins["L0_attn_w_proj"].rearrange("(h d) c -> h d c", d=VD)

        def output_weights(h):
            return [(wp[0:KVL, :], wvo[:, bass.ds(h, 1), :].rearrange("p a c -> p (a c)")),
                    (wp[32:64, :], wproj[h]), (wp[64:96, :], wproj[h])]

        def run_slots(eng, slot):
            slot("first", -1, -1, 1)
            slot("second", 0, 0, 0)
            with eng.Fori(0, HEADS - 2) as h:
                slot("loop", 2 * h + 1, h, 1)
                slot("loop", 2 * h + 2, h + 1, 0)
            slot("loop", 2 * HEADS - 3, HEADS - 2, 1)
            slot("loop", 2 * HEADS - 2, HEADS - 1, 0)
            slot("last", 2 * HEADS - 1, HEADS - 1, 1)
            slot("end", 2 * HEADS, HEADS, 0)

        @block.sync
        def _(sp):
            for name in ("weighted", "out_read"):
                sp.sem_inc(S(name), CREDIT)
            for dst, src in head_loads(0):
                sp.dma_start(dst, src).then_inc(S("head_loaded"), 16)
            for dst, src in output_weights(0):
                sp.dma_start(dst, src).then_inc(S("wp_loaded"), 16)
            for dst, src in later:
                sp.dma_start(dst, src).then_inc(S("later_loaded"), 16)
            before.clear(sp)

            def slot(kind, s, h, b):
                u, ub = s + 1, 1 - b
                if kind == "loop" and b == 1:
                    sp.wait_ge(S("wpg_done"), 2 * h + 2)
                    for dst, src in output_weights(h + 1):
                        sp.dma_start(dst, src).then_inc(S("wp_loaded"), 16)
                if kind in ("second", "loop") and b == 0 and not (isinstance(h, int) and h == HEADS - 1):
                    k, n = ring.at(kind, s, ("k2",))
                    sp.wait_ge(full[k], n + 1)
                    for dst, src in head_loads(h + 1):
                        sp.dma_start(dst, src).then_inc(S("head_loaded"), 16)
                if kind in ("first", "second", "loop"):
                    k, n = ring.at(kind, s, ("mt",))
                    sp.wait_ge(free[k], n + 1)
                    for n in range(NBR):
                        sp.dma_start(qH[ub][96 + n:97 + n, :].bitcast(F32).rearrange("a (j p) -> a j p", p=P),
                                     mT[TB * n:TB * (n + 1), :].bitcast(F32)).then_inc(S(f"maxrows{ub}"), 16)

            run_slots(sp, slot)
            if later:
                sp.wait_ge(S("later_loaded"), 16 * len(later))

        @block.tensor
        def _(pe):
            def slot(kind, s, h, b):
                u, ub = s + 1, 1 - b
                hu = h + 1 if b == 1 else h

                def take(item):
                    k, n = ring.at(kind, s, item)
                    wait_past(pe, free[k], n)
                    return k

                def scores(a, i):
                    ks = slice(P * i, P * (i + 1))
                    for c, lo, hi in pieces(i):
                        k = take(("S", a, i, c))
                        o = bank(k)[:, lo - BANK * c:hi - BANK * c]
                        pe.matmul(o, kH[a][b][0:QK, ks], qL_[b][:, lo:hi], start=True, stop=False)
                        pe.matmul(o, kL[a][b][:, ks], qH[b][0:QK, lo:hi], start=False, stop=False)
                        pe.matmul(o, kH[a][b][0:99, ks], qH[b][0:99, lo:hi], start=False, stop=True).then_inc(full[k], 1)

                def weighted(i):
                    k, n = ring.at(kind, s, ("S", 1, i, 1))
                    pe.wait_ge(free[k], n + 1)
                    pe.wait_ge(S("probs"), 2 * (TB * s + i + 1))
                    if i == 0:
                        pe.wait_ge(S("out_read"), CREDIT + s)
                    for c, lo, hi in pieces(i):
                        stop = (i == TB - 1) or (i == 3 and hi == BANK)
                        for g, (a, lhsT) in enumerate(((0, cN[:, TB * b + i, :]), (1, V[b][:, i, :]),
                                                       (0, ones[:]), (1, ones[:]))):
                            mm = pe.matmul(out_ps[32 * g:32 * g + 32, lo:hi], lhsT, pr[a][i % NPR][:, lo:hi],
                                           start=(i == 0), stop=stop)
                    mm.then_inc(S("weighted"), 1)

                for step in which[kind]:
                    op = step[0]
                    if step == next(x for x in steps if x[0] in PROJECTIONS):
                        pe.wait_ge(S("head_loaded"), NLOAD * (hu + 1))
                    if op == "q":
                        for c in range(2):
                            k = take((op, c))
                            pe.matmul(bank(k)[0:QK, :], wq[:], nqT[:, T * ub + BANK * c:T * ub + BANK * (c + 1)],
                                      start=True, stop=True).then_inc(full[k], 1)
                    elif op == "k":
                        for c in range(2):
                            k = take((op, c))
                            pe.matmul(bank(k)[0:QK, :], wk[:], yT[:, T * ub + BANK * c:T * ub + BANK * (c + 1)],
                                      start=True, stop=True).then_inc(full[k], 1)
                    elif op == "n":
                        for c in range(2):
                            k, m = ring.at(kind, s, (op, c))
                            wait_apart(pe, S, free[k], m)
                            pe.matmul(bank(k)[64:96, :], wdk[64:96, :],
                                      kcT[64:96, T * ub + BANK * c:T * ub + BANK * (c + 1)],
                                      start=True, stop=True).then_inc(full[k], 1)
                    elif op == "v":
                        k = take(step)
                        for t in range(TB):
                            tok = slice(T * ub + P * t, T * ub + P * (t + 1))
                            mm = pe.matmul(bank(k)[:, VD * t:VD * (t + 1)], yT[:, tok], wvw[:], start=True, stop=True)
                        mm.then_inc(full[k], 1)
                    elif op == "k2":
                        k = take(step)
                        sel = selT[:, KEEP * ub:KEEP * (ub + 1)]
                        pe.matmul(bank(k)[0:QK, 0:KEEP], wks[:], sel, start=True, stop=True)
                        pe.matmul(bank(k)[0:KEEP, 64:64 + VD], sel, wvs[:], start=True, stop=True).then_inc(full[k], 1)
                    elif op == "mx":
                        _, branches, j, c = step
                        k = take(step)
                        hi = min(P * (j + 1), BANK * (c + 1))
                        w = hi - BANK * c
                        diag = hi == P * (j + 1)
                        for n, a in enumerate(branches):
                            if step == next(x for x in steps if x[0] == "mx" and a in x[1]):
                                pe.wait_ge(S("qH_done"), 2 * (u + 1))
                                pe.wait_ge(S("kHw_done") if a else S("kH1_done"), 2 * (u + 1))
                            mm = pe.matmul(bank(k)[:, w * n:w * (n + 1)], qH[ub][0:QK, P * j:P * (j + 1)],
                                           kH[a][ub][0:QK, BANK * c:hi], start=True, stop=not diag)
                            if diag:
                                mm = pe.matmul(bank(k)[:, w * (n + 1) - P:w * (n + 1)], K["identb"][:], K["maskb"][:],
                                               start=False, stop=True)
                        mm.then_inc(full[k], 1)
                    elif op == "mx2":
                        k = take(step)
                        pe.wait_ge(S("k2_done"), u + 1)
                        for j in range(TB):
                            mm = pe.matmul(bank(k)[:, KEEP * j:KEEP * (j + 1)], qH[ub][0:QK, P * j:P * (j + 1)],
                                           kH[2][ub][0:QK, :], start=True, stop=True)
                        mm.then_inc(full[k], 1)
                    elif op == "mt":
                        k = take(step)
                        pe.wait_ge(S("mneg"), u + 1)
                        pe.transpose(bank(k)[0:NBR * TB, 0:P], mneg[:].rearrange("p a j -> p (a j)"), ident[:]).then_inc(full[k], 1)
                    elif op == "S":
                        i = step[1]
                        if i == 0:
                            pe.wait_ge(S(f"maxrows{b}"), 48 * (h + 1))
                            pe.wait_ge(S("qL_done"), s + 1)
                            pe.wait_ge(S("kLw_done"), s + 1)
                        scores(0, i)
                        scores(1, i)
                    elif op == "W":
                        weighted(step[1])
                    elif op == "a2s":
                        pe.wait_ge(S("k2_done"), s + 1)
                        for c, lo, hi in pieces(0):
                            k = take((op, c))
                            o = bank(k)[0:KEEP, :]
                            pe.matmul(o, kH[2][b][0:QK, :], qL_[b][:, lo:hi], start=True, stop=False)
                            pe.matmul(o, kL[2][b][:], qH[b][0:QK, lo:hi], start=False, stop=False)
                            pe.matmul(o, kH[2][b][0:99, :], qH[b][0:99, lo:hi], start=False, stop=True).then_inc(full[k], 1)
                    elif op == "a2o":
                        for c in range(2):
                            k, n = ring.at(kind, s, ("a2s", c))
                            pe.wait_ge(free[k], n + 1)
                            k = take((op, c))
                            cols = slice(BANK * c, BANK * (c + 1))
                            pe.matmul(bank(k)[64:128, :], V2[b][:], p2[:, cols], start=True, stop=True).then_inc(full[k], 1)
                    elif op == "wp":
                        pe.wait_ge(S("out_read"), CREDIT + s)
                        pe.wait_ge(S("wpg_done"), s)
                        for c in range(2):
                            k = take((op, c))
                            for t in range(4):
                                j = 4 * c + t
                                mm = pe.matmul(bank(k)[:, P * t:P * (t + 1)], tO[ub][:, P * j:P * (j + 1)], wpg[ub][:],
                                               start=True, stop=True)
                            mm.then_inc(full[k], 1)

            run_slots(pe, slot)

        @block.scalar
        def _(act):
            act.preload_act_table_set("natural_log_exp_and_others")

            def slot(kind, s, h, b):
                u, ub = s + 1, 1 - b

                def filled(item):
                    k, n = ring.at(kind, s, item)
                    act.wait_ge(full[k], n + 1)
                    return k

                def exponentials(a, i):
                    act.wait_ge(S("weighted"), CREDIT + TB * s + max(i - NPR + 1, 0))
                    for c, lo, hi in pieces(i):
                        k = filled(("S", a, i, c))
                        act.activation(pr[a][i % NPR][:, lo:hi], bank(k)[:, lo - BANK * c:hi - BANK * c],
                                       ACT.Exp).then_inc(free[k], 1)

                for step in which[kind]:
                    op = step[0]
                    if op in ("q", "k"):
                        dst = qf if op == "q" else kf
                        wait_past(act, S("qL_done" if op == "q" else "kLw_done"), u)
                        for c in range(2):
                            k = filled((op, c))
                            act.activation(dst[64:96, BANK * c:BANK * (c + 1)], bank(k)[64:96, :], ACT.Copy).then_inc(S(f"{op}plain"), 1)
                    elif op in ("qh", "kh"):
                        o, src, dst = ("q", qf, qH[ub]) if op == "qh" else ("k", kf, kH[1][ub])
                        name = "qH_done" if op == "qh" else "kHw_done"
                        act.wait_ge(S(f"{o}plain"), 2 * (u + 1))
                        act.wait_ge(S(f"{o}rot"), u + 1)
                        for c in range(2):
                            act.activation(dst[0:QK, BANK * c:BANK * (c + 1)], src[:, BANK * c:BANK * (c + 1)], ACT.Copy).then_inc(S(name), 1)
                    elif op == "n":
                        for c in range(2):
                            k = filled((op, c))
                            act.activation(kH[0][ub][64:96, BANK * c:BANK * (c + 1)], bank(k)[64:96, :], ACT.Copy).then_inc(S("kH1_done"), 1)
                    elif op == "v":
                        k = filled(step)
                        act.activation(V[ub][:].rearrange("p t d -> p (t d)"), bank(k)[:, 0:TB * VD], ACT.Copy).then_inc(free[k], 1)
                    elif op == "mt":
                        k = filled(step)
                        if kind == "first":
                            pass
                        elif b == 0:
                            act.wait_ge(S("maxrows0"), 48 * (h + 1))
                        else:
                            act.wait_ge(S("maxrows1"), 48 * (h + 1))
                        act.activation(mT[:], bank(k)[0:NBR * TB, 0:P], ACT.Copy).then_inc(free[k], 1)
                    elif op == "S":
                        exponentials(0, step[1])
                        exponentials(1, step[1])
                    elif op == "a2s":
                        for c, lo, hi in pieces(0):
                            k = filled((op, c))
                            act.activation(p2[:, lo:hi], bank(k)[0:KEEP, :], ACT.Exp).then_inc(free[k], 1)
                    elif op == "a2o":
                        for c in range(2):
                            k = filled((op, c))
                            cols = slice(BANK * c, BANK * (c + 1))
                            act.activation(lnD[64:96, cols], bank(k)[96:128, :], ACT.Ln).then_inc(S("ln2"), 1)
                            act.wait_ge(S("ln2"), 2 * s + c + 1)
                            act.activation(rD[64:96, cols], lnD[64:96, cols], ACT.Exp, scale=-1.0).then_inc(S("rD2"), 1)
                    elif op == "invert":
                        act.wait_ge(S("weighted"), CREDIT + TB * s)
                        act.activation(lnD[0:64, :], out_ps[64:128, :], ACT.Ln).then_inc(S("ln01"), 1)
                        act.wait_ge(S("ln01"), s)
                        act.activation(rD[0:64, :], lnD[0:64, :], ACT.Exp, scale=-1.0).then_inc(S("rD01"), 1)

            run_slots(act, slot)

        @block.gpsimd
        def _(pool):
            def slot(kind, s, h, b):
                u, ub = s + 1, 1 - b
                for step in which[kind]:
                    op = step[0]
                    if op in ("qh", "kh"):
                        o, f, t, hi, lo = ("q", qf, qt, qH[ub], qL_[ub]) if op == "qh" else ("k", kf, kt, kH[1][ub], kL[1][ub])
                        pool.wait_ge(S(f"{o}terms"), 4 * (u + 1))
                        for c in range(2):
                            k, n = ring.at(kind, s, (o, c))
                            pool.wait_ge(free[k], n + 1)
                        pool.tensor_tensor(f[0:ROPE, :], f[0:ROPE, :], t[:], ALU.add).then_inc(S(f"{o}rot"), 1)
                        pool.wait_ge(S("qH_done" if op == "qh" else "kHw_done"), 2 * (u + 1))
                        pool.tensor_tensor(lo[:], f[:], hi[0:QK, :].bitcast(F32), ALU.subtract).then_inc(
                            S("qL_done" if op == "qh" else "kLw_done"), 1)
                    elif op == "S":
                        i = step[1]
                        for a in range(2):
                            k, n = ring.at(kind, s, ("S", a, i, pieces(i)[0][0]))
                            wait_apart(pool, S, free[k], n + 1)
                            d = pr[a][i % NPR][:, P * i:P * (i + 1)]
                            pool.affine_select(out=d, in_=d, pattern=[[1, P]], compare_op=ALU.is_ge, fill=0.0, base=0,
                                               channel_multiplier=-1).then_inc(S("probs"), 1)
                    elif op == "a2o":
                        wait_apart(pool, S, S("wp_loaded"), 48 * (h + 1))
                        pool.tensor_scalar(wpg[b][:], wp[:], K["gcol"][:, b:b + 1], None, ALU.mult).then_inc(S("wpg_done"), 1)

            run_slots(pool, slot)

        @block.vector
        def _(dve):
            def slot(kind, s, h, b):
                u, ub = s + 1, 1 - b

                def filled(item):
                    k, n = ring.at(kind, s, item)
                    dve.wait_ge(full[k], n + 1)
                    return k

                for step in which[kind]:
                    op = step[0]
                    if op in ("q", "k"):
                        f, t = (qf, qt) if op == "q" else (kf, kt)
                        wait_past(dve, S("qL_done" if op == "q" else "kLw_done"), u)
                        for c in range(2):
                            k = filled((op, c))
                            cols = slice(BANK * c, BANK * (c + 1))
                            dve.tensor_tensor(f[0:ROPE, cols], bank(k)[0:ROPE, :], cosT[:, cols], ALU.mult).then_inc(S(f"{op}terms"), 1)
                            dve.tensor_tensor(t[0:HALF, cols], bank(k)[HALF:ROPE, :], sinT[HALF:ROPE, cols], ALU.mult).then_inc(S(f"{op}terms"), 1)
                            dve.wait_ge(S(f"{op}plain"), 2 * u + c + 1)
                            dve.tensor_tensor(t[HALF:ROPE, cols], bank(k)[0:HALF, :], sinT[0:HALF, cols], ALU.mult).then_inc(free[k], 1)
                    elif op == "n":
                        for c in range(2):
                            k = filled((op, c))
                            cols = slice(BANK * c, BANK * (c + 1))
                            dve.wait_ge(S("kH1_done"), 2 * u + c + 1)
                            dve.tensor_tensor(kL[0][ub][64:96, cols], bank(k)[64:96, :], kH[0][ub][64:96, cols].bitcast(F32),
                                              ALU.subtract).then_inc(free[k], 1)
                    elif op == "k2":
                        k = filled(step)
                        kk = bank(k)[:, 0:KEEP]
                        x = S("k2_chain")
                        dve.tensor_tensor(k2f[0:ROPE, :], kk[0:ROPE, :], cosT[:, 0:KEEP], ALU.mult).then_inc(x, 1)
                        dve.tensor_tensor(k2t[0:HALF, :], kk[HALF:ROPE, :], sinT[HALF:ROPE, 0:KEEP], ALU.mult).then_inc(x, 1)
                        dve.tensor_tensor(k2t[HALF:ROPE, :], kk[0:HALF, :], sinT[0:HALF, 0:KEEP], ALU.mult).then_inc(x, 1)
                        dve.tensor_copy(k2f[64:96, :], kk[64:96, :]).then_inc(x, 1)
                        dve.tensor_copy(V2[ub][:, 0:VD], bank(k)[0:KEEP, 64:64 + VD]).then_inc(x, 1)
                        dve.wait_ge(x, 6 * u + 5)
                        dve.tensor_tensor(k2f[0:ROPE, :], k2f[0:ROPE, :], k2t[:], ALU.add).then_inc(free[k], 1)
                        dve.wait_ge(free[k], ring.at(kind, s, step)[1] + 1)
                        dve.tensor_copy(kH[2][ub][0:QK, :], k2f[:]).then_inc(x, 1)
                        dve.wait_ge(x, 6 * u + 6)
                        dve.tensor_tensor(kL[2][ub][:], k2f[:], kH[2][ub][0:QK, :].bitcast(F32), ALU.subtract).then_inc(S("k2_done"), 1)
                    elif op == "mx":
                        _, branches, j, c = step
                        k = filled(step)
                        na = len(branches)
                        a = slice(branches[0], branches[-1] + 1)
                        w = min(P * (j + 1), BANK * (c + 1)) - BANK * c
                        dst = mneg[:, a, j] if c == 0 else mpart[:, a, j - 4]
                        dve.tensor_reduce(dst, bank(k)[:, 0:na * w].rearrange("p (a n) -> p a n", a=na), AX.X, ALU.max, negate=True).then_inc(free[k], 1)
                    elif op == "mx2":
                        k = filled(step)
                        dve.tensor_reduce(mneg[:, 2, :], bank(k)[:, 0:KEEP * TB].rearrange("p (j n) -> p j n", n=KEEP),
                                          AX.X, ALU.max, negate=True).then_inc(free[k], 1)
                    elif op == "mt":
                        for item in [x for x in steps if x[0] in ("mx", "mx2")][-2:]:
                            k, n = ring.at(kind, s, item)
                            dve.wait_ge(free[k], n + 1)
                        dve.tensor_tensor(mneg[:, 0:2, 4:8], mneg[:, 0:2, 4:8], mpart[:], ALU.min).then_inc(S("mneg"), 1)
                    elif op == "a2o":
                        for c in range(2):
                            k = filled((op, c))
                            cols = slice(BANK * c, BANK * (c + 1))
                            dve.wait_ge(S("rD2"), 2 * s + c + 1)
                            dve.tensor_tensor(tO[b][64:96, cols], bank(k)[64:96, :], rD[64:96, cols], ALU.mult).then_inc(free[k], 1)
                    elif op == "norm":
                        dve.wait_ge(S("rD01"), s)
                        dve.tensor_tensor(tO[ub][0:64, :], out_ps[0:64, :], rD[0:64, :], ALU.mult).then_inc(S("out_read"), 1)
                    elif op == "wp":
                        for c in range(2):
                            k = filled((op, c))
                            rows = res[:, TB * ub + 4 * c:TB * ub + 4 * (c + 1), :].rearrange("p t c -> p (t c)")
                            dve.tensor_tensor(rows, bank(k), rows, ALU.add).then_inc(free[k], 1)

            for b in range(B):
                dve.memset(V2[b][:, VD:], 1.0).then_inc(S("v2_ones"), 1)
            run_slots(dve, slot)


def bank_uses(steps_of_kind, uses, loops):
    table, before, total = {}, {}, [0] * 8
    for kind, steps in steps_of_kind.items():
        count = [0] * 8
        for s in steps:
            for n, k in enumerate(uses.get(s, ())):
                table[kind, s, n] = (k, count[k])
                count[k] += 1
        before[kind] = total
        total = [t + n * (loops if kind == "loop" else 1) for t, n in zip(total, count)]
        if kind == "loop":
            per_slot = count

    def at(kind, slot, step, nth=0):
        k, i = table[kind, step, nth]
        return k, (before[kind][k] + i + (per_slot[k] * (slot - 2) if kind == "loop" else 0))

    return at


def ffn_weights(ins, F):
    loads = [(F["shift"][:], ins["c_shift"]), (F["edge"][:], ins["c_edge"]), (F["near"][:], ins["c_near"]),
             (F["flags"][:], ins["c_flags"]), (F["starts"][:], ins["c_starts"]),
             (F["wqkv"][:], ins["L0_ffn_wqkv"].rearrange("l c n -> c l n")),
             (F["wo"][:], ins["L0_ffn_wo"].rearrange("l (m p) c -> p l m c", p=P)),
             (F["w1"][:], ins["L0_ffn_w1"].rearrange("l c n -> c l n"))]
    for l in range(DEPTH):
        loads.append((F["lg"][:, l:l + 1], ins["L0_ffn_ln_g"][l].rearrange("(p a) -> p a", a=1)))
        loads.append((F["lb"][:, l:l + 1], ins["L0_ffn_ln_b"][l].rearrange("(p a) -> p a", a=1)))
        loads.append((F["b2"][:, l, :], ins["L0_ffn_b2"][l:l + 1, :].to_broadcast([P, C])))
        for c, (o, w) in enumerate(HCH):
            loads.append((F["w2"][0:w, l, c, :], ins["L0_ffn_w2"][l, o:o + w, :]))
            for half in range(2):
                loads.append((F["b1"][0:w, l, 3 * half + c:3 * half + c + 1],
                              ins["L0_ffn_b1"][l, HID * half + o:HID * half + o + w].rearrange("(p a) -> p a", a=1)))
    raw, gains = F["raw"], F["gains"]
    loads += [(raw[:, n], ins[name].rearrange("(t p) d -> p t d", p=P))
             for n, name in enumerate(("c_qcos", "c_qsin", "c_kcos", "c_ksin"))]
    for l in range(DEPTH):
        for n, name in ((0, "L0_ffn_q_scale"), (2, "L0_ffn_k_scale")):
            row = ins[name][l:l + 1, :]
            loads.append((gains[:, l, n, :], row.to_broadcast([P, FD])))
            loads.append((gains[:, l, n + 1, 0:HALF], row[:, HALF:FD].to_broadcast([P, HALF])))
            loads.append((gains[:, l, n + 1, HALF:FD], row[:, 0:HALF].to_broadcast([P, HALF])))
    return loads


def ffn_begin(nc, ins, F, ps, S, before):
    with ExitStack() as ctx:
        def sb(name, shape, dt=F32):
            return ctx.enter_context(nc.sbuf_tensor(name, shape, dt))

        stats = sb("f_stats", [P, NT, 6])
        mv = sb("f_mv", [P, NT, 2])
        va = sb("f_va", [P, NT])
        rs = sb("f_rs", [P, NT])
        res, xf = F["res"], F["xf"]
        block = ctx.enter_context(nc.Block())

        @block.sync
        def _(sp):
            before.clear(sp)

        @block.gpsimd
        def _(pool):
            pool.memset(F["kT"][3][:], 0.0).then_inc(S("zeroed"), 1)
            pool.memset(F["vN"][3][:], 0.0).then_inc(S("zeroed"), 1)
            pool.memset(F["vP"][3][:], 0.0).then_inc(S("zeroed"), 1)
            pool.memset(F["sm"][:], 0.0).then_inc(S("zeroed"), 1)
            pool.memset(xf[:, 0, :], 0.0).then_inc(S("zeroed"), 1)
            for c in range(4):
                pool.wait_ge(S("f_var"), c + 1)
                pool.tensor_tensor(rs[:, 4 * c:4 * c + 4], va[:, 4 * c:4 * c + 4], F["minus_half"][:, 0:4],
                                   ALU.pow).then_inc(S("f_rstd"), 1)
            rotation_tables(pool, F, 0, (2, 3), S("tabs"))

        @block.vector
        def _(dve):
            def normalise(c):
                dve.wait_ge(S("f_rstd"), c + 1)
                for t in range(4 * c, 4 * c + 4):
                    dve.tensor_scalar(xf[:, t + 1, :], res[:, t, :], mv[:, t, 0:1], rs[:, t:t + 1],
                                      ALU.subtract, ALU.mult).then_inc(S("xf"), 1)

            for c in range(4):
                for t in range(4 * c, 4 * c + 4):
                    dve.bn_stats(stats[:, t, :], res[:, t, :]).then_inc(S("f_stats"), 1)
                for t in range(4 * c, 4 * c + 4):
                    dve.wait_ge(S("f_stats"), t + 1)
                    dve.bn_aggr(mv[:, t, :], stats[:, t, :]).then_inc(S("f_aggr"), 1)
                dve.wait_ge(S("f_aggr"), 4 * c + 4)
                dve.tensor_scalar(va[:, 4 * c:4 * c + 4], mv[:, 4 * c:4 * c + 4, 1], 1e-5, None, ALU.add).then_inc(S("f_var"), 1)
                if c:
                    normalise(c - 1)
            rotation_tables(dve, F, 0, (0, 1), S("tabs"))
            normalise(3)


def rotation_tables(eng, F, l, which, signals):
    for n in which:
        for b in range(B):
            eng.tensor_tensor(F["tabs"][:, l, n, TB * b:TB * (b + 1), :], F["raw"][:, n],
                              F["gains"][:, l, n:n + 1, :].to_broadcast([P, TB, FD]), ALU.mult).then_inc(signals, 1)


def window_order():
    return ["ax", "co", "ah", "bs0", "aq0", "bs1", "aq1", "bn0", "ar0", "as", "bt0", "aq2", "bn1", "ar1", "bt1",
            "cx", "an0", "bv0", "bt2", "bt3", "bv1", "an1", "at0", "bv2", "at1", "bv3"]


def window_attention(nc, F, ps, l, S):
    steps = window_order()
    kinds = {kind: [s for s in steps if s[0] in which] for kind, which in
             (("first", "a"), ("second", "ab"), ("loop", "abc"), ("last", "bc"), ("end", "c"))}
    at = bank_uses(kinds, {"ah": (0,), "cx": (0,), "aq0": (1,), "aq1": (2,), "aq2": (3,), "at0": (1,),
                           "at1": (2,), "bs0": (4, 5), "bs1": (4, 5), "bt0": (6,), "bt1": (7,), "bt2": (6,), "bt3": (7,),
                           "bv0": (3,)}, 4 * LOOPS + 2)
    with ExitStack() as ctx:
        def sb(name, shape, dt=F32):
            return ctx.enter_context(nc.sbuf_tensor(f"{name}_l{l}", shape, dt))

        xa = sb("xa", [P, C])
        xb = sb("xb", [P, FD])
        hT = sb("hT", [P, P])
        sq = sb("sq", [P, 2, INNER])
        ss = sb("ss", [P, 2 * FH])
        rn = sb("rn", [P, 2 * FH])
        qk = [sb(f"qk{n}", [P, INNER]) for n in range(2)]
        qs = [sb(f"qs{n}", [P, INNER]) for n in range(2)]
        qT = [sb(f"qT{n}", [P, 4, P]) for n in range(2)]
        band = sb("band", [P, P + WIN])
        mx = sb("mx", [P, FH])
        ng = sb("ng", [P, FH])
        rs = sb("rs", [P, FH])
        rr = sb("rr", [P, FH])
        early = sb("early", [P, FH, WIN])
        pT = [sb(f"pT{n}", [P, 3, P]) for n in range(4)]
        oT = sb("oT", [P, 4, P])
        xf, tabs, flags, ident, shift, edge = (F[k] for k in ("xf", "tabs", "flags", "ident", "shift", "edge"))
        near, starts = F["near"], F["starts"]
        vP = F["vP"]
        kT, vN, sm, wqkv, wo = F["kT"], F["vN"], F["sm"], F["wqkv"], F["wo"]
        block = ctx.enter_context(nc.Block())
        full = [S(f"bank{k}_filled") for k in range(8)]
        free = [S(f"bank{k}_read") for k in range(8)]

        def heads(ap):
            return ap.rearrange("p (h d) -> p h d", h=FH)

        def run_slots(eng, slot):
            slot("first", 0, 0)
            slot("second", 1, 1)
            with eng.Fori(0, LOOPS) as i:
                for r in range(2, 6):
                    slot("loop", 4 * i + r, r % 4)
            for t in range(4 * LOOPS + 2, 4 * LOOPS + 4):
                slot("loop", t, t % 4)
            slot("last", 4 * LOOPS + 4, 0)
            slot("end", 4 * LOOPS + 5, 1)

        def slot_before(kind, t, step):
            return at({"second": "first", "loop": "loop", "last": "loop", "end": "last"}[kind], t - 1, step)

        @block.sync
        def _(sp):
            for k in range(8):
                sp.sem_inc(free[k], CREDIT)
            for r in range(4):
                sp.sem_inc(S(f"values_moved{r}"), CREDIT)

            def slot(kind, t, r):
                if kind in ("first", "second", "loop"):
                    k, n = at(kind, t, "aq2")
                    sp.wait_ge(free[k], CREDIT + n + 1)
                    sp.dma_start(vP[r][:], vN[r][WIN:P, :].rearrange("p (m e d) -> p m e d", e=2, d=FD)[:, :, 0, :]).then_inc(
                        S(f"values_moved{r}"), 16)

            run_slots(sp, slot)
            for r in range(4):
                sp.wait_ge(S(f"values_moved{r}"), CREDIT + 16 * (LOOPS + 1))

        @block.tensor
        def _(pe):
            def slot(kind, t, r):
                g = t - 1
                rg, rp = (r - 1) % 4, (r - 2) % 4

                def take(step, nth=0):
                    k, n = at(kind, t, step, nth)
                    pe.wait_ge(free[k], CREDIT + n)
                    return k

                for step in kinds[kind]:
                    if step == "ah":
                        k = take(step)
                        pe.wait_ge(S("x_copied"), 2 * (t + 1))
                        pe.matmul(ps[0:64, k, 0:P], xa[:, 0:FD], ident[:], start=True, stop=True)
                        pe.matmul(ps[64:128, k, 0:P], xa[:, FD:C], shift[:], start=True, stop=False)
                        pe.matmul(ps[64:128, k, 0:P], xb[:], edge[:], start=False, stop=True).then_inc(full[k], 1)
                    elif step[0:2] == "aq":
                        n = int(step[2])
                        if n == 0:
                            hk, hn = at(kind, t, "ah")
                            pe.wait_ge(free[hk], CREDIT + hn + 1)
                        k = take(step)
                        pe.matmul(ps[:, k, :], hT[:], wqkv[:, l, INNER * n:INNER * (n + 1)],
                                  start=True, stop=True).then_inc(full[k], 1)
                    elif step in ("at0", "at1"):
                        n = int(step[2])
                        k = take(step)
                        pe.wait_ge(S("qk_scaled"), 2 * t + n + 1)
                        for m in range(4):
                            mm = pe.transpose(ps[:, k, P * m:P * (m + 1)], qk[n][:, P * m:P * (m + 1)], ident[:])
                        mm.then_inc(full[k], 1)
                    elif step in ("bs0", "bs1"):
                        gr = int(step[2])
                        if gr == 0:
                            for n in range(2):
                                pk, pn = slot_before(kind, t, f"at{n}")
                                pe.wait_ge(free[pk], CREDIT + pn + 1)
                        for o in range(2):
                            k = take(step, o)
                            rows = slice(FD * o, FD * (o + 1))
                            for e in range(2):
                                hp = 2 * gr + e
                                q = qT[rg % 2][rows, hp, :]
                                pe.matmul(ps[:, k, 192 * e:192 * e + 64], q, kT[rp][rows, hp, 64:128], start=True, stop=True)
                                mm = pe.matmul(ps[:, k, 192 * e + 64:192 * e + 192], q, kT[rg][rows, hp, :], start=True, stop=True)
                            mm.then_inc(full[k], 1)
                    elif step[0:2] == "bt":
                        m = int(step[2])
                        k = take(step)
                        pe.wait_ge(S("weights"), 4 * g + 2 * (m // 2) + 2)
                        pe.transpose(ps[:, k, 0:P], early[:, 2 * m:2 * m + 2, :].rearrange("p a n -> p (a n)"), ident[:])
                        for j in range(2):
                            mm = pe.transpose(ps[:, k, P * (j + 1):P * (j + 2)], sm[:, 2 * m + j, P:2 * P], ident[:])
                        mm.then_inc(full[k], 1)
                    elif step[0:2] == "bv":
                        weighted(kind, t, int(step[2]), rg, rp)
                    elif step == "cx":
                        vk, vn = slot_before(kind, t, "bv0")
                        pe.wait_ge(free[vk], CREDIT + vn + 1)
                        k = take(step)
                        for m in range(4):
                            mm = pe.matmul(ps[:, k, 0:P], oT[:, m, :], wo[:, l, m, :], start=(m == 0), stop=(m == 3))
                        mm.then_inc(full[k], 1)

            def weighted(kind, t, m, rg, rp):
                k6, n6 = at(kind, t, f"bt{m}")
                pe.wait_ge(free[k6], CREDIT + n6 + 1)
                k, n = at(kind, t, "bv0")
                if m == 0:
                    pe.wait_ge(free[k], CREDIT + n)
                    pe.wait_ge(S(f"values_moved{rp}"), CREDIT + 4 * (t - 2 - rp) + 16)
                for j in range(2):
                    hh = 2 * m + j
                    cols = slice(FD * hh, FD * (hh + 1))
                    o = ps[FD * j:FD * (j + 1), k, P * m:P * (m + 1)]
                    before = vN[rp][WIN:P, cols] if j else vP[rp][:, m, :]
                    pe.matmul(o, vN[rg][:, cols], pT[m][:, 1 + j, :], start=True, stop=False)
                    mm = pe.matmul(o, before, pT[m][WIN * j:WIN * (j + 1), 0, :], start=False, stop=True)
                if m == 3:
                    mm.then_inc(full[k], 1)

            run_slots(pe, slot)

        @block.scalar
        def _(act):
            def slot(kind, t, r):
                g = t - 1

                def filled(step, nth=0):
                    k, n = at(kind, t, step, nth)
                    act.wait_ge(full[k], n + 1)
                    return k

                for step in kinds[kind]:
                    if step == "ah":
                        k = filled(step)
                        act.activation(hT[:], ps[:, k, 0:P], ACT.Copy).then_inc(free[k], 1)
                    elif step in ("aq0", "aq1"):
                        n = int(step[2])
                        if n == 0:
                            wait_past(act, S("sums"), t)
                        k = filled(step)
                        act.activation(sq[:, n, :], ps[:, k, :], ACT.Square).then_inc(S("squares"), 1)
                    elif step == "aq2":
                        k = filled(step)
                        act.activation(vN[r][:], ps[:, k, :], ACT.Copy).then_inc(free[k], 1)
                    elif step in ("at0", "at1"):
                        dst = (qT[r % 2], kT[r])[int(step[2])]
                        k = filled(step)
                        act.activation(dst[:].rearrange("p a n -> p (a n)"), ps[:, k, :], ACT.Copy).then_inc(free[k], 1)
                    elif step in ("bs0", "bs1"):
                        gr = int(step[2])
                        act.wait_ge(S("neg_max"), 2 * g + gr + 1)
                        for hh in range(4 * gr, 4 * gr + 4):
                            act.activation(sm[:, hh, 64:256], sm[:, hh, 64:256], ACT.Exp, bias=ng[:, hh:hh + 1],
                                           accum_out=rs[:, hh:hh + 1]).then_inc(S("probs"), 1)
                    elif step in ("bt1", "bt3"):
                        k = filled(step)
                        act.activation(pT[int(step[2])][:].rearrange("p a n -> p (a n)"), ps[:, k, 0:3 * P], ACT.Copy).then_inc(free[k], 1)
                    elif step == "co":
                        xk, xn = slot_before(kind, t, "cx")
                        act.wait_ge(full[xk], xn + 1)
                        k, n = slot_before(kind, t, "bv0")
                        act.wait_ge(full[k], n + 1)
                        act.activation(oT[:].rearrange("p a n -> p (a n)"), ps[:, k, :], ACT.Copy).then_inc(free[k], 1)

            run_slots(act, slot)

        @block.gpsimd
        def _(pool):
            def slot(kind, t, r):
                for step in kinds[kind]:
                    if step == "as":
                        pool.wait_ge(S("clipped"), t + 1)
                        pool.tensor_tensor(rn[:], ss[:], F["minus_half"][:, 0:2 * FH], ALU.pow).then_inc(S("rn"), 1)
                    elif step in ("ar0", "ar1"):
                        n = int(step[2])
                        pool.wait_ge(S("cos_terms"), 2 * t + n + 1)
                        k, m = at(kind, t, f"aq{n}")
                        pool.wait_ge(free[k], CREDIT + m + 1)
                        pool.tensor_tensor(qk[n][:], qk[n][:], qs[n][:], ALU.add).then_inc(S("rotated"), 1)

            run_slots(pool, slot)

        @block.vector
        def _(dve):
            def slot(kind, t, r):
                g = t - 1

                def filled(step, nth=0):
                    k, n = at(kind, t, step, nth)
                    dve.wait_ge(full[k], n + 1)
                    return k

                for step in kinds[kind]:
                    if step == "ax":
                        dve.tensor_copy(xa[:], xf[:, t + 1, :]).then_inc(S("x_copied"), 1)
                        dve.tensor_scalar(xb[:], xf[:, t, FD:C], flags[:, bass.ds(t, 1)], None, ALU.mult).then_inc(S("x_copied"), 1)
                    elif step == "as":
                        dve.wait_ge(S("squares"), 2 * (t + 1))
                        dve.tensor_reduce(ss[:], sq[:].rearrange("p a (h d) -> p (a h) d", h=FH), AX.X, ALU.add).then_inc(S("sums"), 1)
                        dve.wait_ge(S("sums"), t + 1)
                        dve.tensor_scalar(ss[:], ss[:], 1e-24, None, ALU.max).then_inc(S("clipped"), 1)
                    elif step in ("ar0", "ar1"):
                        n = int(step[2])
                        k = filled(f"aq{n}")
                        dve.wait_ge(S("squares"), 2 * t + n + 1)
                        dve.tensor_tensor(heads(qk[n][:]), heads(ps[:, k, :]),
                                          tabs[:, l, 2 * n, bass.ds(t, 1), :].to_broadcast([P, FH, FD]), ALU.mult).then_inc(S("cos_terms"), 1)
                        for o in range(2):
                            src = heads(ps[:, k, :])[:, :, HALF * (1 - o):HALF * (2 - o)]
                            dst = heads(qs[n][:])[:, :, HALF * o:HALF * (o + 1)]
                            tab = tabs[:, l, 2 * n + 1, bass.ds(t, 1), HALF * o:HALF * (o + 1)].to_broadcast([P, FH, HALF])
                            dve.tensor_tensor(dst, src, tab, ALU.mult).then_inc(free[k] if o else S("sin_terms"), 1)
                    elif step in ("an0", "an1"):
                        n = int(step[2])
                        dve.wait_ge(S("rn"), t + 1)
                        dve.wait_ge(S("rotated"), 2 * t + n + 1)
                        dve.tensor_tensor(heads(qk[n][:]), heads(qk[n][:]),
                                          rn[:, FH * n:FH * (n + 1)].unsqueeze(2).to_broadcast([P, FH, FD]),
                                          ALU.mult).then_inc(S("qk_scaled"), 1)
                    elif step in ("bs0", "bs1"):
                        gr = int(step[2])
                        if gr == 0:
                            dve.tensor_scalar(band[:, 0:WIN], near[:, 0:WIN], starts[:, bass.ds(g, 1)], None,
                                              ALU.add).then_inc(S("band"), 1)
                            dve.wait_ge(S("band"), g + 2)
                            if kind != "second":
                                pk, pn = slot_before(kind, t, "bt3")
                                dve.wait_ge(free[pk], CREDIT + pn + 1)
                        k4, k5 = filled(step, 0), filled(step, 1)
                        dve.sem_inc(S("passed_DVE"), 1)
                        for o, k in enumerate((k4, k5)):
                            for e in range(2):
                                hh = 4 * gr + 2 * e + o
                                dve.tensor_tensor_reduce(sm[:, hh, 64:256], ps[:, k, 192 * e:192 * e + 192], band[:], 1.0,
                                                         -3.0e38, ALU.add, ALU.max, mx[:, hh:hh + 1]).then_inc(free[k] if e else S("maxed"), 1)
                        dve.wait_ge(S("maxed"), 4 * g + 2 * gr + 2)
                        for o in range(2):
                            k, n = at(kind, t, step, o)
                            dve.wait_ge(free[k], CREDIT + n + 1)
                        dve.tensor_scalar(ng[:, 4 * gr:4 * gr + 4], mx[:, 4 * gr:4 * gr + 4], -1.0, None, ALU.mult).then_inc(S("neg_max"), 1)
                    elif step in ("bt0", "bt2"):
                        k = filled(step)
                        dve.tensor_copy(pT[int(step[2])][:].rearrange("p a n -> p (a n)"), ps[:, k, 0:3 * P]).then_inc(free[k], 1)
                    elif step in ("bn0", "bn1"):
                        gr = int(step[2])
                        hs = slice(4 * gr, 4 * gr + 4)
                        dve.wait_ge(S("probs"), FH * g + 4 * gr + 4)
                        dve.reciprocal(rr[:, hs], rs[:, hs]).then_inc(S("rr"), 1)
                        dve.wait_ge(S("rr"), 2 * g + gr + 1)
                        for w, dst in ((slice(WIN, P), early[:, hs, :]), (slice(P, 2 * P), sm[:, hs, P:2 * P])):
                            dve.tensor_tensor(dst, sm[:, hs, w], rr[:, hs].unsqueeze(2).to_broadcast([P, 4, w.stop - w.start]),
                                              ALU.mult).then_inc(S("weights"), 1)
                    elif step == "cx":
                        k = filled(step)
                        dve.tensor_tensor(xf[:, t - 1, :], ps[:, k, 0:P], xf[:, t - 1, :], ALU.add).then_inc(free[k], 1)

            dve.tensor_copy(band[:], near[:]).then_inc(S("band"), 1)
            run_slots(dve, slot)


def gated_mlp(nc, F, ps, l, S, out_ap=None):
    NC4, W = NT // 4, BANK
    with ExitStack() as ctx:
        def sb(name, shape, dt=F32):
            return ctx.enter_context(nc.sbuf_tensor(f"{name}_m{l}", shape, dt))

        xp = sb("xp", [P, NT, FD])
        hn = sb("hn", [P, NT, C])
        stats = sb("stats", [P, NT, 6])
        mv = sb("mv", [P, NT, 2])
        va = sb("va", [P, NT])
        rs = sb("rs", [P, NT])
        hT = sb("hTm", [P, NT * P])
        gg = sb("gg", [P, 3, W])
        hid = sb("hid", [P, 3, W])
        xf, res, flags, ident, shift, edge = (F[k] for k in ("xf", "res", "flags", "ident", "shift", "edge"))
        w1, w2, b1, b2, lg, lb = (F[k] for k in ("w1", "w2", "b1", "b2", "lg", "lb"))
        last = l == DEPTH - 1
        block = ctx.enter_context(nc.Block())

        @block.gpsimd
        def _(pool):
            for m in range(NC4):
                pool.wait_ge(S("var"), m + 1)
                pool.tensor_tensor(rs[:, 4 * m:4 * m + 4], va[:, 4 * m:4 * m + 4], F["minus_half"][:, 0:4],
                                   ALU.pow).then_inc(S("rstd"), 1)
            if not last:
                rotation_tables(pool, F, l + 1, range(4), S("tabs"))

        @block.vector
        def _(dve):
            for m in range(NC4):
                s = slice(4 * m, 4 * m + 4)
                dve.tensor_tensor(xp[:, s, :], xf[:, s, FD:C], flags[:, s].unsqueeze(2).to_broadcast([P, 4, FD]),
                                  ALU.mult).then_inc(S("xp"), 1)
            def normalise(m):
                dve.wait_ge(S("rstd"), m + 1)
                for t in range(4 * m, 4 * m + 4):
                    dve.tensor_scalar(hn[:, t, :], hn[:, t, :], mv[:, t, 0:1], rs[:, t:t + 1], ALU.subtract, ALU.mult).then_inc(S("normed"), 1)

            for m in range(NC4):
                s = slice(4 * m, 4 * m + 4)
                dve.tensor_copy(hn[:, s, 0:FD], xf[:, 4 * m + 1:4 * m + 5, 0:FD]).then_inc(S("lower"), 1)
                dve.wait_ge(S("shifted"), m + 1)
                dve.tensor_copy(hn[:, s, FD:C], ps[:, m, 0:4 * FD].rearrange("p (t d) -> p t d", t=4)).then_inc(S("upper"), 1)
                dve.wait_ge(S("lower"), m + 1)
                dve.wait_ge(S("upper"), m + 1)
                for t in range(4 * m, 4 * m + 4):
                    dve.bn_stats(stats[:, t, :], hn[:, t, :]).then_inc(S("stats"), 1)
                for t in range(4 * m, 4 * m + 4):
                    dve.wait_ge(S("stats"), t + 1)
                    dve.bn_aggr(mv[:, t, :], stats[:, t, :]).then_inc(S("aggr"), 1)
                dve.wait_ge(S("aggr"), 4 * m + 4)
                dve.tensor_scalar(va[:, s], mv[:, s, 1], 1e-5, None, ALU.add).then_inc(S("var"), 1)
                if m:
                    normalise(m - 1)
            normalise(NC4 - 1)
            for m in range(NC4):
                s = slice(4 * m + 1, 4 * m + 5)
                dve.tensor_tensor(xf[:, s, :], xf[:, s, :], b2[:, l:l + 1, :].to_broadcast([P, 4, C]), ALU.add).then_inc(S("biased"), 1)
            if last:
                for m in range(NC4):
                    s = slice(4 * m + 1, 4 * m + 5)
                    dve.wait_ge(S("biased"), m + 1)
                    dve.tensor_tensor(xf[:, s, :], xf[:, s, :], res[:, 4 * m:4 * m + 4, :], ALU.add).then_inc(S("biased"), 1)
            dve.wait_ge(S("biased"), NC4 * (1 + last))
            with dve.Fori(0, NC4) as m:
                for c, (o, w) in enumerate(HCH):
                    dve.wait_ge(S("a_filled"), 3 * m + c + 1)
                    dve.wait_ge(S("gelu"), CREDIT + 3 * m + c + 1)
                    dve.scalar_tensor_tensor(out=hid[0:w, c, :], in0=ps[0:w, 3 + c, :], scalar=b1[0:w, l, c:c + 1],
                                             in1=gg[0:w, c, :], op0=ALU.add, op1=ALU.mult).then_inc(S("hidden"), 1)
                dve.wait_ge(S("out_filled"), m + 1)
                rows = xf[:, bass.ds(4 * m + 1, 4), :]
                dve.tensor_tensor(rows, ps[:, 7, :].rearrange("p (t c) -> p t c", t=4), rows, ALU.add).then_inc(S("out_done"), 1)

        @block.scalar
        def _(act):
            for g in range(NC4):
                act.wait_ge(S("turned"), g + 1)
                act.activation(hT[:, W * g:W * (g + 1)], ps[:, g, :], ACT.Identity, scale=lg[:, l:l + 1],
                               bias=lb[:, l:l + 1]).then_inc(S("hT"), 1)
            with act.Fori(0, NC4) as m:
                act.wait_ge(S("hidden"), CREDIT + 3 * m)
                for c, (o, w) in enumerate(HCH):
                    act.wait_ge(S("g_filled"), 3 * m + c + 1)
                    act.activation(gg[0:w, c, :], ps[0:w, c, :], ACT.Gelu, bias=b1[0:w, l, 3 + c:4 + c]).then_inc(S("gelu"), 1)

        @block.tensor
        def _(pe):
            for m in range(NC4):
                pe.wait_ge(S("xp"), m + 1)
                o = ps[:, m, 0:4 * FD].rearrange("p (t d) -> p t d", t=4)
                pe.matmul(o, shift[:], xf[:, 4 * m + 1:4 * m + 5, FD:C], start=True, stop=False)
                pe.matmul(o, edge[:], xp[:, 4 * m:4 * m + 4, :], start=False, stop=True).then_inc(S("shifted"), 1)
            pe.wait_ge(S("upper"), NC4)
            for t in range(NT):
                pe.wait_ge(S("normed"), t + 1)
                mm = pe.transpose(ps[:, t // 4, P * (t % 4):P * (t % 4 + 1)], hn[:, t, :], ident[:])
                if t % 4 == 3:
                    mm.then_inc(S("turned"), 1)
            pe.wait_ge(S("hT"), NC4)
            with pe.Fori(0, NC4) as m:
                h = hT[:, bass.ds(W * m, W)]
                pe.wait_ge(S("gelu"), CREDIT + 3 * m)
                for c, (o, w) in enumerate(HCH):
                    pe.matmul(ps[0:w, c, :], w1[:, l, HID + o:HID + o + w], h, start=True, stop=True).then_inc(S("g_filled"), 1)
                pe.wait_ge(S("hidden"), CREDIT + 3 * m)
                for c, (o, w) in enumerate(HCH):
                    pe.matmul(ps[0:w, 3 + c, :], w1[:, l, o:o + w], h, start=True, stop=True).then_inc(S("a_filled"), 1)
                pe.wait_ge(S("out_done"), CREDIT + m)
                pe.wait_ge(S("hidden"), CREDIT + 3 * m + 3)
                for t in range(4):
                    for c, (o, w) in enumerate(HCH):
                        mm = pe.matmul(ps[:, 7, P * t:P * (t + 1)], hid[0:w, c, P * t:P * (t + 1)], w2[0:w, l, c, :],
                                       start=(c == 0), stop=(c == 2))
                mm.then_inc(S("out_filled"), 1)

        @block.sync
        def _(sp):
            for name in ("hidden", "gelu", "out_done"):
                sp.sem_inc(S(name), CREDIT)
            if last:
                o_v = out_ap.rearrange("b (t p) c -> p (b t) c", p=P)
                for m in range(NC4):
                    sp.wait_ge(S("out_done"), CREDIT + m + 1)
                    sp.dma_start(o_v[:, 4 * m:4 * m + 4, :], xf[:, 4 * m + 1:4 * m + 5, :]).then_inc(S("stored"), 16)
                sp.wait_ge(S("stored"), 16 * NC4)


def build(nc, ins, out):
    with ExitStack() as ctx:
        def sb(name, shape, dt=F32):
            return ctx.enter_context(nc.sbuf_tensor(name, shape, dt))

        ps = ctx.enter_context(nc.psum_tensor("ps", [P, 8, BANK], F32))
        res = sb("res", [P, NT, C])
        ident = sb("ident", [P, P])
        minus_half = sb("minus_half", [P, 2 * NT])
        F = dict(res=res, ident=ident, minus_half=minus_half, shift=sb("shift", [P, P]), edge=sb("edge", [P, P]), near=sb("near", [P, P + WIN]),
                 flags=sb("flags", [P, NT]), starts=sb("starts", [P, NT]), wqkv=sb("wqkv", [P, DEPTH, 3 * INNER]),
                 wo=sb("wo", [P, DEPTH, 4, C]), w1=sb("w1", [P, DEPTH, 2 * HID]), w2=sb("w2", [HCH[0][1], DEPTH, 3, C]),
                 b1=sb("b1", [HCH[0][1], DEPTH, 6]), b2=sb("b2", [P, DEPTH, C]), lg=sb("lg", [P, DEPTH]),
                 lb=sb("lb", [P, DEPTH]), raw=sb("raw", [P, 4, TB, FD]),
                 gains=sb("gains", [P, DEPTH, 4, FD]))
        SA = Sems(nc, ctx, "att_")
        with ExitStack() as actx:
            def sba(name, shape, dt=F32):
                return actx.enter_context(nc.sbuf_tensor(name, shape, dt))
            K = dict(res=res, ident=ident, minus_half=minus_half, identb=sba("identb", [P, P], BF16), maskb=sba("maskb", [P, P], BF16),
                     maskf=sba("maskf", [P, P]), cosT=sba("cosT", [ROPE, T]), sinT=sba("sinT", [ROPE, T]),
                     yT=sba("yT", [P, B * T]), nqT=sba("nqT", [QL, B * T]), kcT=sba("kcT", [96, B * T]),
                     ones=sba("ones", [P, VD]), cN=sba("cN", [P, NT, KVL]), wvo=sba("wvo", [KVL, H // 4, 4, C]), selT=sba("selT", [P, B * KEEP]), gcol=sba("gcol", [96, B]),
                     kH1=[sba(f"kH1{b}", [99, T], F32R) for b in range(B)],
                     kL1=[sba(f"kL1{b}", [QK, T], F32R) for b in range(B)],
                     kHw=[sba(f"kHw{b}", [99, T], F32R) for b in range(B)],
                     kH2=[sba(f"kH2{b}", [99, KEEP], F32R) for b in range(B)])
            with ExitStack() as pctx:
                SP_ = Sems(nc, pctx, "prep_")
                prepare(nc, ins, K, ps, SP_)
                latent_attention(nc, ins, K, ps, SA, SP_, ffn_weights(ins, F))
        with ExitStack() as fctx:
            def sbf(name, shape, dt=F32):
                return fctx.enter_context(nc.sbuf_tensor(name, shape, dt))
            F.update(xf=sbf("xf", [P, NT + 1, C]), vP=[sbf(f"vP{n}", [WIN, FH // 2, FD]) for n in range(4)],
                     tabs=sbf("tabs", [P, DEPTH, 4, NT, FD]),
                     sm=sbf("sm", [P, FH, 2 * P]), kT=[sbf(f"kT{n}", [P, 4, P]) for n in range(4)],
                     vN=[sbf(f"vN{n}", [P, INNER]) for n in range(4)])
            with ExitStack() as bctx:
                ffn_begin(nc, ins, F, ps, Sems(nc, bctx, "start_"), SA)
            SW, SM = Sems(nc, fctx, "win_"), Sems(nc, fctx, "mlp_")
            for l in range(DEPTH):
                window_attention(nc, F, ps, l, SW)
                gated_mlp(nc, F, ps, l, SM, out)
                if l < DEPTH - 1:
                    with nc.Block() as between:
                        @between.sync
                        def _(sp):
                            SW.clear(sp)
                            SM.clear(sp)


def _constants():
    f32 = np.float32
    f = (f32(1.0) / f32(10000.0) ** (np.arange(0, ROPE, 2, dtype=f32) / f32(ROPE))).astype(f32)
    a = np.outer(np.arange(T, dtype=f32), f).astype(f32)
    cos, sin = np.cos(a).astype(f32), np.sin(a).astype(f32)
    i, j = np.arange(P)[:, None], np.arange(P)[None, :]
    out = {
        "c_ident": np.eye(P, dtype=f32),
        "c_causal": np.where(j > i, f32(NEG), f32(0.0)).astype(f32),
        "c_cosT": np.ascontiguousarray(np.concatenate([cos, cos], 1).T),
        "c_sinT": np.ascontiguousarray(np.concatenate([sin, -sin], 1).T),
        "c_cosN": cos / f32(H), "c_sinN": sin / f32(H),
        "c_iota": np.tile(np.arange(KEEP, dtype=f32), (P, 1)),
    }
    half = np.arange(0, FD, 2, dtype=f32)
    inv = (f32(1.0) / f32(10000.0) ** (half / f32(FD))).astype(f32)
    ang = (np.arange(T, dtype=f32)[:, None] * inv[None, :]).astype(f32)
    base = ((half + f32(0.4 * FD)) / f32(1.4 * FD)).astype(f32)
    power = ((np.arange(T, dtype=f32) - T // 2) / f32(WIN // 2)).astype(f32)
    scale = (base[None, :] ** power[:, None]).astype(f32)
    both = lambda a: np.concatenate([a, a], 1)
    sgn = np.concatenate([-np.ones(FD // 2, f32), np.ones(FD // 2, f32)])[None, :]
    out["c_qcos"] = both(np.cos(ang) * scale * f32(8.0)).astype(f32)
    out["c_qsin"] = (both(np.sin(ang) * scale * f32(8.0)) * sgn).astype(f32)
    out["c_kcos"] = both(np.cos(ang) / scale).astype(f32)
    out["c_ksin"] = (both(np.sin(ang) / scale) * sgn).astype(f32)
    out["c_shift"] = np.eye(P, k=1, dtype=f32)
    edge = np.zeros((P, P), f32)
    edge[P - 1, 0] = 1.0
    out["c_edge"] = edge
    q, k = np.arange(P)[:, None], np.arange(P + WIN)[None, :] - WIN
    near = (q - k >= 0) & (q - k <= WIN)
    out["c_near"] = np.where(near, f32(0.0), f32(NEG)).astype(f32)
    out["c_starts"] = np.tile(np.where(np.arange(NT) % TB == 0, f32(NEG), f32(0.0)).astype(f32), (P, 1))
    out["c_flags"] = np.tile((np.arange(NT) % TB != 0).astype(f32), (P, 1))
    return out


_INS = ['L0_attn_x', 'L0_attn_w_cq', 'L0_attn_g_qnorm', 'L0_attn_w_dq_nope', 'L0_attn_w_dq_rope', 'L0_attn_w_ckv',
        'L0_attn_g_kvnorm', 'L0_attn_w_dk_nope', 'L0_attn_w_dv', 'L0_attn_w_krope', 'L0_attn_w_imp', 'L0_attn_w_selk',
        'L0_attn_w_selv', 'L0_attn_w_wink', 'L0_attn_w_winv', 'L0_attn_w_gate', 'L0_attn_w_proj', 'L0_ffn_wqkv',
        'L0_ffn_q_scale', 'L0_ffn_k_scale', 'L0_ffn_wo', 'L0_ffn_ln_g', 'L0_ffn_ln_b', 'L0_ffn_w1', 'L0_ffn_b1',
        'L0_ffn_w2', 'L0_ffn_b2']


def kernel(**inputs):
    import concourse.bacc as _bacc
    from concourse.bass_utils import run_bass_kernel_spmd as _run

    nc = _bacc.Bacc("TRN2", target_bir_lowering=False, num_devices=1)
    arrays, aps = {}, {}
    given = {n: np.ascontiguousarray(inputs[n]) for n in _INS}
    given.update(_constants())
    for name, a in given.items():
        arrays[f"in_{name}_dram"] = a
        aps[name] = nc.dram_tensor(f"in_{name}_dram", a.shape, mybir.dt.from_np(a.dtype), kind="ExternalInput").ap()
    out = nc.dram_tensor("out_0_dram", (B, T, C), F32, kind="ExternalOutput").ap()
    build(nc, aps, out)
    r = _run(nc, [arrays], core_ids=[0])
    return r.results[0]["out_0_dram"]
```
